# Optimizing a Trainium2 kernel written in Bass

```python
import numpy as np
import jax
import jax.numpy as jnp

def _softmax(x, axis=-1):
    return jax.nn.softmax(x, axis=axis)
def _gelu(x):
    return jax.nn.gelu(x, approximate=True)
def _silu(x):
    return jax.nn.silu(x)
def _sigmoid(x):
    return jax.nn.sigmoid(x)
def _layernorm(x, axis=-1, eps=1e-5):
    m = jnp.mean(x, axis=axis, keepdims=True)
    v = jnp.var(x, axis=axis, keepdims=True)
    return (x - m) / jnp.sqrt(v + eps)
def _scatter_add(tgt, idx, src, axis=0):
    return tgt.at[idx].add(src)
def _segment_sum(src, seg, n):
    return jax.ops.segment_sum(src, seg, n)

kernel_name = 'mk_conv_attn_hybrid_d2_conv_nhwc128_e8dd3e'

def setup_inputs(seed: int = 0):
    np.random.seed(seed)
    _w = jnp.asarray
    def _rec_inputs():
        import jax
        import jax.numpy as jnp
        _gk = jax.random.key(seed)
        x = -0.0005207 + 1.001 * jax.random.normal(jax.random.fold_in(_gk, 1), (4, 64, 64, 128), jnp.float32)
        return x
    x = _rec_inputs()
    def _L0_conv_setup():
        import jax, jax.numpy as jnp
        import numpy as np
        NUM_HEAD = 8

        def conv_same(x, w, b):
            return jax.lax.conv_general_dilated(x, w, window_strides=(1, 1), padding='SAME', dimension_numbers=('NHWC', 'HWIO', 'NHWC')) + b

        def _gated_resnet(x, W1, b1, W2, b2, Wq, bq, Wk, bk, Wv, bv, W3, b3):
            B, H, W, C = x.shape
            c1 = conv_same(jax.nn.elu(x), W1, b1)
            c2 = conv_same(c1, W2, b2)
            a, b = jnp.split(c2, 2, axis=-1)
            c3 = a * jax.nn.sigmoid(b)
            N = H * W
            f = c3.reshape(B, N, C)
            q = f @ Wq + bq
            k = f @ Wk + bk
            v = f @ Wv + bv
            scale = jnp.float32(np.sqrt(C // 8))
            dot = jnp.einsum('bnd,bmd->bnm', q, k) / scale
            mask = jnp.tril(jnp.ones((N, N), jnp.float32), -1)
            dot = dot - (1.0 - mask) * 10000000000.0
            dot = dot - jnp.max(dot, axis=-1, keepdims=True)
            e = jnp.exp(dot) * mask
            probs = e / (jnp.sum(e, axis=-1, keepdims=True) + 1e-10)
            atten = jnp.einsum('bnm,bmd->bnd', probs, v)
            multihead = jnp.tile(atten, (1, 1, NUM_HEAD)).reshape(B, H, W, -1)
            mh = multihead @ W3 + b3
            c3 = c3 + mh.reshape(B, H, W, C)
            return x + c3
        key = jax.random.key(seed)
        ks = jax.random.split(key, 8)
        B, H, W, C = (4, 64, 64, 128)
        DQK, DV = (4, 16)
        s = 0.02
        return {'x': jax.random.normal(ks[0], (B, H, W, C), dtype=jnp.float32), 'W1': jax.random.normal(ks[1], (3, 3, C, C), dtype=jnp.float32) * s, 'b1': jnp.zeros((C,), jnp.float32), 'W2': jax.random.normal(ks[2], (3, 3, C, 2 * C), dtype=jnp.float32) * s, 'b2': jnp.zeros((2 * C,), jnp.float32), 'Wq': jax.random.normal(ks[3], (C, DQK), dtype=jnp.float32) * s, 'bq': jnp.zeros((DQK,), jnp.float32), 'Wk': jax.random.normal(ks[4], (C, DQK), dtype=jnp.float32) * s, 'bk': jnp.zeros((DQK,), jnp.float32), 'Wv': jax.random.normal(ks[5], (C, DV), dtype=jnp.float32) * s, 'bv': jnp.zeros((DV,), jnp.float32), 'W3': jax.random.normal(ks[6], (NUM_HEAD * DV, C), dtype=jnp.float32) * s, 'b3': jnp.zeros((C,), jnp.float32)}
    _L0_conv_all = _L0_conv_setup()
    _L0_conv_in = {k: v for k, v in _L0_conv_all.items() if k in ('W1', 'b1', 'W2', 'b2', 'Wq', 'bq', 'Wk', 'bk', 'Wv', 'bv', 'W3', 'b3', )}
    del _L0_conv_all

    def _L1_attn_setup():
        import jax, jax.numpy as jnp
        import numpy as np
        CHUNK = 64
        D_MODEL = 128
        D_STATE = 64
        HEADDIM = 64
        D_INNER = 2 * D_MODEL
        NHEADS = D_INNER // HEADDIM
        CONV_DIM = D_INNER + 2 * D_STATE
        K = 4
        D_IN_PROJ = 2 * D_INNER + 2 * D_STATE + NHEADS
        EPS = 1e-05

        def _segsum(t):
            L = t.shape[-1]
            cs = jnp.cumsum(t, -1)
            seg = cs[..., :, None] - cs[..., None, :]
            mask = jnp.tril(jnp.ones((L, L), bool))
            return jnp.where(mask, seg, -jnp.inf)

        def _ssd(xh, dt, A, Bm, Cm):
            b, l, h, p = xh.shape
            n = Bm.shape[-1]
            c = l // CHUNK
            xdt = xh * dt[..., None]
            dA = dt * A
            rc = lambda t: t.reshape(b, c, CHUNK, *t.shape[2:])
            xc, dAc, Bc, Cc = (rc(xdt), rc(dA), rc(Bm), rc(Cm))
            Acs = jnp.cumsum(dAc, axis=2)
            Lmat = jnp.exp(_segsum(dAc.transpose(0, 1, 3, 2)))
            Y_diag = jnp.einsum('bcln,bcsn,bchls,bcshp->bclhp', Cc, Bc, Lmat, xc)
            decay_st = jnp.exp(Acs[:, :, -1:, :] - Acs)
            states = jnp.einsum('bcln,bclh,bclhp->bchpn', Bc, decay_st, xc)
            chunk_decay = jnp.exp(Acs[:, :, -1])

            def step(carry, inp):
                st, dec = inp
                new = st + carry * dec[:, :, None, None]
                return (new, carry)
            init = jnp.zeros((b, h, p, n), xh.dtype)
            _, prev = jax.lax.scan(step, init, (states.transpose(1, 0, 2, 3, 4), chunk_decay.transpose(1, 0, 2)))
            prev = prev.transpose(1, 0, 2, 3, 4)
            Y_off = jnp.einsum('bcln,bchpn,bclh->bclhp', Cc, prev, jnp.exp(Acs))
            return (Y_diag + Y_off).reshape(b, l, h, p)

        def _mamba3(x, in_proj, conv_w, conv_b, A_log, dt_bias, D, norm_w, out_proj):
            b, l, _ = x.shape
            zxbcdt = x @ in_proj
            z, xbc, dt = jnp.split(zxbcdt, [D_INNER, D_INNER + CONV_DIM], axis=-1)
            xp = jnp.pad(xbc, ((0, 0), (K - 1, 0), (0, 0)))
            conv = sum((xp[:, i:i + l, :] * conv_w[:, i] for i in range(K))) + conv_b
            xbc = jax.nn.silu(conv)
            xh, Bm, Cm = jnp.split(xbc, [D_INNER, D_INNER + D_STATE], axis=-1)
            xh = xh.reshape(b, l, NHEADS, HEADDIM)
            dt = jax.nn.softplus(dt + dt_bias)
            A = -jnp.exp(A_log)
            y = _ssd(xh, dt, A, Bm, Cm) + xh * D[None, None, :, None]
            yg = y.reshape(b, l, D_INNER) * jax.nn.silu(z)
            yn = yg * jax.lax.rsqrt(jnp.mean(yg * yg, -1, keepdims=True) + EPS) * norm_w
            return yn @ out_proj
        key = jax.random.key(seed)
        ks = jax.random.split(key, 19)
        inp = {'x': jax.random.normal(ks[0], (16, 4096, D_MODEL), jnp.float32)}
        for i, pre in enumerate(['fwd', 'bwd']):
            o = 1 + 9 * i
            inp[pre + '_in_proj'] = jax.random.normal(ks[o], (D_MODEL, D_IN_PROJ), jnp.float32) * D_MODEL ** (-0.5)
            inp[pre + '_conv_w'] = jax.random.normal(ks[o + 1], (CONV_DIM, K), jnp.float32) * 0.3
            inp[pre + '_conv_b'] = jnp.zeros((CONV_DIM,), jnp.float32)
            inp[pre + '_A_log'] = jnp.log(jax.random.uniform(ks[o + 2], (NHEADS,), jnp.float32, 1.0, 16.0))
            inp[pre + '_dt_bias'] = jax.random.normal(ks[o + 3], (NHEADS,), jnp.float32) * 0.5
            inp[pre + '_D'] = jnp.ones((NHEADS,), jnp.float32)
            inp[pre + '_norm_w'] = jnp.ones((D_INNER,), jnp.float32)
            inp[pre + '_out_proj'] = jax.random.normal(ks[o + 4], (D_INNER, D_MODEL), jnp.float32) * D_INNER ** (-0.5)
        return inp
    _L1_attn_all = _L1_attn_setup()
    _L1_attn_in = {k: v for k, v in _L1_attn_all.items() if k in ('fwd_in_proj', 'fwd_conv_w', 'fwd_conv_b', 'fwd_A_log', 'fwd_dt_bias', 'fwd_D', 'fwd_norm_w', 'fwd_out_proj', 'bwd_in_proj', 'bwd_conv_w', 'bwd_conv_b', 'bwd_A_log', 'bwd_dt_bias', 'bwd_D', 'bwd_norm_w', 'bwd_out_proj', )}
    del _L1_attn_all

    def _L1_ffn_setup():
        import jax, jax.numpy as jnp
        import numpy as np
        PADDED_SL = 8192
        TEMPERATURE = 1.0
        SIGMA_POW = 0.25

        def _stu_conv(phi, u, n):
            b, sl, d = u.shape
            sgn = jnp.where(jnp.arange(sl) % 2 == 0, 1.0, -1.0).astype(u.dtype)
            sgn3 = sgn[None, :, None]
            Vf = jnp.fft.rfft(phi, n=n, axis=0)
            Uf_p = jnp.fft.rfft(u, n=n, axis=1)
            Uf_m = jnp.fft.rfft(u * sgn3, n=n, axis=1)
            U_plus = jnp.fft.irfft(Vf[None, :, :, None] * Uf_p[:, :, None, :], n=n, axis=1)[:, :sl]
            U_minus = jnp.fft.irfft(Vf[None, :, :, None] * Uf_m[:, :, None, :], n=n, axis=1)[:, :sl]
            U_minus = U_minus * sgn[None, :, None, None]
            return (U_plus, U_minus)

        def _compute_spectral(u, sigma, phi, Mpp, Mpm):
            U_plus, U_minus = _stu_conv(phi, u, PADDED_SL)
            s = sigma ** SIGMA_POW
            out = jnp.einsum('btkd,k,kde->bte', U_plus, s, Mpp)
            out = out + jnp.einsum('btkd,k,kde->bte', U_minus, s, Mpm)
            return out

        def _compute_ar_u(Mu, u):
            sl = u.shape[1]
            out = jnp.zeros(u.shape[:2] + (Mu.shape[-1],), dtype=u.dtype)
            for i in range(Mu.shape[0]):
                ui = jnp.pad(u, ((0, 0), (i, 0), (0, 0)))[:, :sl]
                out = out + jnp.einsum('btd,de->bte', ui, Mu[i])
            return out

        def _stu(u, sigma, phi, Mu, Mpp, Mpm):
            return _compute_spectral(u, sigma, phi, Mpp, Mpm) + _compute_ar_u(Mu, u)
        key = jax.random.key(seed)
        ks = jax.random.split(key, 8)
        b, sl, d, K, k_u = (2, 4096, 128, 16, 3)
        x = jax.random.normal(ks[0], (b, sl, d), dtype=jnp.float32)
        sigma = jax.random.uniform(ks[1], (K,), dtype=jnp.float32, minval=0.001, maxval=1.0)
        phi = jax.random.normal(ks[2], (sl, K), dtype=jnp.float32) / np.sqrt(sl)
        M_u = jax.random.normal(ks[3], (4, k_u, d, d), dtype=jnp.float32) * 0.02
        M_phi_plus = jax.random.normal(ks[4], (4, K, d, d), dtype=jnp.float32) * 0.02
        M_phi_minus = jax.random.normal(ks[5], (4, K, d, d), dtype=jnp.float32) * 0.02
        log_weights = jnp.ones((4,), dtype=jnp.float32)
        u01 = jax.random.uniform(ks[6], (4,), dtype=jnp.float32, minval=1e-06, maxval=1.0 - 1e-06)
        gumbel = -jnp.log(-jnp.log(u01))
        return {'x': x, 'sigma': sigma, 'phi': phi, 'M_u': M_u, 'M_phi_plus': M_phi_plus, 'M_phi_minus': M_phi_minus, 'log_weights': log_weights, 'gumbel': gumbel}
    _L1_ffn_all = _L1_ffn_setup()
    _L1_ffn_in = {k: v for k, v in _L1_ffn_all.items() if k in ('sigma', 'phi', 'M_u', 'M_phi_plus', 'M_phi_minus', 'log_weights', 'gumbel', )}
    del _L1_ffn_all

    return {
        "x": x,
        "L0_conv_W1": _L0_conv_in["W1"],
        "L0_conv_b1": _L0_conv_in["b1"],
        "L0_conv_W2": _L0_conv_in["W2"],
        "L0_conv_b2": _L0_conv_in["b2"],
        "L0_conv_Wq": _L0_conv_in["Wq"],
        "L0_conv_bq": _L0_conv_in["bq"],
        "L0_conv_Wk": _L0_conv_in["Wk"],
        "L0_conv_bk": _L0_conv_in["bk"],
        "L0_conv_Wv": _L0_conv_in["Wv"],
        "L0_conv_bv": _L0_conv_in["bv"],
        "L0_conv_W3": _L0_conv_in["W3"],
        "L0_conv_b3": _L0_conv_in["b3"],
        "L1_attn_fwd_in_proj": _L1_attn_in["fwd_in_proj"],
        "L1_attn_fwd_conv_w": _L1_attn_in["fwd_conv_w"],
        "L1_attn_fwd_conv_b": _L1_attn_in["fwd_conv_b"],
        "L1_attn_fwd_A_log": _L1_attn_in["fwd_A_log"],
        "L1_attn_fwd_dt_bias": _L1_attn_in["fwd_dt_bias"],
        "L1_attn_fwd_D": _L1_attn_in["fwd_D"],
        "L1_attn_fwd_norm_w": _L1_attn_in["fwd_norm_w"],
        "L1_attn_fwd_out_proj": _L1_attn_in["fwd_out_proj"],
        "L1_attn_bwd_in_proj": _L1_attn_in["bwd_in_proj"],
        "L1_attn_bwd_conv_w": _L1_attn_in["bwd_conv_w"],
        "L1_attn_bwd_conv_b": _L1_attn_in["bwd_conv_b"],
        "L1_attn_bwd_A_log": _L1_attn_in["bwd_A_log"],
        "L1_attn_bwd_dt_bias": _L1_attn_in["bwd_dt_bias"],
        "L1_attn_bwd_D": _L1_attn_in["bwd_D"],
        "L1_attn_bwd_norm_w": _L1_attn_in["bwd_norm_w"],
        "L1_attn_bwd_out_proj": _L1_attn_in["bwd_out_proj"],
        "L1_ffn_sigma": _L1_ffn_in["sigma"],
        "L1_ffn_phi": _L1_ffn_in["phi"],
        "L1_ffn_M_u": _L1_ffn_in["M_u"],
        "L1_ffn_M_phi_plus": _L1_ffn_in["M_phi_plus"],
        "L1_ffn_M_phi_minus": _L1_ffn_in["M_phi_minus"],
        "L1_ffn_log_weights": _L1_ffn_in["log_weights"],
        "L1_ffn_gumbel": _L1_ffn_in["gumbel"],
    }

def reference(x, L0_conv_W1, L0_conv_b1, L0_conv_W2, L0_conv_b2, L0_conv_Wq, L0_conv_bq, L0_conv_Wk, L0_conv_bk, L0_conv_Wv, L0_conv_bv, L0_conv_W3, L0_conv_b3, L1_attn_fwd_in_proj, L1_attn_fwd_conv_w, L1_attn_fwd_conv_b, L1_attn_fwd_A_log, L1_attn_fwd_dt_bias, L1_attn_fwd_D, L1_attn_fwd_norm_w, L1_attn_fwd_out_proj, L1_attn_bwd_in_proj, L1_attn_bwd_conv_w, L1_attn_bwd_conv_b, L1_attn_bwd_A_log, L1_attn_bwd_dt_bias, L1_attn_bwd_D, L1_attn_bwd_norm_w, L1_attn_bwd_out_proj, L1_ffn_sigma, L1_ffn_phi, L1_ffn_M_u, L1_ffn_M_phi_plus, L1_ffn_M_phi_minus, L1_ffn_log_weights, L1_ffn_gumbel):
    import jax
    import jax.numpy as jnp
    def _L0_conv_ref(x, W1, b1, W2, b2, Wq, bq, Wk, bk, Wv, bv, W3, b3):
        import jax, jax.numpy as jnp
        import numpy as np
        NUM_HEAD = 8

        def conv_same(x, w, b):
            return jax.lax.conv_general_dilated(x, w, window_strides=(1, 1), padding='SAME', dimension_numbers=('NHWC', 'HWIO', 'NHWC')) + b

        def _gated_resnet(x, W1, b1, W2, b2, Wq, bq, Wk, bk, Wv, bv, W3, b3):
            B, H, W, C = x.shape
            c1 = conv_same(jax.nn.elu(x), W1, b1)
            c2 = conv_same(c1, W2, b2)
            a, b = jnp.split(c2, 2, axis=-1)
            c3 = a * jax.nn.sigmoid(b)
            N = H * W
            f = c3.reshape(B, N, C)
            q = f @ Wq + bq
            k = f @ Wk + bk
            v = f @ Wv + bv
            scale = jnp.float32(np.sqrt(C // 8))
            dot = jnp.einsum('bnd,bmd->bnm', q, k) / scale
            mask = jnp.tril(jnp.ones((N, N), jnp.float32), -1)
            dot = dot - (1.0 - mask) * 10000000000.0
            dot = dot - jnp.max(dot, axis=-1, keepdims=True)
            e = jnp.exp(dot) * mask
            probs = e / (jnp.sum(e, axis=-1, keepdims=True) + 1e-10)
            atten = jnp.einsum('bnm,bmd->bnd', probs, v)
            multihead = jnp.tile(atten, (1, 1, NUM_HEAD)).reshape(B, H, W, -1)
            mh = multihead @ W3 + b3
            c3 = c3 + mh.reshape(B, H, W, C)
            return x + c3
        return _gated_resnet(x, W1, b1, W2, b2, Wq, bq, Wk, bk, Wv, bv, W3, b3)

    def _L1_attn_ref(x, fwd_in_proj, fwd_conv_w, fwd_conv_b, fwd_A_log, fwd_dt_bias, fwd_D, fwd_norm_w, fwd_out_proj, bwd_in_proj, bwd_conv_w, bwd_conv_b, bwd_A_log, bwd_dt_bias, bwd_D, bwd_norm_w, bwd_out_proj):
        import jax, jax.numpy as jnp
        import numpy as np
        CHUNK = 64
        D_MODEL = 128
        D_STATE = 64
        HEADDIM = 64
        D_INNER = 2 * D_MODEL
        NHEADS = D_INNER // HEADDIM
        CONV_DIM = D_INNER + 2 * D_STATE
        K = 4
        D_IN_PROJ = 2 * D_INNER + 2 * D_STATE + NHEADS
        EPS = 1e-05

        def _segsum(t):
            L = t.shape[-1]
            cs = jnp.cumsum(t, -1)
            seg = cs[..., :, None] - cs[..., None, :]
            mask = jnp.tril(jnp.ones((L, L), bool))
            return jnp.where(mask, seg, -jnp.inf)

        def _ssd(xh, dt, A, Bm, Cm):
            b, l, h, p = xh.shape
            n = Bm.shape[-1]
            c = l // CHUNK
            xdt = xh * dt[..., None]
            dA = dt * A
            rc = lambda t: t.reshape(b, c, CHUNK, *t.shape[2:])
            xc, dAc, Bc, Cc = (rc(xdt), rc(dA), rc(Bm), rc(Cm))
            Acs = jnp.cumsum(dAc, axis=2)
            Lmat = jnp.exp(_segsum(dAc.transpose(0, 1, 3, 2)))
            Y_diag = jnp.einsum('bcln,bcsn,bchls,bcshp->bclhp', Cc, Bc, Lmat, xc)
            decay_st = jnp.exp(Acs[:, :, -1:, :] - Acs)
            states = jnp.einsum('bcln,bclh,bclhp->bchpn', Bc, decay_st, xc)
            chunk_decay = jnp.exp(Acs[:, :, -1])

            def step(carry, inp):
                st, dec = inp
                new = st + carry * dec[:, :, None, None]
                return (new, carry)
            init = jnp.zeros((b, h, p, n), xh.dtype)
            _, prev = jax.lax.scan(step, init, (states.transpose(1, 0, 2, 3, 4), chunk_decay.transpose(1, 0, 2)))
            prev = prev.transpose(1, 0, 2, 3, 4)
            Y_off = jnp.einsum('bcln,bchpn,bclh->bclhp', Cc, prev, jnp.exp(Acs))
            return (Y_diag + Y_off).reshape(b, l, h, p)

        def _mamba3(x, in_proj, conv_w, conv_b, A_log, dt_bias, D, norm_w, out_proj):
            b, l, _ = x.shape
            zxbcdt = x @ in_proj
            z, xbc, dt = jnp.split(zxbcdt, [D_INNER, D_INNER + CONV_DIM], axis=-1)
            xp = jnp.pad(xbc, ((0, 0), (K - 1, 0), (0, 0)))
            conv = sum((xp[:, i:i + l, :] * conv_w[:, i] for i in range(K))) + conv_b
            xbc = jax.nn.silu(conv)
            xh, Bm, Cm = jnp.split(xbc, [D_INNER, D_INNER + D_STATE], axis=-1)
            xh = xh.reshape(b, l, NHEADS, HEADDIM)
            dt = jax.nn.softplus(dt + dt_bias)
            A = -jnp.exp(A_log)
            y = _ssd(xh, dt, A, Bm, Cm) + xh * D[None, None, :, None]
            yg = y.reshape(b, l, D_INNER) * jax.nn.silu(z)
            yn = yg * jax.lax.rsqrt(jnp.mean(yg * yg, -1, keepdims=True) + EPS) * norm_w
            return yn @ out_proj
        h_f = _mamba3(x, fwd_in_proj, fwd_conv_w, fwd_conv_b, fwd_A_log, fwd_dt_bias, fwd_D, fwd_norm_w, fwd_out_proj)
        xr = x[:, ::-1, :]
        h_b = _mamba3(xr, bwd_in_proj, bwd_conv_w, bwd_conv_b, bwd_A_log, bwd_dt_bias, bwd_D, bwd_norm_w, bwd_out_proj)[:, ::-1, :]
        return h_f + h_b

    def _L1_ffn_ref(x, sigma, phi, M_u, M_phi_plus, M_phi_minus, log_weights, gumbel):
        import jax, jax.numpy as jnp
        import numpy as np
        PADDED_SL = 8192
        TEMPERATURE = 1.0
        SIGMA_POW = 0.25

        def _stu_conv(phi, u, n):
            b, sl, d = u.shape
            sgn = jnp.where(jnp.arange(sl) % 2 == 0, 1.0, -1.0).astype(u.dtype)
            sgn3 = sgn[None, :, None]
            Vf = jnp.fft.rfft(phi, n=n, axis=0)
            Uf_p = jnp.fft.rfft(u, n=n, axis=1)
            Uf_m = jnp.fft.rfft(u * sgn3, n=n, axis=1)
            U_plus = jnp.fft.irfft(Vf[None, :, :, None] * Uf_p[:, :, None, :], n=n, axis=1)[:, :sl]
            U_minus = jnp.fft.irfft(Vf[None, :, :, None] * Uf_m[:, :, None, :], n=n, axis=1)[:, :sl]
            U_minus = U_minus * sgn[None, :, None, None]
            return (U_plus, U_minus)

        def _compute_spectral(u, sigma, phi, Mpp, Mpm):
            U_plus, U_minus = _stu_conv(phi, u, PADDED_SL)
            s = sigma ** SIGMA_POW
            out = jnp.einsum('btkd,k,kde->bte', U_plus, s, Mpp)
            out = out + jnp.einsum('btkd,k,kde->bte', U_minus, s, Mpm)
            return out

        def _compute_ar_u(Mu, u):
            sl = u.shape[1]
            out = jnp.zeros(u.shape[:2] + (Mu.shape[-1],), dtype=u.dtype)
            for i in range(Mu.shape[0]):
                ui = jnp.pad(u, ((0, 0), (i, 0), (0, 0)))[:, :sl]
                out = out + jnp.einsum('btd,de->bte', ui, Mu[i])
            return out

        def _stu(u, sigma, phi, Mu, Mpp, Mpm):
            return _compute_spectral(u, sigma, phi, Mpp, Mpm) + _compute_ar_u(Mu, u)
        T = x.shape[1]
        outs = []
        for i, frac in enumerate((1, 2, 4, 8)):
            xi = x[:, :T // frac]
            si = _stu(xi, sigma, phi, M_u[i], M_phi_plus[i], M_phi_minus[i])
            si = jnp.pad(si, ((0, 0), (0, T - si.shape[1]), (0, 0)))
            outs.append(si)
        y_soft = jax.nn.softmax((log_weights + gumbel) / TEMPERATURE)
        y_hard = jax.nn.one_hot(jnp.argmax(y_soft), 4, dtype=y_soft.dtype)
        weights = y_hard - jax.lax.stop_gradient(y_soft) + y_soft
        stacked = jnp.stack(outs, axis=-1)
        return jnp.sum(stacked * weights, axis=-1)

    def _gn(v, G=32, eps=1e-5):
        B_, H_, W_, C_ = v.shape
        g = v.reshape(B_, H_, W_, G, C_ // G)
        m = jnp.mean(g, axis=(1, 2, 4), keepdims=True)
        s = jnp.var(g, axis=(1, 2, 4), keepdims=True)
        return ((g - m) / jnp.sqrt(s + eps)).reshape(v.shape)

    def _ln_c(v, eps=1e-6):
        m = jnp.mean(v, axis=-1, keepdims=True)
        s = jnp.var(v, axis=-1, keepdims=True)
        return (v - m) / jnp.sqrt(s + eps)

    def _ln_t(v, eps=1e-5):
        m = jnp.mean(v, axis=-1, keepdims=True)
        s = jnp.var(v, axis=-1, keepdims=True)
        return (v - m) / jnp.sqrt(s + eps)

    def _to_tokens(v):
        B_, H_, W_, C_ = v.shape
        return v.reshape(B_, H_ * W_, C_)
    def _from_tokens(t, like):
        return t.reshape(like.shape)

    x = _L0_conv_ref(x, L0_conv_W1, L0_conv_b1, L0_conv_W2, L0_conv_b2, L0_conv_Wq, L0_conv_bq, L0_conv_Wk, L0_conv_bk, L0_conv_Wv, L0_conv_bv, L0_conv_W3, L0_conv_b3)
    t = _to_tokens(x)
    t = t + _L1_attn_ref(_ln_t(t), L1_attn_fwd_in_proj, L1_attn_fwd_conv_w, L1_attn_fwd_conv_b, L1_attn_fwd_A_log, L1_attn_fwd_dt_bias, L1_attn_fwd_D, L1_attn_fwd_norm_w, L1_attn_fwd_out_proj, L1_attn_bwd_in_proj, L1_attn_bwd_conv_w, L1_attn_bwd_conv_b, L1_attn_bwd_A_log, L1_attn_bwd_dt_bias, L1_attn_bwd_D, L1_attn_bwd_norm_w, L1_attn_bwd_out_proj)
    t = t + _L1_ffn_ref(_ln_t(t), L1_ffn_sigma, L1_ffn_phi, L1_ffn_M_u, L1_ffn_M_phi_plus, L1_ffn_M_phi_minus, L1_ffn_log_weights, L1_ffn_gumbel)
    x = _from_tokens(t, x)
    return x


_drawn_inputs = setup_inputs


def setup_inputs(seed=0):
    import zlib

    import numpy as np

    out = dict(_drawn_inputs(seed))
    spreads = {'L0_conv_b1': (0.0, 0.1),
     'L0_conv_b2': (0.0, 0.1),
     'L0_conv_bq': (0.0, 2.0),
     'L0_conv_bk': (0.0, 2.0),
     'L0_conv_bv': (0.0, 0.1),
     'L0_conv_b3': (0.0, 0.1),
     'L1_attn_fwd_conv_b': (0.0, 0.1),
     'L1_attn_fwd_D': (1.0, 0.2),
     'L1_attn_fwd_norm_w': (1.0, 0.2),
     'L1_attn_bwd_conv_b': (0.0, 0.1),
     'L1_attn_bwd_D': (1.0, 0.2),
     'L1_attn_bwd_norm_w': (1.0, 0.2),
     'L1_ffn_log_weights': (1.0, 0.2)}
    factors = {'L0_conv_Wq': 64.0, 'L0_conv_Wk': 64.0, 'L0_conv_Wv': 8.0}
    for name, (base, spread) in spreads.items():
        noise = np.random.default_rng([zlib.crc32(name.encode()), seed]).standard_normal(out[name].shape)
        drawn = base * np.exp(spread * noise) if base else spread * noise
        out[name] = jnp.asarray(drawn.astype(out[name].dtype))
    for name, factor in factors.items():
        out[name] = (out[name] * factor).astype(out[name].dtype)
    return out
```

```python
from contextlib import ExitStack

import numpy as np

import concourse.bass as bass
from concourse import mybir

F32 = mybir.dt.float32
BF16 = mybir.dt.bfloat16
F32R = mybir.dt.float32r
ALU = mybir.AluOpType
ACT = mybir.ActivationFunctionType
AX = mybir.AxisListType

P = 128
B, IMG = 4, 64
T = IMG * IMG
N = B * T
BANK = 512
TILES = N // BANK

DQK, DV, HEADS = 4, 16, 8
PARTS = 3
PAIRS = PARTS * PARTS * DQK
MROW = 64
MASK1, MASK2 = -1.0e30, -2.0e38

CH = 128
NCH = T // CH
NH, HD, DS, DI = 4, 64, 64, 256
TAPS = 4

K = 16
BL, NB, HALF = 128, 32, 64
NF = 2 * NB
KG = 4
FRACS = (1, 2, 4, 8)


class Scope:

    def __init__(self, nc, sems, name):
        self.nc, self.sems, self.name, self.stack = nc, sems, name, ExitStack()

    def sb(self, name, shape, dt=F32):
        return self.stack.enter_context(self.nc.sbuf_tensor(f"{self.name}_{name}", shape, dt))

    def ps(self, name, shape, dt=F32):
        return self.stack.enter_context(self.nc.psum_tensor(f"{self.name}_{name}", shape, dt))

    def sem(self, name):
        self.sems.append(self.nc.alloc_semaphore(name=f"{self.name}_{name}"))
        return self.sems[-1]


def product(pe, out, stationary, moving, start, stop, **kw):
    for n, (a, b) in enumerate(((0, 0), (0, 1), (1, 0))):
        mm = pe.matmul(out, stationary[a], moving[b], start=start and n == 0, stop=stop and n == 2, **kw)
    return mm


def low_part(v, out, full, high):
    return v.tensor_tensor(out, full, high.bitcast(F32), ALU.subtract)


def hold(eng, passed):
    eng.sem_inc(passed, 1)


def release(nc, sems):
    nc.clear_and_free_semaphores(sems)
    nc.all_engine_barrier()
    sems.clear()


def layer_norm(nc, sems, name, addends, total, out, c_mean):
    s = Scope(nc, sems, name)
    na = len(addends)
    G, ITER = 4, TILES // 8
    with s.stack:
        mean_w = s.sb("mean_w", [P, P])
        eps = s.sb("eps", [P, 1])
        x = s.sb("x", [P, 2, na, G, BANK])
        xc = s.sb("xc", [P, 2, G, BANK])
        sq = s.sb("sq", [P, G, BANK])
        rs = s.sb("rs", [P, G, BANK])
        y = s.sb("y", [P, 2, G, BANK])
        mean = s.ps("mean", [P, G, BANK])
        var = s.ps("var", [P, G, BANK])
        loaded, stored = ([s.sem(f"{n}{k}") for k in range(2)] for n in ("loaded", "stored"))
        w_in, summed, mean_done, centred, squared, var_done, logged, rooted, normed, eps_set = (
            s.sem(n) for n in ("w_in", "summed", "mean_done", "centred", "squared", "var_done", "logged", "rooted",
                               "normed", "eps_set"))
        per_store = 16 * (2 if total is not None else 1)
        views = [a.rearrange("p (t n) -> p t n", n=G * BANK) for a in addends]
        out_v = out.rearrange("p (t n) -> p t n", n=G * BANK)
        tot_v = total.rearrange("p (t n) -> p t n", n=G * BANK) if total is not None else None
        flat = lambda ap: ap.rearrange("p g n -> p (g n)")
        with nc.Block() as block:

            @block.sync
            def _(sp):
                sp.dma_start(mean_w[:], c_mean).then_inc(w_in, 16)
                with sp.Fori(0, ITER) as i:
                    for k in range(2):
                        sp.wait_ge(normed, i * (2 * G) + (k + 1) * G)
                        sp.wait_ge(stored[k], i * per_store + per_store)
                        for a in range(na):
                            sp.dma_start(flat(x[:, k, a]), views[a][:, i * 2 + k, :]).then_inc(loaded[k], 16)

            @block.vector
            def _(v):
                v.memset(eps[:], 1e-5).then_inc(eps_set, 1)
                v.sem_inc(normed, 2 * G)
                v.sem_inc(centred, G)
                with v.Fori(0, ITER) as i:
                    for k in range(2):
                        v.wait_ge(loaded[k], i * (16 * na) + 16 * na)
                        for a in range(1, na):
                            for t in range(G):
                                if a > 1:
                                    v.wait_ge(summed, (i * 2 + k) * ((na - 1) * G) + (a - 2) * G + t + 1)
                                v.tensor_tensor(x[:, k, 0, t], x[:, k, 0, t], x[:, k, a, t], ALU.add
                                                ).then_inc(summed, 1)
                        for t in range(G):
                            v.wait_ge(mean_done, (i * 2 + k) * G + t + 1)
                            v.tensor_tensor(xc[:, k, t], x[:, k, 0, t], mean[:, t], ALU.subtract).then_inc(centred, 1)
                        v.wait_ge(stored[k], i * per_store + per_store)
                        for t in range(G):
                            v.wait_ge(rooted, (i * 2 + k) * G + t + 1)
                            v.tensor_tensor(y[:, k, t], xc[:, k, t], rs[:, t], ALU.mult).then_inc(normed, 1)

            @block.tensor
            def _(pe):
                pe.wait_ge(w_in, 16)
                with pe.Fori(0, ITER) as i:
                    for k in range(2):
                        pe.wait_ge(loaded[k], i * (16 * na) + 16 * na)
                        for t in range(G):
                            if na > 1:
                                pe.wait_ge(summed, (i * 2 + k) * ((na - 1) * G) + (na - 2) * G + t + 1)
                            pe.wait_ge(centred, (i * 2 + k) * G + t + 1)
                            pe.matmul(mean[:, t], mean_w[:], x[:, k, 0, t], start=True, stop=True
                                      ).then_inc(mean_done, 1)
                        for t in range(G):
                            pe.wait_ge(squared, (i * 2 + k) * G + t + 1)
                            pe.matmul(var[:, t], mean_w[:], sq[:, t], start=True, stop=True).then_inc(var_done, 1)

            @block.scalar
            def _(act):
                for k in range(2):
                    act.sem_inc(stored[k], per_store)
                act.wait_ge(eps_set, 1)
                with act.Fori(0, ITER) as i:
                    for k in range(2):
                        for t in range(G):
                            act.wait_ge(centred, (i * 2 + k) * G + t + 1 + G)
                            act.activation(sq[:, t], xc[:, k, t], ACT.Square).then_inc(squared, 1)
                        for t in range(G):
                            act.wait_ge(var_done, (i * 2 + k) * G + t + 1)
                            act.wait_ge(normed, (i * 2 + k) * G + t + 1 + G)
                            act.activation(rs[:, t], var[:, t], ACT.Ln, bias=eps[:, 0:1]).then_inc(logged, 1)
                        for t in range(G):
                            act.wait_ge(logged, (i * 2 + k) * G + t + 1)
                            act.activation(rs[:, t], rs[:, t], ACT.Exp, scale=-0.5).then_inc(rooted, 1)
                        act.wait_ge(normed, (i * 2 + k) * G + 3 * G)
                        act.dma_start(out_v[:, i * 2 + k, :], flat(y[:, k])).then_inc(stored[k], 16)
                        if total is not None:
                            act.dma_start(tot_v[:, i * 2 + k, :], flat(x[:, k, 0])).then_inc(stored[k], 16)
                for k in range(2):
                    act.wait_ge(stored[k], per_store * (ITER + 1))


PW = IMG + 2
ROWS = BANK // IMG
GT = T // BANK


def conv_block(nc, sems, g, c3):
    s = Scope(nc, sems, "conv")
    Q = 4
    QR = IMG // Q
    with s.stack:
        w1 = s.sb("w1", [P, 9, P])
        w2 = s.sb("w2", [P, 9, 2 * P])
        bias = s.sb("bias", [P, 3])
        x = s.sb("x", [P, IMG, IMG])
        neg = s.sb("neg", [P, 2, QR, IMG])
        pos = s.sb("pos", [P, 2, QR, IMG])
        ex = s.sb("ex", [P, 2, QR, IMG])
        xp = s.sb("xp", [P, PW, PW])
        c1 = s.sb("c1", [P, PW, PW])
        sg = s.sb("sg", [P, 2, BANK])
        co = s.sb("co", [P, 2, BANK])
        p1 = s.ps("p1", [P, 2, BANK])
        pa = s.ps("pa", [P, 2, BANK])
        pb = s.ps("pb", [P, 2, BANK])
        w_in, x_in, halves, exped, elu_done, c1_mm, c1_evac, c2_mm, gated, sig_done, bordered, passed = (
            s.sem(n) for n in ("w_in", "x_in", "halves", "exped", "elu_done", "c1_mm", "c1_evac", "c2_mm", "gated",
                               "sig_done", "bordered", "passed"))
        stored = [s.sem(f"stored{k}") for k in range(2)]
        xv = g["x"].rearrange("p (b h w) -> p b h w", b=B, h=IMG)
        cv = c3.rearrange("p (b g n) -> p b g n", b=B, g=GT)
        with nc.Block() as block:

            @block.sync
            def _(sp):
                sp.dma_start(x[:], xv[:, 0]).then_inc(x_in, 16)
                sp.dma_start(w1[:], g["W1"].rearrange("h w i o -> i (h w) o")).then_inc(w_in, 16)
                sp.dma_start(w2[:], g["W2"].rearrange("h w i o -> i (h w) o")).then_inc(w_in, 16)
                for k, name in enumerate(("b1", "b2a", "b2b")):
                    sp.dma_start(bias[:, k:k + 1], g[name]).then_inc(w_in, 16)
                with sp.Fori(0, B - 1) as b:
                    sp.wait_ge(halves, b * (2 * Q) + 2 * Q)
                    sp.dma_start(x[:], xv[:, b + 1]).then_inc(x_in, 16)

            @block.gpsimd
            def _(pool):
                with pool.Fori(0, B) as b:
                    pool.wait_ge(x_in, b * 16 + 16)
                    for q in range(Q):
                        pool.wait_ge(elu_done, b * Q + q + 1)
                        hold(pool, passed)
                        rows = x[:, q * QR:(q + 1) * QR, :]
                        pool.tensor_scalar(neg[:, q % 2], rows, 0.0, None, ALU.min).then_inc(halves, 1)
                        pool.tensor_scalar(pos[:, q % 2], rows, 0.0, None, ALU.max).then_inc(halves, 1)

            @block.tensor
            def _(pe):
                pe.sem_inc(c1_mm, GT)
                pe.wait_ge(w_in, 80)
                pe.wait_ge(bordered, 2)
                with pe.Fori(0, B) as b:
                    for t in range(GT):
                        pe.wait_ge(elu_done, b * Q + min(ROWS * (t + 1), IMG - 1) // QR + 1 + 2)
                        pe.wait_ge(c1_evac, b * GT + t + 1)
                        for k in range(9):
                            dy, dx = divmod(k, 3)
                            mm = pe.matmul(p1[:, t % 2, :], w1[:, k, :],
                                           xp[:, t * ROWS + dy:t * ROWS + dy + ROWS, dx:dx + IMG],
                                           start=(k == 0), stop=(k == 8))
                        mm.then_inc(c1_mm, 1)
                    for t in range(GT):
                        pe.wait_ge(c1_evac, b * GT + min(t + 2, GT) + 2)
                        pe.wait_ge(gated, b * GT + t + 1)
                        for half, bank in enumerate((pa, pb)):
                            for k in range(9):
                                dy, dx = divmod(k, 3)
                                mm = pe.matmul(bank[:, t % 2, :], w2[:, k, half * P:(half + 1) * P],
                                               c1[:, t * ROWS + dy:t * ROWS + dy + ROWS, dx:dx + IMG],
                                               start=(k == 0), stop=(k == 8))
                        mm.then_inc(c2_mm, 1)

            @block.scalar
            def _(act):
                act.sem_inc(c1_evac, 2)
                for k in range(2):
                    act.sem_inc(stored[k], 16)

                def exps(b):
                    for q in range(Q):
                        act.wait_ge(halves, b * (2 * Q) + 2 * q + 2)
                        act.activation(ex[:, q % 2], neg[:, q % 2], ACT.Exp).then_inc(exped, 1)

                def store(b, t):
                    act.wait_ge(gated, b * GT + t + 1 + 2)
                    act.dma_start(cv[:, b, t, :], co[:, t % 2, :]).then_inc(stored[t % 2], 16)

                def batch(b):
                    for t in range(GT):
                        act.wait_ge(c1_mm, b * GT + t + 1 + GT)
                        act.activation(c1[:, 1 + t * ROWS:1 + (t + 1) * ROWS, 1:1 + IMG],
                                       p1[:, t % 2, :].rearrange("p (r c) -> p r c", c=IMG), ACT.Identity,
                                       bias=bias[:, 0:1]).then_inc(c1_evac, 1)
                    for t in range(GT):
                        act.wait_ge(c2_mm, b * GT + t + 1)
                        act.activation(sg[:, t % 2, :], pb[:, t % 2, :], ACT.Sigmoid, bias=bias[:, 2:3]
                                       ).then_inc(sig_done, 1)
                        if t:
                            store(b, t - 1)
                    store(b, GT - 1)

                act.wait_ge(w_in, 80)
                act.wait_ge(bordered, 2)
                exps(0)
                with act.Fori(0, B - 1) as b:
                    batch(b)
                    exps(b + 1)
                batch(B - 1)
                for k in range(2):
                    act.wait_ge(stored[k], 16 * (B * GT // 2 + 1))

            @block.vector
            def _(v):
                v.sem_inc(elu_done, 2)
                v.sem_inc(gated, 2)
                v.memset(xp[:], 0.0).then_inc(bordered, 1)
                v.memset(c1[:], 0.0).then_inc(bordered, 1)
                v.wait_ge(bordered, 2)

                def elus(b):
                    v.wait_ge(c1_mm, b * GT + GT)
                    for q in range(Q):
                        v.wait_ge(exped, b * Q + q + 1)
                        v.scalar_tensor_tensor(xp[:, 1 + q * QR:1 + (q + 1) * QR, 1:1 + IMG], ex[:, q % 2], -1.0,
                                               pos[:, q % 2], ALU.add, ALU.add).then_inc(elu_done, 1)

                def gates(b):
                    for t in range(GT):
                        v.wait_ge(sig_done, b * GT + t + 1)
                        v.wait_ge(stored[t % 2], b * (16 * GT // 2) + (t // 2) * 16 + 16)
                        v.scalar_tensor_tensor(co[:, t % 2, :], pa[:, t % 2, :], bias[:, 1:2], sg[:, t % 2, :],
                                               ALU.add, ALU.mult).then_inc(gated, 1)

                elus(0)
                with v.Fori(0, B - 1) as b:
                    gates(b)
                    elus(b + 1)
                gates(B - 1)


def attention_constants():
    rows = np.arange(P)
    sel = np.zeros((P, 4), np.float32)
    for side in range(2):
        for i in range(PARTS):
            for j in range(PARTS):
                part = (i, j)[side]
                for d in range(DQK):
                    r = 64 * side + (i * PARTS + j) * DQK + d
                    sel[r, 0], sel[r, 1] = -float(part >= 1), -float(part >= 2)
    for part in range(PARTS):
        sel[MROW + part, 2], sel[MROW + part, 3] = -float(part >= 1), -float(part >= 2)
    mask = np.stack([np.where(rows[None, :] >= rows[:, None], MASK1, 0.0),
                     np.where(rows[:, None] >= rows[None, :], MASK2, 0.0)])
    fold = (rows[:, None] % DV == np.arange(DV)[None, :]).astype(np.float32)
    return {"c_sel": sel, "c_mask": mask.astype(np.float32), "c_ident": np.eye(P, dtype=np.float32),
            "c_fold": fold}


def attention(nc, sems, g, c3, t0):
    s = Scope(nc, sems, "att")
    m_dram = nc.dram_tensor("row_max", (B, T), F32, kind="Internal").ap()
    with s.stack:
        qs = s.sb("qs", [MROW + PARTS, B, T], BF16)
        ks = s.sb("ks", [MROW + PARTS, B, T], BF16)
        va = s.sb("va", [P, B, T // P, 48])
        ident = s.sb("ident", [P, P])
        identb = s.sb("identb", [P, P], BF16)
        mask = s.sb("mask", [P, 2, P], BF16)
        sel = s.sb("sel", [P, 4])
        attention_maximum(nc, sems, g, c3, m_dram, qs, ks, va, ident, identb, mask, sel)
        attention_rows(nc, sems, m_dram, qs, sel)
        attention_values(nc, sems, g, c3, t0, qs, ks, va, identb, mask)


def attention_maximum(nc, sems, g, c3, m_dram, qs, ks, va, ident, identb, mask, sel):
    s = Scope(nc, sems, "amax")
    NT = T // P
    units = [[(i, u) for u in range((i // 4 + 2) // 2)] for i in range(NT)]
    flat = [x for r in units for x in r]
    NU = len(flat)
    with s.stack:
        wqk = s.sb("wqk", [P, P])
        wv = s.sb("wv", [P, DV])
        bqk = s.sb("bqk", [P, 1])
        bv = s.sb("bv", [P, DV])
        mk = s.sb("mk", [P, 2, P])
        f = s.sb("f", [P, T])
        qf = s.sb("qf", [P, 2, BANK])
        h1 = s.sb("h1", [P, 2, BANK], BF16)
        r1 = s.sb("r1", [P, 2, BANK])
        h2 = s.sb("h2", [P, 2, BANK], BF16)
        mp = s.sb("mp", [P, NT, 4])
        mall = s.sb("mall", [P, NT])
        mt = s.sb("mt", [NT, P])
        pq = s.ps("pq", [P, 2, BANK])
        pv = s.ps("pv", [P, BANK])
        pm = s.ps("pm", [NT, P])
        sc = s.ps("sc", [P, 2, 2 * BANK])
        w_in, f_in, qk_mm, v_mm, qf_done, h1_done, r1_done, h2_done, split, v_done, sc_mm, maxed, m_done, mt_mm, \
            mt_done, m_stored, ready = (s.sem(n) for n in (
                "w_in", "f_in", "qk_mm", "v_mm", "qf_done", "h1_done", "r1_done", "h2_done", "split", "v_done",
                "sc_mm", "maxed", "m_done", "mt_mm", "mt_done", "m_stored", "ready"))
        cv = c3.rearrange("p (b n) -> p b n", b=B)
        NW = 7 * 16
        with nc.Block() as block:

            @block.sync
            def _(sp):
                for dst, name in ((wqk[:], "Wqk"), (wv[:], "Wv"), (bqk[:], "bqk"), (bv[:], "bv"), (ident[:], "c_ident"),
                                  (sel[:], "c_sel"), (mk[:], "c_mask")):
                    src = g[name].rearrange("m p n -> p m n") if name == "c_mask" else g[name]
                    sp.dma_start(dst, src).then_inc(w_in, 16)
                with sp.Fori(0, B) as b:
                    sp.wait_ge(v_mm, b + 1)
                    sp.dma_start(f[:], cv[:, b, :]).then_inc(f_in, 16)

            @block.gpsimd
            def _(pool):
                pool.wait_ge(w_in, NW)
                pool.tensor_copy(identb[:], ident[:]).then_inc(ready, 1)
                pool.tensor_copy(mask[:], mk[:]).then_inc(ready, 1)
                pool.memset(va[:, :, :, DV:2 * DV], 0.0).then_inc(ready, 1)
                pool.memset(va[:, :, :, 2 * DV:3 * DV], 1.0).then_inc(ready, 1)

            @block.tensor
            def _(pe):
                pe.sem_inc(v_mm, 1)
                pe.wait_ge(w_in, NW)
                pe.wait_ge(ready, 7)
                with pe.Fori(0, B) as b:
                    pe.wait_ge(f_in, b * 16 + 16)
                    for t in range(GT):
                        pe.wait_ge(qf_done, b * GT + t + 1)
                        pe.matmul(pq[:, t % 2, :], wqk[:], f[:, t * BANK:(t + 1) * BANK], start=True, stop=True
                                  ).then_inc(qk_mm, 1)
                    pe.wait_ge(v_done, b + 1)
                    for t in range(NT):
                        mm = pe.matmul(pv[:, t * DV:(t + 1) * DV], f[:, t * P:(t + 1) * P], wv[:], start=True,
                                       stop=True, skip_group_check=True)
                    mm.then_inc(v_mm, 1)
                    for n, (i, u) in enumerate(flat):
                        if u == 0 and i % 4 == 0:
                            pe.wait_ge(split, b * (2 * GT) + 2 * (i // 4 + 1) + 4)
                        pe.wait_ge(maxed, b * NU + n + 1)
                        for bank in range(2 * u, min(2 * u + 2, i // 4 + 1)):
                            diag = bank == i // 4
                            wid = (i % 4 + 1) * P if diag else BANK
                            o = (bank - 2 * u) * BANK
                            mm = pe.matmul(sc[:, n % 2, o:o + wid], qs[:, b, i * P:(i + 1) * P],
                                           ks[:, b, bank * BANK:bank * BANK + wid], start=True, stop=not diag,
                                           skip_group_check=True)
                            if diag:
                                mm = pe.matmul(sc[:, n % 2, o + wid - P:o + wid], identb[:], mask[:, 0, :],
                                               start=False, stop=True, skip_group_check=True)
                        mm.then_inc(sc_mm, 1)
                    pe.wait_ge(m_done, b + 1)
                    pe.wait_ge(mt_done, b + 1)
                    pe.transpose(pm[:], mall[:], ident[:]).then_inc(mt_mm, 1)

            @block.scalar
            def _(act):
                act.sem_inc(qf_done, 2)
                act.sem_inc(mt_done, 1)
                act.sem_inc(m_stored, 16)
                act.wait_ge(w_in, NW)
                with act.Fori(0, B) as b:
                    for t in range(GT + 1):
                        if t < GT:
                            act.wait_ge(qk_mm, b * GT + t + 1)
                            act.wait_ge(split, b * (2 * GT) + 2 * t + 2)
                            act.activation(qf[:, t % 2, :], pq[:, t % 2, :], ACT.Identity, bias=bqk[:, 0:1]
                                           ).then_inc(qf_done, 1)
                            act.wait_ge(qf_done, b * GT + t + 1 + 2)
                            act.activation(h1[:, t % 2, :], qf[:, t % 2, :], ACT.Copy).then_inc(h1_done, 1)
                        if t:
                            act.wait_ge(r1_done, b * GT + t)
                            act.activation(h2[:, (t - 1) % 2, :], r1[:, (t - 1) % 2, :], ACT.Copy).then_inc(h2_done, 1)
                    act.wait_ge(mt_mm, b + 1)
                    act.wait_ge(m_stored, b * 16 + 16)
                    act.activation(mt[:], pm[:], ACT.Copy).then_inc(mt_done, 1)
                    act.wait_ge(mt_done, b + 2)
                    act.dma_start(m_dram[b].rearrange("(t q) -> t q", q=P), mt[:]).then_inc(m_stored, 16)
                act.wait_ge(m_stored, 16 * (B + 1))

            @block.vector
            def _(v):
                v.memset(ks[MROW:MROW + PARTS], -1.0).then_inc(ready, 1)
                v.memset(qs[MROW:MROW + PARTS], 0.0).then_inc(ready, 1)
                v.memset(mp[:], MASK2).then_inc(ready, 1)
                v.sem_inc(v_done, 1)
                v.sem_inc(maxed, 2)
                v.sem_inc(split, 4)
                v.wait_ge(w_in, NW)
                v.wait_ge(ready, 7)
                with v.Fori(0, B) as b:
                    for t in range(GT + 1):
                        if t < GT:
                            v.wait_ge(h1_done, b * GT + t + 1)
                            v.scalar_tensor_tensor(r1[:, t % 2, :], h1[:, t % 2, :], sel[:, 0:1], qf[:, t % 2, :],
                                                   ALU.mult, ALU.add).then_inc(r1_done, 1)
                        if t:
                            k = t - 1
                            v.wait_ge(h2_done, b * GT + t)
                            for dst, p0 in ((qs, 0), (ks, 64)):
                                v.scalar_tensor_tensor(dst[0:64, b, k * BANK:(k + 1) * BANK],
                                                       h2[p0:p0 + 64, k % 2, :], sel[p0:p0 + 64, 1:2],
                                                       r1[p0:p0 + 64, k % 2, :], ALU.mult, ALU.add
                                                       ).then_inc(split, 1)
                    v.wait_ge(v_mm, b + 2)
                    v.tensor_tensor(va[:, b, :, 0:DV], pv[:].rearrange("p (t d) -> p t d", d=DV),
                                    bv[:].unsqueeze(1).broadcast_to((P, NT, DV)), ALU.add).then_inc(v_done, 1)
                    for n, (i, u) in enumerate(flat):
                        v.wait_ge(sc_mm, b * NU + n + 1)
                        wid = min(2 * BANK, (i + 1) * P - u * 2 * BANK)
                        v.tensor_reduce(mp[:, i, u:u + 1], sc[:, n % 2, 0:wid], AX.X, ALU.max).then_inc(maxed, 1)
                    v.wait_ge(maxed, b * NU + NU + 2)
                    v.wait_ge(mt_done, b + 1)
                    v.tensor_reduce(mall[:], mp[:], AX.X, ALU.max).then_inc(m_done, 1)


def attention_rows(nc, sems, m_dram, qs, sel):
    s = Scope(nc, sems, "arow")
    MH = T // 2
    with s.stack:
        m = s.sb("m", [MROW + PARTS, 2, MH])
        h = s.sb("h", [MROW + PARTS, 2, MH], BF16)
        r = s.sb("r", [MROW + PARTS, 2, MH])
        h2 = s.sb("h2", [MROW + PARTS, 2, MH], BF16)
        h_done, r_done, h2_done, split = (s.sem(n) for n in ("h_done", "r_done", "h2_done", "split"))
        m_in = [s.sem(f"m_in{k}") for k in range(2)]
        rows = slice(MROW, MROW + PARTS)
        with nc.Block() as block:

            @block.sync
            def _(sp):
                with sp.Fori(0, B) as b:
                    for k in range(2):
                        sp.wait_ge(split, b * 2 + k + 1)
                        for r0 in range(PARTS):
                            sp.dma_start(m[MROW + r0:MROW + r0 + 1, k, :], m_dram[bass.ds(b, 1), k * MH:(k + 1) * MH]
                                         ).then_inc(m_in[k], 16)

            @block.scalar
            def _(act):
                with act.Fori(0, B) as b:
                    for k in range(2):
                        act.wait_ge(m_in[k], b * (16 * PARTS) + 16 * PARTS)
                        act.activation(h[rows, k], m[rows, k], ACT.Copy).then_inc(h_done, 1)
                    for k in range(2):
                        act.wait_ge(r_done, b * 2 + k + 1)
                        act.activation(h2[rows, k], r[rows, k], ACT.Copy).then_inc(h2_done, 1)

            @block.vector
            def _(v):
                v.sem_inc(split, 2)
                with v.Fori(0, B) as b:
                    for k in range(2):
                        v.wait_ge(h_done, b * 2 + k + 1)
                        v.scalar_tensor_tensor(r[rows, k], h[rows, k], sel[rows, 2:3], m[rows, k], ALU.mult, ALU.add
                                               ).then_inc(r_done, 1)
                    for k in range(2):
                        v.wait_ge(h2_done, b * 2 + k + 1)
                        v.scalar_tensor_tensor(qs[rows, b, k * MH:(k + 1) * MH], h2[rows, k], sel[rows, 3:4],
                                               r[rows, k], ALU.mult, ALU.add).then_inc(split, 1)


def attention_values(nc, sems, g, c3, t0, qs, ks, va, identb, mask):
    s = Scope(nc, sems, "aval")
    items = [(G, kt) for G in range(GT) for kt in range(4 * G + 4)]
    NI = len(items)
    first = {G: 2 * G * (G + 1) for G in range(GT + 1)}
    LAG, NS, NE = 2, 4, 4
    with s.stack:
        fold = s.sb("fold", [P, DV])
        w3 = s.sb("w3", [P, P])
        w3s = s.sb("w3s", [DV, P])
        b3 = s.sb("b3", [P, 1])
        vc = s.sb("vc", [P, T // P, 48])
        e = s.sb("e", [P, NE, BANK])
        xr = s.sb("xr", [P, 2, BANK])
        cr = s.sb("cr", [P, 2, BANK])
        den = s.sb("den", [DV, BANK])
        rec = s.sb("rec", [DV, BANK])
        at = s.sb("at", [DV, BANK])
        o1 = s.sb("o1", [P, BANK])
        o2 = s.sb("o2", [P, 2, BANK])
        sc = s.ps("sc", [P, NS, BANK])
        po = s.ps("po", [64, 2, BANK])
        pm = s.ps("pm", [P, 2, BANK])
        w_in, fold_mm, fold_done, vc_done, sc_mm, exped, pv_mm, den_done, rec_done, at_done, mh_mm, o1_done, o2_done \
            = (s.sem(n) for n in ("w_in", "fold_mm", "fold_done", "vc_done", "sc_mm", "exped", "pv_mm", "den_done",
                                  "rec_done", "at_done", "mh_mm", "o1_done", "o2_done"))
        r_in = [s.sem(f"r_in{k}") for k in range(2)]
        stored = [s.sem(f"stored{k}") for k in range(2)]
        xv, cv, tv = (a.rearrange("p (b g n) -> p b g n", b=B, g=GT) for a in (g["x"], c3, t0))
        with nc.Block() as block:

            @block.sync
            def _(sp):
                for dst, name in ((fold, "c_fold"), (w3, "W3"), (b3, "b3")):
                    sp.dma_start(dst[:], g[name]).then_inc(w_in, 16)
                with sp.Fori(0, B) as b:
                    for G in range(GT):
                        sp.wait_ge(o2_done, b * GT + G + 1)
                        sp.dma_start(xr[:, G % 2, :], xv[:, b, G, :]).then_inc(r_in[G % 2], 16)
                        sp.dma_start(cr[:, G % 2, :], cv[:, b, G, :]).then_inc(r_in[G % 2], 16)

            @block.gpsimd
            def _(pool):
                with pool.Fori(0, B) as b:
                    pool.wait_ge(pv_mm, b * NI + NI)
                    pool.tensor_copy(vc[:], va[:, b]).then_inc(vc_done, 1)

            @block.tensor
            def _(pe):
                pe.sem_inc(pv_mm, NI)
                pe.wait_ge(w_in, 48)
                pe.matmul(pm[0:DV, 0, 0:P], fold[:], w3[:], start=True, stop=True).then_inc(fold_mm, 1)
                pe.wait_ge(fold_done, 1)
                with pe.Fori(0, B) as b:

                    def scores(n):
                        G, kt = items[n]
                        c0 = max(0, kt - 4 * G) * P
                        diag = kt >= 4 * G
                        pe.wait_ge(exped, b * NI + n + 1)
                        mm = pe.matmul(sc[:, n % NS, c0:], ks[:, b, kt * P:(kt + 1) * P],
                                       qs[:, b, G * BANK + c0:(G + 1) * BANK], start=True, stop=not diag)
                        if diag:
                            mm = pe.matmul(sc[:, n % NS, c0:c0 + P], identb[:], mask[:, 1, :], start=False, stop=True)
                        mm.then_inc(sc_mm, 1)

                    def values(n):
                        G, kt = items[n]
                        c0 = max(0, kt - 4 * G) * P
                        if n == 0:
                            pe.wait_ge(vc_done, b + 1)
                        if kt == 0:
                            pe.wait_ge(at_done, b * GT + G + 1)
                        pe.wait_ge(exped, b * NI + n + 1 + NS)
                        pe.matmul(po[0:48, G % 2, c0:], vc[:, kt, :], e[:, n % NE, c0:], start=(kt == 0),
                                  stop=(kt == 4 * G + 3)).then_inc(pv_mm, 1)

                    def project(G):
                        pe.wait_ge(at_done, b * GT + G + 1 + 2)
                        pe.wait_ge(o1_done, b * GT + G + 1)
                        pe.matmul(pm[:, G % 2, :], w3s[:], at[:], start=True, stop=True).then_inc(mh_mm, 1)

                    for n in range(NI + LAG):
                        if n < NI:
                            scores(n)
                        if n >= LAG:
                            values(n - LAG)
                            G, kt = items[n - LAG]
                            if kt == 3 and G:
                                project(G - 1)
                    project(GT - 1)

            def store(act, b, G):
                act.wait_ge(o2_done, b * GT + G + 1 + 2)
                act.dma_start(tv[:, b, G, :], o2[:, G % 2, :]).then_inc(stored[G % 2], 16)

            @block.scalar
            def _(act):
                act.sem_inc(exped, NS)
                for k in range(2):
                    act.sem_inc(stored[k], 16)
                act.wait_ge(fold_mm, 1)
                act.activation(w3s[:], pm[0:DV, 0, 0:P], ACT.Copy).then_inc(fold_done, 1)
                with act.Fori(0, B) as b:
                    for n, (G, kt) in enumerate(items):
                        c0 = max(0, kt - 4 * G) * P
                        act.wait_ge(sc_mm, b * NI + n + 1)
                        act.wait_ge(pv_mm, b * NI + n + 1 + NI - NE)
                        act.activation(e[:, n % NE, c0:], sc[:, n % NS, c0:], ACT.Exp, scale=1.0 / float(np.sqrt(P // 8))
                                       ).then_inc(exped, 1)
                        if kt == 3 and G > 1:
                            store(act, b, G - 2)
                    store(act, b, GT - 2)
                    store(act, b, GT - 1)
                for k in range(2):
                    act.wait_ge(stored[k], 16 * (B * GT // 2 + 1))

            @block.vector
            def _(v):
                v.sem_inc(at_done, 2)
                v.sem_inc(o1_done, 2)
                v.sem_inc(o2_done, 2)

                def normalise(b, G):
                    v.wait_ge(pv_mm, b * NI + first[G + 1] + NI)
                    v.tensor_scalar(den[:], po[32:48, G % 2, :], 1e-10, None, ALU.add).then_inc(den_done, 1)
                    v.wait_ge(den_done, b * GT + G + 1)
                    v.reciprocal(rec[:], den[:]).then_inc(rec_done, 1)
                    v.wait_ge(rec_done, b * GT + G + 1)
                    if G:
                        v.wait_ge(mh_mm, b * GT + G)
                    v.tensor_tensor(at[:], po[0:DV, G % 2, :], rec[:], ALU.mult).then_inc(at_done, 1)

                def residual(b, G):
                    v.wait_ge(mh_mm, b * GT + G + 1)
                    v.wait_ge(r_in[G % 2], b * (32 * GT // 2) + (G // 2) * 32 + 32)
                    v.wait_ge(o2_done, b * GT + G + 2)
                    v.scalar_tensor_tensor(o1[:], pm[:, G % 2, :], b3[:, 0:1], cr[:, G % 2, :], ALU.add, ALU.add
                                           ).then_inc(o1_done, 1)
                    v.wait_ge(o1_done, b * GT + G + 1 + 2)
                    v.wait_ge(stored[G % 2], b * (16 * GT // 2) + (G // 2) * 16 + 16)
                    v.tensor_tensor(o2[:, G % 2, :], o1[:], xr[:, G % 2, :], ALU.add).then_inc(o2_done, 1)

                with v.Fori(0, B) as b:
                    for G in range(GT):
                        normalise(b, G)
                        residual(b, G)


class Signal:

    def __init__(self, sem, per):
        self.sem, self.per = sem, per

    def credit(self, eng):
        eng.sem_inc(self.sem, self.per)

    def now(self, eng, it, k):
        eng.wait_ge(self.sem, it * self.per + (self.per + k))

    def before(self, eng, it, k):
        eng.wait_ge(self.sem, it * self.per + k)


def mamba_constants():
    r = np.arange(P)
    upto = (r[:, None] <= r[None, :]).astype(np.float32)
    after = (r[:, None] > r[None, :]).astype(np.float32)
    return {"c_tri": np.stack([upto, after, np.ones((P, P), np.float32)], 1),
            "c_flip": np.ascontiguousarray(np.eye(P, dtype=np.float32)[::-1]),
            "c_causal": np.tile(np.where(r[:, None] > r[None, :], MASK1, 0.0).astype(np.float32), (1, NH))}


def mamba(nc, sems, g, hn, outs):
    s = Scope(nc, sems, "mb")
    with s.stack:
        step = {n: s.sb(n, [P, 2, NCH, B * NH]) for n in ("dt", "da", "nacs", "eacs", "dtdec", "etot")}
        mamba_steps(nc, sems, g, hn, step)
        mamba_scan(nc, sems, g, hn, step, outs)


def mamba_steps(nc, sems, g, hn, st):
    s = Scope(nc, sems, "ms")
    W = NCH * B * NH
    with s.stack:
        wdt = s.sb("wdt", [P, 2 * NH])
        bias = s.sb("bias", [P, 2, NH])
        alog = s.sb("alog", [P, 2, NH])
        aneg = s.sb("aneg", [P, 2, NH])
        tri = s.sb("tri", [P, 3, P])
        flip = s.sb("flip", [P, P])
        h = s.sb("h", [P, 2, T])
        raw = s.sb("raw", [P, 2, NCH, B, NH])
        x = s.sb("x", [P, 2, W])
        ax = s.sb("ax", [P, 2, W])
        ex = s.sb("ex", [P, 2, W])
        lg = s.sb("lg", [P, 2, W])
        dec = s.sb("dec", [P, 2, W])
        pd = s.ps("pd", [P, 2, BANK])
        pf = s.ps("pf", [P, BANK])
        pc = s.ps("pc", [P, 5, BANK])
        w_in, dt_mm, gathered, flip_mm, step, exp_done, sum_mm, sum_exp, dec_done = (
            s.sem(n) for n in ("w_in", "dt_mm", "gathered", "flip_mm", "step", "exp_done", "sum_mm", "sum_exp",
                               "dec_done"))
        h_in = [s.sem(f"h_in{k}") for k in range(2)]
        hv = hn.rearrange("p (b n) -> p b n", b=B)
        with nc.Block() as block:

            @block.sync
            def _(sp):
                for dst, name in ((wdt, "Wdt"), (bias, "dt_bias"), (alog, "A_log"), (tri, "c_tri"), (flip, "c_flip")):
                    sp.dma_start(dst[:], g[name]).then_inc(w_in, 16)
                with sp.Fori(0, B // 2) as i:
                    for k in range(2):
                        sp.wait_ge(dt_mm, i * 2 + k + 1)
                        sp.dma_start(h[:, k], hv[:, i * 2 + k, :]).then_inc(h_in[k], 16)

            @block.tensor
            def _(pe):
                pe.sem_inc(dt_mm, 2)
                pe.wait_ge(w_in, 80)
                with pe.Fori(0, B // 2) as i:
                    for k in range(2):
                        pe.wait_ge(h_in[k], i * 16 + 16)
                        pe.wait_ge(gathered, i * 2 + k + 1)
                        for c in range(NCH):
                            mm = pe.matmul(pd[:, k, c * 2 * NH:(c + 1) * 2 * NH], h[:, k, c * P:(c + 1) * P], wdt[:],
                                           start=True, stop=True, skip_group_check=True)
                        mm.then_inc(dt_mm, 1)
                pe.wait_ge(gathered, B + 2)
                pe.matmul(pf[:], flip[:], raw[:, 1].rearrange("p c b h -> p (c b h)"), start=True, stop=True
                          ).then_inc(flip_mm, 1)
                pe.wait_ge(dec_done, 1)
                for d in range(2):
                    daf = st["da"][:, d].rearrange("p c n -> p (c n)")
                    for k in range(3):
                        n = 3 * d + k
                        if n == 5:
                            pe.wait_ge(sum_exp, 2)
                        pe.matmul(pc[:, n % 5, :], tri[:, k, :], daf, start=True, stop=True).then_inc(sum_mm, 1)

            @block.scalar
            def _(act):
                act.wait_ge(step, 3)
                act.activation(ex[:].rearrange("p d n -> p (d n)"), ax[:].rearrange("p d n -> p (d n)"), ACT.Exp,
                               scale=-1.0).then_inc(exp_done, 1)
                act.wait_ge(w_in, 80)
                act.activation(aneg[:].rearrange("p d n -> p (d n)"), alog[:].rearrange("p d n -> p (d n)"), ACT.Exp
                               ).then_inc(exp_done, 1)
                act.wait_ge(exp_done, 2)
                act.activation(lg[:].rearrange("p d n -> p (d n)"), ex[:].rearrange("p d n -> p (d n)"), ACT.Ln,
                               bias=1.0).then_inc(exp_done, 1)
                for d in range(2):
                    for k in range(3):
                        n = 3 * d + k
                        act.wait_ge(sum_mm, n + 1)
                        if k == 0:
                            act.activation(st["nacs"][:, d].rearrange("p c n -> p (c n)"), pc[:, n % 5, :], ACT.Copy,
                                           scale=-1.0).then_inc(sum_exp, 1)
                        dst = (st["eacs"][:, d].rearrange("p c n -> p (c n)"), dec[:, d, :],
                               st["etot"][:, d].rearrange("p c n -> p (c n)"))[k]
                        act.activation(dst, pc[:, n % 5, :], ACT.Exp).then_inc(sum_exp, 1)

            @block.vector
            def _(v):
                v.sem_inc(gathered, 2)
                with v.Fori(0, B // 2) as i:
                    for k in range(2):
                        v.wait_ge(dt_mm, i * 2 + k + 3)
                        v.tensor_copy(raw[:, :, :, i * 2 + k, :],
                                      pd[:, k, 0:2 * NH * NCH].rearrange("p (c d h) -> p d c h", d=2, h=NH)
                                      ).then_inc(gathered, 1)
                v.wait_ge(w_in, 80)
                v.wait_ge(gathered, B + 2)
                v.tensor_tensor(x[:, 0].rearrange("p (n h) -> p n h", h=NH),
                                raw[:, 0].rearrange("p c b h -> p (c b) h"),
                                bias[:, 0].unsqueeze(1).broadcast_to((P, NCH * B, NH)), ALU.add).then_inc(step, 1)
                v.wait_ge(flip_mm, 1)
                v.tensor_tensor(x[:, 1].rearrange("p (c b h) -> p c b h", b=B, h=NH),
                                pf[:].rearrange("p (c b h) -> p c b h", b=B, h=NH)[:, ::-1],
                                bias[:, 1].unsqueeze(1).unsqueeze(1).broadcast_to((P, NCH, B, NH)), ALU.add
                                ).then_inc(step, 1)
                v.wait_ge(step, 2)
                v.scalar_tensor_tensor(ax[:], x[:], -1.0, x[:], ALU.mult, ALU.max).then_inc(step, 1)
                v.wait_ge(exp_done, 3)
                dtf = st["dt"][:].rearrange("p d c n -> p d (c n)")
                v.scalar_tensor_tensor(dtf, x[:], 0.0, lg[:], ALU.max, ALU.add).then_inc(step, 1)
                v.wait_ge(step, 4)
                for d in range(2):
                    mm = v.scalar_tensor_tensor(st["da"][:, d].rearrange("p c (b h) -> p (c b) h", h=NH),
                                                st["dt"][:, d].rearrange("p c (b h) -> p (c b) h", h=NH), -1.0,
                                                aneg[:, d].unsqueeze(1).broadcast_to((P, NCH * B, NH)),
                                                ALU.mult, ALU.mult)
                    mm.then_inc(step, 1)
                v.wait_ge(step, 6)
                v.sem_inc(dec_done, 1)
                v.wait_ge(sum_exp, 8)
                v.tensor_tensor(st["dtdec"][:].rearrange("p d c n -> p d (c n)"), dtf, dec[:], ALU.mult
                                ).then_inc(step, 1)


def mamba_scan(nc, sems, g, hn, st, outs):
    s = Scope(nc, sems, "mm")
    XB = 3
    H2 = B // 2
    PER = dict(xin=16, xc=1, dac=1, halo=1, proj=3, evac=6, zmm=2, thz=2, zs=2, lmm=4, lexp=16, taps=9, th=3, silu=4,
               gmm=1, w=4, xtmm=2, btmm=1, bt=1, xd=4, yomm=2, ydmm=2, y=2, yadd=2, gate=2, stmm=2, stmp=1,
               st=2, sq=4, rs1=1, rs=1, yn=4, ytmm=2, yta=1, ytv=1, omm=1, ob=1, stored=16)
    FROM = dict(scalar="evac thz lexp th bt sq yn yta ob stored", vector="taps zs silu w xd y yadd st ytv",
                tensor="proj zmm lmm gmm xtmm btmm yomm ydmm stmm ytmm omm", gpsimd="xc dac halo gate stmp rs1 rs",
                sync="xin")
    with s.stack:
        identb = s.sb("identb", [P, P], BF16)
        ident = s.sb("ident", [P, P])
        cm = s.sb("cm", [P, NH * P])
        cmb = s.sb("cmb", [P, NH * P], BF16)
        tri = s.sb("tri", [P, P])
        nhalf = s.sb("nhalf", [P, B])
        D = []
        for d in range(2):
            t = {n: s.sb(f"{n}{d}", shape) for n, shape in (
                ("wi", [P, 2 * DI + 2 * DS]), ("cw", [P, XB, TAPS]), ("cb", [P, XB]), ("dcol", [P, 2]),
                ("nw", [P, 2]), ("dg", [P, 2, P]), ("wo", [P, 2, P]),
                ("xin", [P, B, CH]), ("xc", [P, B, CH]), ("dac", [P, B * NH]), ("raw", [P, XB, B, CH + TAPS - 1]),
                ("acc", [P, XB, B, CH]), ("th", [P, XB, B, CH]), ("xs", [P, 2, B, CH]), ("bs", [DS, B, CH]),
                ("cs", [DS, B, CH]), ("L", [P, B, NH, CH]), ("xdt", [P, B, NH, HD]), ("xdd", [P, B, NH, HD]),
                ("bt", [P, B, DS]), ("state", [DS, B, DI]), ("stmp", [DS, B, DI]), ("zs", [P, B, DI]),
                ("y", [P, B, DI]), ("yn", [P, B, DI]), ("yt", [P, 2, B, CH]), ("ob", [P, B, CH]),
                ("ssq", [P, B]), ("rs", [P, B]))}
            for n in "ABCD":
                t[n] = s.ps(f"{n}{d}", [P, BANK])
            t["sig"] = {n: Signal(s.sem(f"{n}{d}"), per) for n, per in PER.items()}
            D.append(t)
        w_in, ready, passed_sp, passed_pool = (s.sem(n) for n in ("w_in", "ready", "passed_sp", "passed_pool"))
        hv = hn.rearrange("p (b c n) -> p b c n", b=B, n=CH)
        ov = [o.rearrange("p (b c n) -> p b c n", b=B, n=CH) for o in outs]
        DMAS = 3 + 2 * 6
        READY = 3 + 2 * 9

        def credits(eng, name):
            for t in D:
                for n in FROM[name].split():
                    t["sig"][n].credit(eng)

        def chunk(it, d):
            return it if d == 0 else (NCH - 1) - it

        with nc.Block() as block:

            @block.sync
            def _(sp):
                sp.dma_start(ident[:], g["c_ident"]).then_inc(w_in, 16)
                sp.dma_start(cm[:], g["c_causal"]).then_inc(w_in, 16)
                sp.dma_start(tri[:], g["c_tri"][:, 0, :]).then_inc(w_in, 16)
                for d, t in enumerate(D):
                    for n, name in (("wi", "in_proj"), ("cw", "conv_w"), ("cb", "conv_b"), ("dcol", "D"), ("nw", "norm_w"),
                                    ("wo", "out_proj")):
                        sp.dma_start(t[n][:], g[f"{name}{d}"]).then_inc(w_in, 16)
                credits(sp, "sync")
                with sp.Fori(0, NCH) as it:
                    for d, t in enumerate(D):
                        t["sig"]["xc"].before(sp, it, 1)
                        hold(sp, passed_sp)
                        sp.dma_start(t["xin"][:], hv[:, :, chunk(it, d), :]).then_inc(t["sig"]["xin"].sem, 16)

            @block.gpsimd
            def _(pool):
                pool.wait_ge(w_in, 16 * DMAS)
                pool.tensor_copy(identb[:], ident[:]).then_inc(ready, 1)
                pool.tensor_copy(cmb[:], cm[:]).then_inc(ready, 1)
                pool.memset(nhalf[:], -0.5).then_inc(ready, 1)
                for t in D:
                    pool.memset(t["raw"][:], 0.0).then_inc(ready, 1)
                    pool.memset(t["state"][:], 0.0).then_inc(ready, 1)
                    for k in range(2):
                        pool.tensor_scalar(t["dg"][:, k, :], ident[:], t["dcol"][:, k:k + 1], None, ALU.mult
                                           ).then_inc(ready, 1)
                        pool.tensor_scalar(t["wo"][:, k, :], t["wo"][:, k, :], t["nw"][:, k:k + 1], None, ALU.mult
                                           ).then_inc(ready, 1)
                    pool.tensor_scalar(t["wi"][:, 0:DI], t["wi"][:, 0:DI], 0.5, None, ALU.mult).then_inc(ready, 1)
                    pool.tensor_scalar(t["cw"][:], t["cw"][:], 0.5, None, ALU.mult).then_inc(ready, 1)
                    pool.tensor_scalar(t["cb"][:], t["cb"][:], 0.5, None, ALU.mult).then_inc(ready, 1)
                credits(pool, "gpsimd")
                pool.wait_ge(ready, READY)
                with pool.Fori(0, NCH) as it:
                    for d, t in enumerate(D):
                        S = t["sig"]
                        S["xin"].now(pool, it, 16)
                        S["zmm"].before(pool, it, 2)
                        hold(pool, passed_pool)
                        pool.tensor_copy(t["xc"][:], t["xin"][:] if d == 0 else t["xin"][:, :, ::-1]
                                         ).then_inc(S["xc"].sem, 1)
                        S["lmm"].before(pool, it, 4)
                        hold(pool, passed_pool)
                        pool.tensor_copy(t["dac"][:], st["da"][:, d, it, :]).then_inc(S["dac"].sem, 1)
                        S["taps"].before(pool, it, 9)
                        hold(pool, passed_pool)
                        pool.tensor_copy(t["raw"][:, :, :, 0:TAPS - 1].rearrange("p x b n -> p (x b) n"),
                                         t["raw"][:, :, :, CH:CH + TAPS - 1].rearrange("p x b n -> p (x b) n")
                                         ).then_inc(S["halo"].sem, 1)
                    for d, t in enumerate(D):
                        S = t["sig"]
                        S["st"].before(pool, it, 2)
                        pool.tensor_tensor(t["stmp"][:].rearrange("p b (h e) -> p (b h) e", h=NH),
                                           t["state"][:].rearrange("p b (h e) -> p (b h) e", h=NH),
                                           st["etot"][0:DS, d, it, :].unsqueeze(2).broadcast_to((DS, B * NH, HD)),
                                           ALU.mult).then_inc(S["stmp"].sem, 1)
                    for d, t in enumerate(D):
                        S = t["sig"]
                        for k in range(2):
                            S["yadd"].now(pool, it, k + 1)
                            S["zs"].now(pool, it, k + 1)
                            sl = slice(k * H2, (k + 1) * H2)
                            pool.tensor_tensor(t["y"][:, sl], t["y"][:, sl], t["zs"][:, sl], ALU.mult
                                               ).then_inc(S["gate"].sem, 1)
                    for d, t in enumerate(D):
                        S = t["sig"]
                        S["sq"].now(pool, it, 4)
                        hold(pool, passed_pool)
                        pool.tensor_scalar(t["rs"][:], t["ssq"][:], 1.0 / DI, 1e-5, ALU.mult, ALU.add
                                           ).then_inc(S["rs1"].sem, 1)
                        S["rs1"].now(pool, it, 1)
                        pool.tensor_tensor(t["rs"][:], t["rs"][:], nhalf[:], ALU.pow).then_inc(S["rs"].sem, 1)

            @block.tensor
            def _(pe):
                credits(pe, "tensor")
                pe.wait_ge(w_in, 16 * DMAS)
                pe.wait_ge(ready, READY)

                def flat(ap):
                    return ap.rearrange("p b n -> p (b n)")

                def project(it, d, t, S):
                    S["xc"].now(pe, it, 1)
                    for k, (bank, free, cnt) in enumerate((("A", "ob", 1), ("B", "st", 2), ("C", "yta", 1))):
                        S[free].before(pe, it, cnt)
                        pe.matmul(t[bank][:], t["wi"][:, DI + k * P:DI + (k + 1) * P], flat(t["xc"][:]), start=True,
                                  stop=True).then_inc(S["proj"].sem, 1)

                def gate(it, d, t, S, k):
                    if k == 0:
                        S["ytv"].before(pe, it, 1)
                    else:
                        S["zs"].now(pe, it, 1)
                    for j in range(2):
                        mm = pe.matmul(t["D"][:, j * DI:(j + 1) * DI], t["xc"][:, 2 * k + j, :], t["wi"][:, 0:DI],
                                       start=True, stop=True, skip_group_check=True)
                    mm.then_inc(S["zmm"].sem, 1)

                def decay(it, d, t, S, b):
                    if b == 0:
                        S["dac"].now(pe, it, 1)
                    if b < 2:
                        S["evac"].now(pe, it, 2 * (b + 1))
                    else:
                        S["lexp"].now(pe, it, NH * (b - 1))
                    bank = t["AB"[b % 2]]
                    pe.matmul(bank[:], identb[:], cmb[:], start=True, stop=False, skip_group_check=True)
                    for h in range(NH):
                        n = b * NH + h
                        mm = pe.matmul(bank[:, h * P:(h + 1) * P], t["dac"][:, n:n + 1].broadcast_to((P, P)), tri[:],
                                       start=False, stop=(h == NH - 1), skip_group_check=True)
                    mm.then_inc(S["lmm"].sem, 1)

                def turn(it, d, t, S):
                    S["silu"].now(pe, it, 4)
                    S["evac"].now(pe, it, 6)
                    S["zs"].now(pe, it, 2)
                    for b in range(B):
                        mm = pe.matmul(t["C"][:, b * P:(b + 1) * P], t["bs"][:, b, :], t["cs"][:, b, :], start=True,
                                       stop=True, skip_group_check=True)
                    mm.then_inc(S["gmm"].sem, 1)
                    for b in range(B):
                        mm = pe.transpose(t["D"][:, b * DS:(b + 1) * DS], t["bs"][:, b, :], ident[0:DS, 0:DS])
                    mm.then_inc(S["btmm"].sem, 1)
                    for k in range(2):
                        S["lexp"].now(pe, it, 12 + 4 * k)
                        for j in range(2):
                            for x in range(2):
                                mm = pe.transpose(t["AB"[k]][:, (2 * j + x) * P:(2 * j + x + 1) * P],
                                                  t["xs"][:, x, 2 * k + j, :], ident[:])
                        mm.then_inc(S["xtmm"].sem, 1)

                def outputs(it, d, t, S):
                    S["st"].before(pe, it, 2)
                    for k in range(2):
                        S["xd"].now(pe, it, 2 * k + 2)
                        for j in range(2):
                            mm = pe.matmul(t["AB"[k]][:, j * DI:(j + 1) * DI], t["cs"][:, 2 * k + j, :],
                                           t["state"][:, 2 * k + j, :], start=True, stop=True, skip_group_check=True)
                        mm.then_inc(S["yomm"].sem, 1)
                    S["w"].now(pe, it, 4)
                    for k in range(2):
                        if k == 1:
                            S["bt"].now(pe, it, 1)
                        bank = t["CD"[k]]
                        for j in range(2):
                            b = 2 * k + j
                            for x in range(2):
                                o = j * DI + x * P
                                pe.matmul(bank[:, o:o + P], t["xs"][:, x, b, :], t["dg"][:, x, :], start=(x == 0),
                                          stop=False, skip_group_check=True)
                            for h in range(NH):
                                o = j * DI + h * HD
                                mm = pe.matmul(bank[:, o:o + HD], t["L"][:, b, h, :], t["xdt"][:, b, h, :],
                                               start=False, stop=(h == NH - 1), skip_group_check=True)
                        mm.then_inc(S["ydmm"].sem, 1)

                def states(it, d, t, S):
                    for k in range(2):
                        S["y"].now(pe, it, k + 1)
                        for j in range(2):
                            b = 2 * k + j
                            mm = pe.matmul(t["AB"[k]][0:DS, j * DI:(j + 1) * DI], t["bt"][:, b, :],
                                           t["xdd"][:, b].rearrange("p h e -> p (h e)"), start=True, stop=True,
                                           skip_group_check=True)
                        mm.then_inc(S["stmm"].sem, 1)

                def turn_back(it, d, t, S):
                    S["yn"].now(pe, it, 4)
                    for x in range(2):
                        S["yadd"].now(pe, it, x + 1)
                        for b in range(B):
                            mm = pe.transpose(t["CD"[x]][:, b * P:(b + 1) * P], t["yn"][:, b, x * P:(x + 1) * P],
                                              ident[:])
                        mm.then_inc(S["ytmm"].sem, 1)

                def project_out(it, d, t, S):
                    S["st"].now(pe, it, 1)
                    S["yta"].now(pe, it, 1)
                    pe.matmul(t["A"][:], t["wo"][:, 0, :], flat(t["yt"][:, 0]), start=True, stop=False)
                    S["ytv"].now(pe, it, 1)
                    pe.matmul(t["A"][:], t["wo"][:, 1, :], flat(t["yt"][:, 1]), start=False, stop=True
                              ).then_inc(S["omm"].sem, 1)

                with pe.Fori(0, NCH) as it:

                    def both(stage, *more):
                        for d, t in enumerate(D):
                            stage(it, d, t, t["sig"], *more)

                    both(project)
                    both(gate, 0)
                    both(decay, 0)
                    both(decay, 1)
                    both(gate, 1)
                    both(decay, 2)
                    both(decay, 3)
                    both(turn)
                    both(outputs)
                    both(states)
                    both(turn_back)
                    both(project_out)

            @block.scalar
            def _(act):
                credits(act, "scalar")
                act.wait_ge(w_in, 16 * DMAS)
                act.wait_ge(ready, READY)

                def flat(ap):
                    return ap.rearrange("p b n -> p (b n)")

                def raws(it, d, t, S):
                    S["halo"].now(act, it, 1)
                    S["silu"].before(act, it, 4)
                    for k in range(XB):
                        S["proj"].now(act, it, k + 1)
                        pj = t["ABC"[k]][:].rearrange("p (b n) -> p b n", b=B)
                        act.activation(t["raw"][:, k, :, TAPS - 1:], pj, ACT.Copy).then_inc(S["evac"].sem, 1)
                        act.activation(t["acc"][:, k], pj, ACT.Identity, bias=t["cb"][:, k:k + 1],
                                       scale=t["cw"][:, k, TAPS - 1:TAPS]).then_inc(S["evac"].sem, 1)

                def z_tanh(it, d, t, S, k):
                    S["zmm"].now(act, it, k + 1)
                    S["gate"].before(act, it, 2)
                    act.activation(flat(t["zs"][:, k * H2:(k + 1) * H2]), t["D"][:], ACT.Tanh).then_inc(S["thz"].sem, 1)

                def decays(it, d, t, S, b):
                    S["lmm"].now(act, it, b + 1)
                    S["ydmm"].before(act, it, 2)
                    for h in range(NH):
                        n = b * NH + h
                        act.activation(t["L"][:, b, h, :], t["AB"[b % 2]][:, h * P:(h + 1) * P], ACT.Exp,
                                       bias=st["nacs"][:, d, it, n:n + 1]).then_inc(S["lexp"].sem, 1)

                def tanhs(it, d, t, S):
                    for k in range(XB):
                        S["taps"].now(act, it, 6 + k + 1)
                        act.activation(t["th"][:, k], t["acc"][:, k], ACT.Tanh).then_inc(S["th"].sem, 1)

                def b_tokens(it, d, t, S):
                    S["btmm"].now(act, it, 1)
                    S["stmm"].before(act, it, 2)
                    act.activation(flat(t["bt"][:]), t["D"][:, 0:B * DS], ACT.Copy).then_inc(S["bt"].sem, 1)

                def squares(it, d, t, S):
                    S["ytmm"].before(act, it, 2)
                    for b in range(B):
                        S["gate"].now(act, it, b // 2 + 1)
                        act.activation(t["yn"][:, b, :], t["y"][:, b, :], ACT.Square, accum_out=t["ssq"][:, b:b + 1]
                                       ).then_inc(S["sq"].sem, 1)

                def norms(it, d, t, S):
                    S["rs"].now(act, it, 1)
                    for b in range(B):
                        act.activation(t["yn"][:, b, :], t["y"][:, b, :], ACT.Copy, scale=t["rs"][:, b:b + 1]
                                       ).then_inc(S["yn"].sem, 1)

                def turned(it, d, t, S):
                    S["ytmm"].now(act, it, 1)
                    S["omm"].before(act, it, 1)
                    act.activation(flat(t["yt"][:, 0]), t["C"][:], ACT.Copy).then_inc(S["yta"].sem, 1)

                def result(it, d, t, S):
                    S["omm"].now(act, it, 1)
                    S["stored"].before(act, it, 16)
                    dst = t["ob"][:] if d == 0 else t["ob"][:, :, ::-1]
                    act.activation(dst, t["A"][:].rearrange("p (b n) -> p b n", b=B), ACT.Copy).then_inc(S["ob"].sem, 1)
                    S["ob"].now(act, it, 1)
                    act.dma_start(ov[d][:, :, chunk(it, d), :], t["ob"][:]).then_inc(S["stored"].sem, 16)

                with act.Fori(0, NCH) as it:

                    def both(stage, *more):
                        for d, t in enumerate(D):
                            stage(it, d, t, t["sig"], *more)

                    both(raws)
                    both(z_tanh, 0)
                    both(decays, 0)
                    both(decays, 1)
                    both(z_tanh, 1)
                    both(tanhs)
                    both(decays, 2)
                    both(decays, 3)
                    both(b_tokens)
                    both(squares)
                    both(norms)
                    both(turned)
                    both(result)
                for t in D:
                    act.wait_ge(t["sig"]["stored"].sem, 16 * (NCH + 1))

            @block.vector
            def _(v):
                credits(v, "vector")
                v.wait_ge(w_in, 16 * DMAS)
                v.wait_ge(ready, READY)

                def taps(it, d, t, S, i):
                    for k in range(XB):
                        S["evac"].now(v, it, 2 * k + 2)
                        if i:
                            S["taps"].now(v, it, (i - 1) * XB + k + 1)
                        v.scalar_tensor_tensor(t["acc"][:, k], t["raw"][:, k, :, i:i + CH], t["cw"][:, k, i:i + 1],
                                               t["acc"][:, k], ALU.mult, ALU.add).then_inc(S["taps"].sem, 1)

                def z_silu(it, d, t, S, k):
                    S["thz"].now(v, it, k + 1)
                    zf = t["zs"][:, k * H2:(k + 1) * H2].rearrange("p b n -> p (b n)")
                    v.scalar_tensor_tensor(zf, zf, 1.0, t["D"][:], ALU.add, ALU.mult).then_inc(S["zs"].sem, 1)

                def silus(it, d, t, S):
                    S["ydmm"].before(v, it, 2)
                    S["stmm"].before(v, it, 2)
                    for dst, k, p0, p1 in ((t["xs"][:, 0], 0, 0, P), (t["xs"][:, 1], 1, 0, P), (t["bs"][:], 2, 0, DS),
                                           (t["cs"][:], 2, DS, 2 * DS)):
                        S["th"].now(v, it, k + 1)
                        v.scalar_tensor_tensor(dst, t["th"][p0:p1, k], 1.0, t["acc"][p0:p1, k], ALU.add, ALU.mult
                                               ).then_inc(S["silu"].sem, 1)

                def weights(it, d, t, S):
                    S["gmm"].now(v, it, 1)
                    for b in range(B):
                        S["lexp"].now(v, it, NH * (b + 1))
                        v.tensor_tensor(t["L"][:, b], t["L"][:, b],
                                        t["C"][:, b * P:(b + 1) * P].unsqueeze(1).broadcast_to((P, NH, P)), ALU.mult
                                        ).then_inc(S["w"].sem, 1)

                def spread(ap, it, d, k):
                    return ap[:, d, it, k * H2 * NH:(k + 1) * H2 * NH].unsqueeze(2).broadcast_to((P, H2 * NH, HD))

                def heads(ap):
                    return ap.rearrange("p (n e) -> p n e", e=HD)

                def steps(it, d, t, S):
                    for k in range(2):
                        S["xtmm"].now(v, it, k + 1)
                        for n, f in (("xdt", "dt"), ("xdd", "dtdec")):
                            v.tensor_tensor(t[n][:, k * H2:(k + 1) * H2].rearrange("p b h e -> p (b h) e"),
                                            heads(t["AB"[k]][:]), spread(st[f], it, d, k), ALU.mult
                                            ).then_inc(S["xd"].sem, 1)

                def ys(it, d, t, S):
                    S["yn"].before(v, it, 4)
                    for k in range(2):
                        S["yomm"].now(v, it, k + 1)
                        v.tensor_tensor(t["y"][:, k * H2:(k + 1) * H2].rearrange("p b (h e) -> p (b h) e", e=HD),
                                        heads(t["AB"[k]][:]), spread(st["eacs"], it, d, k), ALU.mult
                                        ).then_inc(S["y"].sem, 1)
                    for k in range(2):
                        S["ydmm"].now(v, it, k + 1)
                        S["y"].now(v, it, k + 1)
                        yf = t["y"][:, k * H2:(k + 1) * H2].rearrange("p b n -> p (b n)")
                        v.tensor_tensor(yf, yf, t["CD"[k]][:], ALU.add).then_inc(S["yadd"].sem, 1)

                def states(it, d, t, S):
                    S["stmp"].now(v, it, 1)
                    S["yomm"].now(v, it, 2)
                    for k in range(2):
                        S["stmm"].now(v, it, k + 1)
                        sl = slice(k * H2, (k + 1) * H2)
                        v.tensor_tensor(t["state"][:, sl].rearrange("p b n -> p (b n)"),
                                        t["stmp"][:, sl].rearrange("p b n -> p (b n)"), t["AB"[k]][0:DS, :], ALU.add
                                        ).then_inc(S["st"].sem, 1)

                def turned(it, d, t, S):
                    S["ytmm"].now(v, it, 2)
                    S["omm"].before(v, it, 1)
                    v.tensor_copy(t["yt"][:, 1].rearrange("p b n -> p (b n)"), t["D"][:]).then_inc(S["ytv"].sem, 1)

                with v.Fori(0, NCH) as it:

                    def both(stage, *more):
                        for d, t in enumerate(D):
                            stage(it, d, t, t["sig"], *more)

                    both(taps, 0)
                    both(z_silu, 0)
                    both(taps, 1)
                    both(taps, 2)
                    both(z_silu, 1)
                    both(silus)
                    both(steps)
                    both(weights)
                    both(ys)
                    both(states)
                    both(turned)


def stu_constants():
    a = np.arange(NB)
    ang = 2 * np.pi * np.outer(a, np.arange(NB)) / NF
    re, im = np.cos(ang), -np.sin(ang)
    alt = (-1.0) ** a
    fwd = np.stack([re, im], 1)
    fwd[:, 1, 0] = alt
    dft_u = np.zeros((2, B, NB, 2, 2, NB))
    for b in range(B):
        dft_u[b // 2, b, :, :, b % 2, :] = fwd
    blk = np.zeros((NB, 2, NB, 2))
    blk[:, 0, :, 0], blk[:, 1, :, 0], blk[:, 0, :, 1], blk[:, 1, :, 1] = re, im, -im, re
    blk[:, 1, 0, 0] = blk[:, 0, 0, 1] = 0
    blk[:, 1, 0, 1] = alt
    inv = np.stack([2 * re, 2 * im], 2).transpose(2, 1, 0) / NF
    inv[0, 0], inv[1, 0] = 1 / NF, alt / NF
    f = lambda m, *shape: np.ascontiguousarray(m.reshape(shape), np.float32)
    return {"c_dft_u": f(dft_u, 2, P, P), "c_dft_phi": f(blk, NB, P), "c_idft": f(inv, 2 * NB, NB)}


def spectral(nc, sems, g, hn, t1, out):
    s0 = Scope(nc, sems, "stu")
    u_hat = nc.dram_tensor("u_hat", (2, NB, 2, B, 2, P, HALF), F32, kind="Internal").ap()
    g_hat = nc.dram_tensor("g_hat", (2, NB, 2, K, 2, BL, 2), F32, kind="Internal").ap()
    y_hat = nc.dram_tensor("y_hat", (2, B, NB, HALF, 2, P), F32, kind="Internal").ap()
    with s0.stack:
        me = s0.sb("me", [P, 2, 2, K, P], F32R)
        mu = s0.sb("mu", [P, 3, P])
        seg = s0.sb("seg", [P, 4])
        stu_matrices(nc, sems, g, me, mu, seg)
        stu_transforms(nc, sems, g, hn, u_hat, g_hat)
        stu_convolve(nc, sems, me, u_hat, g_hat, y_hat)
        stu_finish(nc, sems, g, mu, seg, y_hat, hn, t1, out)


def stu_matrices(nc, sems, g, me, mu, seg):
    s = Scope(nc, sems, "mat")
    with s.stack:
        lw = s.sb("lw", [P, 4])
        gum = s.sb("gum", [P, 4])
        sig = s.sb("sig", [P, K])
        quarter = s.sb("quarter", [P, K])
        sk = s.sb("sk", [P, K])
        z = s.sb("z", [P, 4])
        e = s.sb("e", [P, 4])
        soft = s.sb("soft", [P, 4])
        eq = s.sb("eq", [P, 4])
        hard = s.sb("hard", [P, 4])
        left = s.sb("left", [P, 4])
        w = s.sb("w", [P, 4])
        one = s.sb("one", [P, 4])
        raw = s.sb("raw", [P, 2, 4, K * P])
        rmu = s.sb("rmu", [P, 4, 3 * P])
        acc = s.sb("acc", [P, 2, K * P])
        small_in, big_in, mu_in, z_done, e_done, step, pow_done = (
            s.sem(n) for n in ("small_in", "big_in", "mu_in", "z_done", "e_done", "step", "pow_done"))
        with nc.Block() as block:

            @block.sync
            def _(sp):
                sp.dma_start(lw[:], g["log_weights"]).then_inc(small_in, 16)
                sp.dma_start(gum[:], g["gumbel"]).then_inc(small_in, 16)
                sp.dma_start(sig[:], g["sigma"]).then_inc(small_in, 16)
                for i in range(4):
                    for m, name in enumerate(("M_phi_plus", "M_phi_minus")):
                        sp.dma_start(raw[:, m, i, :].rearrange("d (k e) -> d k e", e=P),
                                     g[name][i].rearrange("k d e -> d k e")).then_inc(big_in, 16)
                for i in range(4):
                    sp.dma_start(rmu[:, i, :].rearrange("d (k e) -> d k e", e=P),
                                 g["M_u"][i].rearrange("k d e -> d k e")).then_inc(mu_in, 16)

            @block.gpsimd
            def _(pool):
                pool.memset(quarter[:], 0.25).then_inc(pow_done, 1)
                pool.wait_ge(pow_done, 1)
                pool.wait_ge(small_in, 48)
                pool.tensor_tensor(sk[:], sig[:], quarter[:], ALU.pow).then_inc(pow_done, 1)

            @block.scalar
            def _(act):
                act.wait_ge(z_done, 1)
                act.activation(e[:], z[:], ACT.Exp).then_inc(e_done, 1)

            @block.vector
            def _(v):
                done = [0]

                def then(ins):
                    done[0] += 1
                    ins.then_inc(step, 1)
                    v.wait_ge(step, done[0])

                then(v.memset(one[:], 1.0))
                v.wait_ge(small_in, 48)
                then(v.tensor_tensor(z[:], lw[:], gum[:], ALU.add))
                then(v.tensor_reduce(w[:, 0:1], z[:], AX.X, ALU.max))
                v.tensor_scalar(z[:], z[:], w[:, 0:1], None, ALU.subtract).then_inc(z_done, 1)
                v.wait_ge(e_done, 1)
                then(v.tensor_reduce(w[:, 0:1], e[:], AX.X, ALU.add))
                then(v.reciprocal(w[:, 1:2], w[:, 0:1]))
                then(v.tensor_scalar(soft[:], e[:], w[:, 1:2], None, ALU.mult))
                then(v.tensor_reduce(w[:, 0:1], soft[:], AX.X, ALU.max))
                then(v.tensor_scalar(eq[:], soft[:], w[:, 0:1], None, ALU.is_ge))
                then(v.tensor_copy(hard[:, 0:1], eq[:, 0:1]))
                then(v.tensor_tensor(left[:, 0:1], one[:, 0:1], eq[:, 0:1], ALU.subtract))
                for i in range(1, 4):
                    then(v.tensor_tensor(hard[:, i:i + 1], eq[:, i:i + 1], left[:, i - 1:i], ALU.mult))
                    then(v.tensor_tensor(left[:, i:i + 1], left[:, i - 1:i], hard[:, i:i + 1], ALU.subtract))
                then(v.tensor_tensor(w[:], hard[:], soft[:], ALU.subtract))
                then(v.tensor_tensor(w[:], w[:], soft[:], ALU.add))
                then(v.tensor_copy(seg[:, 3:4], hard[:, 0:1]))
                for j in (2, 1, 0):
                    then(v.tensor_tensor(seg[:, j:j + 1], seg[:, j + 1:j + 2], hard[:, 3 - j:4 - j], ALU.add))
                v.wait_ge(mu_in, 64)
                mu_f = mu[:].rearrange("d k e -> d (k e)")
                then(v.tensor_scalar(mu_f, rmu[:, 0, :], w[:, 0:1], None, ALU.mult))
                for i in range(1, 4):
                    then(v.scalar_tensor_tensor(mu_f, rmu[:, i, :], w[:, i:i + 1], mu_f, ALU.mult, ALU.add))
                v.wait_ge(big_in, 128)
                for m in range(2):
                    then(v.tensor_scalar(acc[:, m, :], raw[:, m, 0, :], w[:, 0:1], None, ALU.mult))
                    for i in range(1, 4):
                        then(v.scalar_tensor_tensor(acc[:, m, :], raw[:, m, i, :], w[:, i:i + 1], acc[:, m, :],
                                                    ALU.mult, ALU.add))
                v.wait_ge(pow_done, 2)
                for m, op in enumerate((ALU.add, ALU.subtract)):
                    then(v.tensor_tensor(raw[:, m, 0, :], acc[:, 0, :], acc[:, 1, :], op))
                    full = raw[:, m, 1, :].rearrange("d (k e) -> d k e", e=P)
                    then(v.tensor_tensor(full, raw[:, m, 0, :].rearrange("d (k e) -> d k e", e=P),
                                         sk[:].unsqueeze(2).broadcast_to((P, K, P)), ALU.mult))
                    then(v.tensor_copy(me[:, 0, m], full))
                    then(low_part(v, me[:, 1, m], full, me[:, 0, m]))


def stu_transforms(nc, sems, g, hn, u_hat, g_hat):
    DC = 16
    STEPS = P // DC
    s = Scope(nc, sems, "dft")
    with s.stack:
        wp = s.sb("wp", [NB, P])
        wu = s.sb("wu", [P, 2, P])
        ph = s.sb("ph", [NB, K, 2 * BL])
        gs = s.sb("gs", [2 * NB, 2, K, 2, BL, 2], F32R)
        u = s.sb("u", [P, 2, DC, BL])
        uo = s.sb("uo", [P, 2, 2, 2, 2, DC, HALF], F32R)
        pp = s.ps("pp", [P, 2, BANK])
        pu = s.ps("pu", [P, 4, BANK])
        w_in, ph_in, ph_mm, ph_high, ph_out, g_stored, u_mm, u_high, u_low, u_used = (
            s.sem(n) for n in ("w_in", "ph_in", "ph_mm", "ph_high", "ph_out", "g_stored", "u_mm", "u_high", "u_low",
                               "u_used"))
        u_in = [s.sem(f"u_in{k}") for k in range(2)]
        u_stored = [s.sem(f"u_stored{k}") for k in range(2)]
        NP = K * 2 * BL // BANK
        MM = DC * BL // BANK
        hv = hn.rearrange("d (ba n) -> ba d n", n=BL)
        with nc.Block() as block:

            @block.sync
            def _(sp):
                sp.dma_start(wp[:], g["c_dft_phi"]).then_inc(w_in, 16)
                sp.dma_start(wu[:], g["c_dft_u"].rearrange("r p m -> p r m")).then_inc(w_in, 16)
                for half in range(2):
                    sp.dma_start(ph[:, :, half * BL:(half + 1) * BL],
                                 g["phi"][:, half * BL:half * BL + T].rearrange("k (a m) -> a k m", m=BL)
                                 ).then_inc(ph_in, 16)
                for c in range(STEPS):
                    if c >= 2:
                        sp.wait_ge(u_used, c - 1)
                    sp.dma_start(u[:, c % 2], hv[:, c * DC:(c + 1) * DC, :]).then_inc(u_in[c % 2], 16)
                sp.wait_ge(ph_out, 4 * NP)
                for part in range(2):
                    sp.dma_start(g_hat[part].rearrange("w x k r m y -> (w x) (k r m y)"),
                                 gs[:, part].rearrange("p k r m y -> p (k r m y)").bitcast(F32)).then_inc(g_stored, 16)
                sp.wait_ge(g_stored, 32)
                for k in range(2):
                    sp.wait_ge(u_stored[k], 256 * (STEPS // 2))

            @block.tensor
            def _(pe):
                pe.wait_ge(w_in, 32)
                pe.wait_ge(ph_in, 32)
                phf = ph[:].rearrange("a k m -> a (k m)")
                for n in range(NP):
                    for y in range(2):
                        if n >= 1:
                            pe.wait_ge(ph_out, 2 * (2 * n + y - 1))
                        pe.matmul(pp[0:2 * NB, y, :], wp[:, y * 2 * NB:(y + 1) * 2 * NB],
                                  phf[:, n * BANK:(n + 1) * BANK], start=True, stop=True).then_inc(ph_mm, 1)
                for c in range(STEPS):
                    pe.wait_ge(u_in[c % 2], 16 * (c // 2 + 1))
                    uf = u[:, c % 2].rearrange("p d n -> p (d n)")
                    for n in range(2 * MM):
                        tot = c * 2 * MM + n
                        if tot >= 4:
                            pe.wait_ge(u_low, tot - 3)
                        mm = pe.matmul(pu[:, tot % 4, :], wu[:, n // MM, :], uf[:, n % MM * BANK:(n % MM + 1) * BANK],
                                       start=True, stop=True)
                        mm.then_inc(u_mm, 1)
                    mm = None
                    pe.wait_ge(u_mm, (c + 1) * 2 * MM)
                    pe.sem_inc(u_used, 1)

            def tokens(eng, step):
                for c in range(STEPS):
                    if c >= 2:
                        eng.wait_ge(u_stored[c % 2], 256 * (c // 2))
                    for n in range(2 * MM):
                        d0 = n % MM * (BANK // BL)
                        tot = c * 2 * MM + n
                        for q in range(2):
                            src = pu[:, tot % 4, :].rearrange("p (d j q) -> p q d j", q=2, j=HALF)[:, q, :, ::-1]
                            step(tot, q, src, *(uo[:, c % 2, part, n // MM, q, d0:d0 + BANK // BL, :]
                                                for part in range(2)))

            @block.vector
            def _(v):
                for n in range(NP):
                    for y in range(2):
                        v.wait_ge(ph_mm, 2 * n + y + 1)
                        full = pp[0:2 * NB, y, :].rearrange("p (k m r) -> p k r m", k=2, r=2)
                        high, low = (gs[:, part, 2 * n:2 * n + 2, :, :, y] for part in range(2))
                        v.tensor_copy(high, full).then_inc(ph_high, 1)
                        v.wait_ge(ph_high, 2 * n + y + 1)
                        for k in range(2):
                            low_part(v, low[:, k], full[:, k], high[:, k]).then_inc(ph_out, 1)

                def low_tokens(tot, q, src, high, low):
                    v.wait_ge(u_high, 2 * tot + 2)
                    ins = low_part(v, low, src, high)
                    if q:
                        ins.then_inc(u_low, 1)

                tokens(v, low_tokens)

            @block.scalar
            def _(act):
                def high_tokens(tot, q, src, high, low):
                    act.wait_ge(u_mm, tot + 1)
                    act.activation(high, src, ACT.Copy).then_inc(u_high, 1)

                tokens(act, high_tokens)

            @block.gpsimd
            def _(pool):
                for c in range(STEPS):
                    pool.wait_ge(u_low, (c + 1) * 2 * MM)
                    for part in range(2):
                        for r in range(2):
                            for x in range(2):
                                for b2 in range(2):
                                    p0 = x * HALF + b2 * NB
                                    pool.dma_start(u_hat[part, :, x, 2 * r + b2, :, c * DC:(c + 1) * DC, :],
                                                   uo[p0:p0 + NB, c % 2, part, r].bitcast(F32)).then_inc(u_stored[c % 2], 16)


def stu_convolve(nc, sems, me, u_hat, g_hat, y_hat):
    s = Scope(nc, sems, "cv")
    NG = K // KG
    W = 2
    NI = NB // W
    GPB = W * NG
    with s.stack:
        u = s.sb("u", [P, W, 2, B, 2, 2, HALF], F32R)
        tp = s.sb("tp", [P, 2, 2, KG, 2, 2 * (HALF + 1)], F32R)
        vb = s.sb("vb", [P, 2, 2, 4, KG, B, P], F32R)
        yo = s.sb("yo", [P, 2, B, P])
        pv = s.ps("pv", [P, 4, BANK])
        py = s.ps("py", [P, 4, BANK])
        u_in = [s.sem(f"u_in{k}") for k in range(W)]
        t_in = [s.sem(f"t_in{k}") for k in range(2)]
        y_stored = [s.sem(f"y_stored{k}") for k in range(2)]
        v_mm, v_high, v_low, g_done, y_evac, yo_free = (
            s.sem(n) for n in ("v_mm", "v_high", "v_low", "g_done", "y_evac", "yo_free"))
        VT = 16
        with nc.Block() as block:

            @block.sync
            def _(sp):
                with sp.Fori(0, NI) as i:
                    for gg in range(GPB):
                        w, kg = divmod(gg, NG)
                        if kg == 0:
                            sp.wait_ge(v_mm, (i * GPB + (w + 1) * NG) * VT)
                            for part in range(2):
                                for x in range(2):
                                    sp.dma_start(u[:, w, part, :, :, x, :].rearrange("d b q j -> d (b q) j").bitcast(F32),
                                                 u_hat[part, i * W + w, x].rearrange("b q d j -> d (b q) j")
                                                 ).then_inc(u_in[w], 16)
                        sp.wait_ge(g_done, i * GPB + gg + 1)
                        for part in range(2):
                            for x in range(2):
                                row = g_hat[part, i * W + w, x, kg * KG:(kg + 1) * KG]
                                src = bass.AP(row.tensor, row.offset,
                                              ap=[[2, HALF], [2 * BL, KG * 2], [1, 2 * HALF + 2]])
                                sp.dma_start(tp[x * HALF:(x + 1) * HALF, gg % 2, part].rearrange("p k r m -> p (k r) m").bitcast(F32),
                                             src).then_inc(t_in[gg % 2], 16)

            @block.tensor
            def _(pe):
                pe.sem_inc(v_mm, GPB * VT)
                pe.sem_inc(g_done, 2)
                with pe.Fori(0, NI) as i:

                    def make_v(gg):
                        w, kg = divmod(gg, NG)
                        if kg == 0:
                            pe.wait_ge(u_in[w], i * 64 + 64)
                        for n in range(VT):
                            qt, b = divmod(n, B)
                            q, ty = divmod(qt, 2)
                            pe.wait_ge(v_low, (i * GPB + gg) * VT + n + 1)
                            product(pe, pv[:, n % 4, :], [u[:, w, part, b, q] for part in range(2)],
                                    [me[:, part, ty, kg * KG:(kg + 1) * KG, :] for part in range(2)],
                                    start=True, stop=True).then_inc(v_mm, 1)

                    def toeplitz(gg):
                        w, kg = divmod(gg, NG)
                        pe.wait_ge(t_in[gg % 2], i * (32 * GPB) + (gg // 2 + 1) * 64)
                        pe.wait_ge(v_low, (i * GPB + gg + 1) * VT + 4)
                        for p in range(2):
                            if kg == 0:
                                pe.wait_ge(y_evac, i * (2 * W) + 2 * w + p + 1)
                            for k in range(KG):
                                for q in range(2):
                                    par = p ^ q
                                    off = 0 if (p, q) == (0, 1) else 1
                                    mm = product(pe, py[:, 2 * w + p, :],
                                                 [tp[:, gg % 2, part, k, par, 2 * off:2 * off + P] for part in range(2)],
                                                 [vb[:, gg % 2, part, 2 * q + par, k] for part in range(2)],
                                                 start=(kg == 0 and k == 0 and q == 0),
                                                 stop=(kg == NG - 1 and k == KG - 1 and q == 1))
                        mm.then_inc(g_done, 1)

                    make_v(0)
                    for gg in range(GPB):
                        if gg + 1 < GPB:
                            make_v(gg + 1)
                        toeplitz(gg)

            def split_v(eng, step, i, gg):
                eng.wait_ge(g_done, i * GPB + gg + 1)
                for n in range(VT):
                    qt, b = divmod(n, B)
                    step(n, pv[:, n % 4, :].rearrange("p (k e) -> p k e", e=P),
                         *(vb[:, gg % 2, part, qt, :, b, :] for part in range(2)))

            @block.gpsimd
            def _(pool):
                pool.sem_inc(yo_free, 2)
                with pool.Fori(0, NI) as i:
                    for w in range(W):
                        for p in range(2):
                            pool.wait_ge(y_evac, i * (2 * W) + 2 * w + p + 1 + 2 * W)
                            pool.dma_start(y_hat[p, :, i * W + w].rearrange("b j y e -> (j y) b e"),
                                           yo[:, p]).then_inc(y_stored[p], 16)
                        for p in range(2):
                            pool.wait_ge(y_stored[p], i * (16 * W) + w * 16 + 16)
                            pool.sem_inc(yo_free, 1)

            @block.scalar
            def _(act):
                with act.Fori(0, NI) as i:
                    for gg in range(GPB):

                        def high_v(n, full, high, low):
                            act.wait_ge(v_mm, (i * GPB + gg + GPB) * VT + n + 1)
                            act.activation(high, full, ACT.Copy).then_inc(v_high, 1)

                        split_v(act, high_v, i, gg)

            @block.vector
            def _(v):
                v.sem_inc(v_low, 4)
                v.sem_inc(y_evac, 2 * W)

                def copy_y(i, w):
                    v.wait_ge(g_done, (i * GPB + (w + 1) * NG) + 2)
                    for p in range(2):
                        v.wait_ge(yo_free, i * (2 * W) + 2 * w + 2)
                        v.tensor_copy(yo[:, p].rearrange("p b e -> p (b e)"), py[:, 2 * w + p, :]).then_inc(y_evac, 1)

                with v.Fori(0, NI) as i:
                    for gg in range(GPB):

                        def low_v(n, full, high, low):
                            v.wait_ge(v_high, (i * GPB + gg) * VT + n + 1)
                            low_part(v, low, full, high).then_inc(v_low, 1)

                        split_v(v, low_v, i, gg)
                        if gg % NG == 1 and gg > NG:
                            copy_y(i, gg // NG - 1)
                    copy_y(i, W - 1)


def stu_finish(nc, sems, g, mu, seg, y_hat, hn, t1, out):
    s = Scope(nc, sems, "fin")
    JB = BANK // NB
    with s.stack:
        wi = s.sb("wi", [2 * NB, NB])
        yh = s.sb("yh", [2 * NB, 2, HALF, P])
        ys = s.sb("ys", [P, NB, HALF, 2])
        h = s.sb("h", [P, 2 + T])
        t = s.sb("t", [P, T])
        o = s.sb("o", [P, T])
        py = s.ps("py", [P, 2, BANK])
        pa = s.ps("pa", [P, 2, BANK])
        yh_in = [s.sem(f"yh_in{k}") for k in range(2)]
        w_in, h_in, t_in, yh_used, y_mm, y_evac, ar_mm, summed, kept, o_stored, zeroed = (
            s.sem(n) for n in ("w_in", "h_in", "t_in", "yh_used", "y_mm", "y_evac", "ar_mm", "summed", "kept",
                               "o_stored", "zeroed"))
        NT = T // BANK
        NJ = 2 * HALF // JB
        SEG = (0, 1, 2, 2, 3, 3, 3, 3)
        hv, tv, ov = (a.rearrange("p (b n) -> p b n", b=B) for a in (hn, t1, out))
        with nc.Block() as block:

            @block.sync
            def _(sp):
                sp.dma_start(wi[:], g["c_idft"]).then_inc(w_in, 16)
                with sp.Fori(0, B) as b:
                    sp.wait_ge(ar_mm, b * NT + NT)
                    sp.wait_ge(kept, b * NT + NT)
                    sp.dma_start(h[:, 2:], hv[:, b, :]).then_inc(h_in, 16)
                    sp.dma_start(t[:], tv[:, b, :]).then_inc(t_in, 16)
                    for p in range(2):
                        sp.wait_ge(yh_used, b * 2 + p + 1)
                        for x in range(2):
                            sp.dma_start(yh[x * NB:(x + 1) * NB, p], y_hat[p, b, :, :, x, :]).then_inc(yh_in[p], 16)

            @block.gpsimd
            def _(pool):
                pool.memset(h[:, 0:2], 0.0).then_inc(zeroed, 1)

            @block.tensor
            def _(pe):
                pe.sem_inc(ar_mm, NT)
                pe.sem_inc(yh_used, 2)
                pe.wait_ge(w_in, 16)
                pe.wait_ge(zeroed, 1)
                with pe.Fori(0, B) as b:
                    for p in range(2):
                        pe.wait_ge(yh_in[p], b * 32 + 32)
                        for c in range(NJ // 2):
                            n = p * (NJ // 2) + c
                            pe.wait_ge(y_evac, b * NJ + n + 1)
                            for jj in range(JB):
                                mm = pe.matmul(py[:, n % 2, jj * NB:(jj + 1) * NB], yh[:, p, c * JB + jj, :], wi[:],
                                               start=True, stop=True, skip_group_check=True)
                            mm.then_inc(y_mm, 1)
                        pe.wait_ge(y_mm, b * NJ + (p + 1) * (NJ // 2))
                        pe.sem_inc(yh_used, 1)
                    pe.wait_ge(h_in, b * 16 + 16)
                    for c in range(NT):
                        pe.wait_ge(summed, b * NT + c + 1)
                        for d in range(3):
                            mm = pe.matmul(pa[:, c % 2, :], mu[:, d, :], h[:, 2 - d + c * BANK:2 - d + (c + 1) * BANK],
                                           start=(d == 0), stop=(d == 2))
                        mm.then_inc(ar_mm, 1)

            @block.vector
            def _(v):
                v.sem_inc(y_evac, 2)
                v.sem_inc(summed, 2)
                v.sem_inc(kept, NT)
                with v.Fori(0, B) as b:
                    v.wait_ge(kept, b * NT + NT)
                    for n in range(NJ):
                        p, c = divmod(n, NJ // 2)
                        v.wait_ge(y_mm, b * NJ + n + 1)
                        v.tensor_copy(ys[:, :, c * JB:(c + 1) * JB, p],
                                      py[:, n % 2, :].rearrange("e (j a) -> e a j", a=NB)).then_inc(y_evac, 1)
                    v.wait_ge(y_evac, b * NJ + NJ + 2)
                    v.wait_ge(t_in, b * 16 + 16)
                    v.wait_ge(o_stored, b * 16 + 16)
                    yf = ys[:].rearrange("e a j q -> e (a j q)")
                    for c in range(NT):
                        sl = slice(c * BANK, (c + 1) * BANK)
                        v.wait_ge(ar_mm, b * NT + c + 1 + NT)
                        v.tensor_tensor(yf[:, sl], yf[:, sl], pa[:, c % 2, :], ALU.add).then_inc(summed, 1)
                        v.wait_ge(summed, b * NT + c + 3)
                        v.scalar_tensor_tensor(o[:, sl], yf[:, sl], seg[:, SEG[c]:SEG[c] + 1], t[:, sl],
                                               ALU.mult, ALU.add).then_inc(kept, 1)

            @block.scalar
            def _(act):
                act.sem_inc(o_stored, 16)
                with act.Fori(0, B) as b:
                    act.wait_ge(kept, b * NT + 2 * NT)
                    act.dma_start(ov[:, b, :], o[:]).then_inc(o_stored, 16)
                act.wait_ge(o_stored, 16 * (B + 1))


def program(nc, g, out):
    def scratch(name):
        return nc.dram_tensor(name, (P, N), F32, kind="Internal").ap()

    c3, t0, t1, hn1, hn2, hf, hb = (scratch(n) for n in ("c3", "t0", "t1", "hn1", "hn2", "h_forward", "h_backward"))
    sems = []
    conv_block(nc, sems, g, c3)
    attention(nc, sems, g, c3, t0)
    layer_norm(nc, sems, "ln1", [t0], None, hn1, g["c_mean"])
    release(nc, sems)
    mamba(nc, sems, g, hn1, (hf, hb))
    release(nc, sems)
    layer_norm(nc, sems, "ln2", [t0, hf, hb], t1, hn2, g["c_mean"])
    spectral(nc, sems, g, hn2, t1, out)


def laid_out(inputs):
    i = {k: np.asarray(v) for k, v in inputs.items()}
    col = lambda a: a[:, None]
    rep = lambda a: np.broadcast_to(a, (P,) + a.shape)
    c = {k[8:]: v for k, v in i.items() if k.startswith("L0_conv_")}
    m = [{k[12:]: v for k, v in i.items() if k.startswith(f"L1_attn_{p}")} for p in ("fwd", "bwd")]
    f = {k[7:]: v for k, v in i.items() if k.startswith("L1_ffn_")}
    a = {"x": i["x"].reshape(N, P).T, "W1": c["W1"], "W2": c["W2"], "b1": col(c["b1"]), "b2a": col(c["b2"][:P]),
         "b2b": col(c["b2"][P:]), "Wv": c["Wv"], "bv": rep(c["bv"]), "W3": c["W3"], "b3": col(c["b3"])}
    a["Wqk"], a["bqk"] = np.zeros((P, P), np.float32), np.zeros((P, 1), np.float32)
    for n in range(PARTS * PARTS):
        for at, w, b in ((0, "Wq", "bq"), (64, "Wk", "bk")):
            a["Wqk"][:, at + n * DQK:at + (n + 1) * DQK] = c[w]
            a["bqk"][at + n * DQK:at + (n + 1) * DQK, 0] = c[b]
    nz = 2 * DI + 2 * DS
    a["Wdt"] = np.concatenate([d["in_proj"][:, nz:] for d in m], 1)
    a["dt_bias"] = rep(np.stack([d["dt_bias"] for d in m]))
    a["A_log"] = rep(np.stack([d["A_log"] for d in m]))
    for n, d in enumerate(m):
        a[f"in_proj{n}"] = d["in_proj"][:, :nz]
        a[f"conv_w{n}"] = d["conv_w"].reshape(3, P, TAPS).transpose(1, 0, 2)
        a[f"conv_b{n}"] = d["conv_b"].reshape(3, P).T
        a[f"D{n}"] = np.repeat(d["D"], HD).reshape(2, P).T
        a[f"norm_w{n}"] = d["norm_w"].reshape(2, P).T
        a[f"out_proj{n}"] = d["out_proj"].reshape(2, P, P).transpose(1, 0, 2)
    a["phi"] = np.zeros((K, BL + T), np.float32)
    a["phi"][:, BL:] = f["phi"].T
    a.update(M_u=f["M_u"], M_phi_plus=f["M_phi_plus"], M_phi_minus=f["M_phi_minus"], sigma=rep(f["sigma"]),
             log_weights=rep(f["log_weights"]), gumbel=rep(f["gumbel"]), c_mean=np.full((P, P), 1 / P, np.float32))
    for constants in (attention_constants(), mamba_constants(), stu_constants()):
        a.update(constants)
    return {k: np.ascontiguousarray(v) for k, v in a.items()}


def kernel(**inputs):
    import concourse.bacc as bacc
    from concourse.bass_utils import run_bass_kernel_spmd

    arrays = laid_out(inputs)
    nc = bacc.Bacc("TRN2", target_bir_lowering=False, num_devices=1)
    g = {k: nc.dram_tensor(f"in_{k}", v.shape, F32, kind="ExternalInput").ap() for k, v in arrays.items()}
    out = nc.dram_tensor("out", (P, N), F32, kind="ExternalOutput").ap()
    program(nc, g, out)
    r = run_bass_kernel_spmd(nc, [{f"in_{k}": v for k, v in arrays.items()}], core_ids=[0])
    return r.results[0]["out"].T.reshape(B, IMG, IMG, P)
```

```python
from contextlib import ExitStack

import numpy as np

import concourse.bass as bass
from concourse import mybir

F32 = mybir.dt.float32
BF16 = mybir.dt.bfloat16
F32R = mybir.dt.float32r
ALU = mybir.AluOpType
ACT = mybir.ActivationFunctionType
AX = mybir.AxisListType

P = 128
B, IMG = 4, 64
T = IMG * IMG
N = B * T
BANK = 512
TILES = N // BANK

DQK, DV, HEADS = 4, 16, 8
PARTS = 3
PAIRS = PARTS * PARTS * DQK
MROW = 64
MASK1, MASK2 = -1.0e30, -2.0e38

CH = 128
NCH = T // CH
NH, HD, DS, DI = 4, 64, 64, 256
TAPS = 4

K = 16
BL, NB, HALF = 128, 32, 64
NF = 2 * NB
KG = 4
FRACS = (1, 2, 4, 8)


class Scope:

    def __init__(self, nc, sems, name):
        self.nc, self.sems, self.name, self.stack = nc, sems, name, ExitStack()

    def sb(self, name, shape, dt=F32):
        return self.stack.enter_context(self.nc.sbuf_tensor(f"{self.name}_{name}", shape, dt))

    def ps(self, name, shape, dt=F32):
        return self.stack.enter_context(self.nc.psum_tensor(f"{self.name}_{name}", shape, dt))

    def sem(self, name):
        self.sems.append(self.nc.alloc_semaphore(name=f"{self.name}_{name}"))
        return self.sems[-1]


def product(pe, out, stationary, moving, start, stop, **kw):
    for n, (a, b) in enumerate(((0, 0), (0, 1), (1, 0))):
        mm = pe.matmul(out, stationary[a], moving[b], start=start and n == 0, stop=stop and n == 2, **kw)
    return mm


def low_part(v, out, full, high):
    return v.tensor_tensor(out, full, high.bitcast(F32), ALU.subtract)


def hold(eng, passed):
    eng.sem_inc(passed, 1)


def release(nc, sems):
    nc.clear_and_free_semaphores(sems)
    nc.all_engine_barrier()
    sems.clear()


def layer_norm(nc, sems, name, addends, total, out, c_mean):
    s = Scope(nc, sems, name)
    na = len(addends)
    G, ITER = 4, TILES // 8
    with s.stack:
        mean_w = s.sb("mean_w", [P, P])
        eps = s.sb("eps", [P, 1])
        x = s.sb("x", [P, 2, na, G, BANK])
        xc = s.sb("xc", [P, 2, G, BANK])
        sq = s.sb("sq", [P, G, BANK])
        rs = s.sb("rs", [P, G, BANK])
        y = s.sb("y", [P, 2, G, BANK])
        mean = s.ps("mean", [P, G, BANK])
        var = s.ps("var", [P, G, BANK])
        loaded, stored = ([s.sem(f"{n}{k}") for k in range(2)] for n in ("loaded", "stored"))
        w_in, summed, mean_done, centred, squared, var_done, logged, rooted, normed, eps_set = (
            s.sem(n) for n in ("w_in", "summed", "mean_done", "centred", "squared", "var_done", "logged", "rooted",
                               "normed", "eps_set"))
        per_store = 16 * (2 if total is not None else 1)
        views = [a.rearrange("p (t n) -> p t n", n=G * BANK) for a in addends]
        out_v = out.rearrange("p (t n) -> p t n", n=G * BANK)
        tot_v = total.rearrange("p (t n) -> p t n", n=G * BANK) if total is not None else None
        flat = lambda ap: ap.rearrange("p g n -> p (g n)")
        with nc.Block() as block:

            @block.sync
            def _(sp):
                sp.dma_start(mean_w[:], c_mean).then_inc(w_in, 16)
                with sp.Fori(0, ITER) as i:
                    for k in range(2):
                        sp.wait_ge(normed, i * (2 * G) + (k + 1) * G)
                        sp.wait_ge(stored[k], i * per_store + per_store)
                        for a in range(na):
                            sp.dma_start(flat(x[:, k, a]), views[a][:, i * 2 + k, :]).then_inc(loaded[k], 16)

            @block.vector
            def _(v):
                v.memset(eps[:], 1e-5).then_inc(eps_set, 1)
                v.sem_inc(normed, 2 * G)
                v.sem_inc(centred, G)
                with v.Fori(0, ITER) as i:
                    for k in range(2):
                        v.wait_ge(loaded[k], i * (16 * na) + 16 * na)
                        for a in range(1, na):
                            for t in range(G):
                                if a > 1:
                                    v.wait_ge(summed, (i * 2 + k) * ((na - 1) * G) + (a - 2) * G + t + 1)
                                v.tensor_tensor(x[:, k, 0, t], x[:, k, 0, t], x[:, k, a, t], ALU.add
                                                ).then_inc(summed, 1)
                        for t in range(G):
                            v.wait_ge(mean_done, (i * 2 + k) * G + t + 1)
                            v.tensor_tensor(xc[:, k, t], x[:, k, 0, t], mean[:, t], ALU.subtract).then_inc(centred, 1)
                        v.wait_ge(stored[k], i * per_store + per_store)
                        for t in range(G):
                            v.wait_ge(rooted, (i * 2 + k) * G + t + 1)
                            v.tensor_tensor(y[:, k, t], xc[:, k, t], rs[:, t], ALU.mult).then_inc(normed, 1)

            @block.tensor
            def _(pe):
                pe.wait_ge(w_in, 16)
                with pe.Fori(0, ITER) as i:
                    for k in range(2):
                        pe.wait_ge(loaded[k], i * (16 * na) + 16 * na)
                        for t in range(G):
                            if na > 1:
                                pe.wait_ge(summed, (i * 2 + k) * ((na - 1) * G) + (na - 2) * G + t + 1)
                            pe.wait_ge(centred, (i * 2 + k) * G + t + 1)
                            pe.matmul(mean[:, t], mean_w[:], x[:, k, 0, t], start=True, stop=True
                                      ).then_inc(mean_done, 1)
                        for t in range(G):
                            pe.wait_ge(squared, (i * 2 + k) * G + t + 1)
                            pe.matmul(var[:, t], mean_w[:], sq[:, t], start=True, stop=True).then_inc(var_done, 1)

            @block.scalar
            def _(act):
                for k in range(2):
                    act.sem_inc(stored[k], per_store)
                act.wait_ge(eps_set, 1)
                with act.Fori(0, ITER) as i:
                    for k in range(2):
                        for t in range(G):
                            act.wait_ge(centred, (i * 2 + k) * G + t + 1 + G)
                            act.activation(sq[:, t], xc[:, k, t], ACT.Square).then_inc(squared, 1)
                        for t in range(G):
                            act.wait_ge(var_done, (i * 2 + k) * G + t + 1)
                            act.wait_ge(normed, (i * 2 + k) * G + t + 1 + G)
                            act.activation(rs[:, t], var[:, t], ACT.Ln, bias=eps[:, 0:1]).then_inc(logged, 1)
                        for t in range(G):
                            act.wait_ge(logged, (i * 2 + k) * G + t + 1)
                            act.activation(rs[:, t], rs[:, t], ACT.Exp, scale=-0.5).then_inc(rooted, 1)
                        act.wait_ge(normed, (i * 2 + k) * G + 3 * G)
                        act.dma_start(out_v[:, i * 2 + k, :], flat(y[:, k])).then_inc(stored[k], 16)
                        if total is not None:
                            act.dma_start(tot_v[:, i * 2 + k, :], flat(x[:, k, 0])).then_inc(stored[k], 16)
                for k in range(2):
                    act.wait_ge(stored[k], per_store * (ITER + 1))


PW = IMG + 2
ROWS = BANK // IMG
GT = T // BANK


def conv_block(nc, sems, g, c3):
    s = Scope(nc, sems, "conv")
    Q = 4
    QR = IMG // Q
    with s.stack:
        w_raw = s.sb("w_raw", [P, 27 * P])
        w = s.sb("w", [P, 2, 27 * P], F32R)
        bias = s.sb("bias", [P, 3])
        x = s.sb("x", [P, IMG, IMG])
        neg = s.sb("neg", [P, 2, QR, IMG])
        pos = s.sb("pos", [P, 2, QR, IMG])
        ex = s.sb("ex", [P, 2, QR, IMG])
        xp = s.sb("xp", [P, 2, PW, PW], F32R)
        c1 = s.sb("c1", [P, 2, PW, PW], F32R)
        sg = s.sb("sg", [P, 2, BANK])
        co = s.sb("co", [P, 2, BANK])
        p1 = s.ps("p1", [P, 2, BANK])
        pa = s.ps("pa", [P, 2, BANK])
        pb = s.ps("pb", [P, 2, BANK])
        w_in, w_high, w_low, x_in, halves, exped, added, x_high, elu_done, c1_mm, c1_high, c1_evac, c2_mm, gated, \
            sig_done, bordered, passed = (s.sem(n) for n in (
                "w_in", "w_high", "w_low", "x_in", "halves", "exped", "added", "x_high", "elu_done", "c1_mm", "c1_high",
                "c1_evac", "c2_mm", "gated", "sig_done", "bordered", "passed"))
        w1 = [w[:, part, 0:9 * P].rearrange("i (k o) -> i k o", o=P) for part in range(2)]
        w2 = [w[:, part, 9 * P:].rearrange("i (k o) -> i k o", o=2 * P) for part in range(2)]
        stored = [s.sem(f"stored{k}") for k in range(2)]
        xv = g["x"].rearrange("p (b h w) -> p b h w", b=B, h=IMG)
        cv = c3.rearrange("p (b g n) -> p b g n", b=B, g=GT)

        def interior(part, t):
            return c1[:, part, 1 + t * ROWS:1 + (t + 1) * ROWS, 1:1 + IMG]

        def image(ap):
            return ap.rearrange("p (r c) -> p r c", c=IMG)

        with nc.Block() as block:

            @block.sync
            def _(sp):
                sp.dma_start(x[:], xv[:, 0]).then_inc(x_in, 16)
                sp.dma_start(w_raw[:, 0:9 * P].rearrange("i (k o) -> i k o", o=P),
                             g["W1"].rearrange("h w i o -> i (h w) o")).then_inc(w_in, 16)
                sp.dma_start(w_raw[:, 9 * P:].rearrange("i (k o) -> i k o", o=2 * P),
                             g["W2"].rearrange("h w i o -> i (h w) o")).then_inc(w_in, 16)
                for k, name in enumerate(("b1", "b2a", "b2b")):
                    sp.dma_start(bias[:, k:k + 1], g[name]).then_inc(w_in, 16)
                with sp.Fori(0, B - 1) as b:
                    sp.wait_ge(halves, b * (2 * Q) + 2 * Q)
                    sp.dma_start(x[:], xv[:, b + 1]).then_inc(x_in, 16)

            @block.gpsimd
            def _(pool):
                with pool.Fori(0, B) as b:
                    pool.wait_ge(x_in, b * 16 + 16)
                    for q in range(Q):
                        pool.wait_ge(elu_done, b * Q + q + 1)
                        hold(pool, passed)
                        rows = x[:, q * QR:(q + 1) * QR, :]
                        pool.tensor_scalar(neg[:, q % 2], rows, 0.0, None, ALU.min).then_inc(halves, 1)
                        pool.tensor_scalar(pos[:, q % 2], rows, 0.0, None, ALU.max).then_inc(halves, 1)

            @block.tensor
            def _(pe):
                pe.sem_inc(c1_mm, GT)
                pe.wait_ge(w_low, 1)
                pe.wait_ge(bordered, 4)
                with pe.Fori(0, B) as b:
                    for t in range(GT):
                        pe.wait_ge(elu_done, b * Q + min(ROWS * (t + 1), IMG - 1) // QR + 1 + 2)
                        pe.wait_ge(c1_evac, b * GT + t + 1)
                        for k in range(9):
                            dy, dx = divmod(k, 3)
                            mm = product(pe, p1[:, t % 2, :], [w1[part][:, k, :] for part in range(2)],
                                         [xp[:, part, t * ROWS + dy:t * ROWS + dy + ROWS, dx:dx + IMG]
                                          for part in range(2)], start=(k == 0), stop=(k == 8))
                        mm.then_inc(c1_mm, 1)
                    for t in range(GT):
                        pe.wait_ge(c1_evac, b * GT + min(t + 2, GT) + 2)
                        pe.wait_ge(gated, b * GT + t + 1)
                        for half, bank in enumerate((pa, pb)):
                            for k in range(9):
                                dy, dx = divmod(k, 3)
                                mm = product(pe, bank[:, t % 2, :],
                                             [w2[part][:, k, half * P:(half + 1) * P] for part in range(2)],
                                             [c1[:, part, t * ROWS + dy:t * ROWS + dy + ROWS, dx:dx + IMG]
                                              for part in range(2)], start=(k == 0), stop=(k == 8))
                        mm.then_inc(c2_mm, 1)

            @block.scalar
            def _(act):
                for k in range(2):
                    act.sem_inc(stored[k], 16)

                def exps(b):
                    for q in range(Q):
                        act.wait_ge(halves, b * (2 * Q) + 2 * q + 2)
                        act.activation(ex[:, q % 2], neg[:, q % 2], ACT.Exp).then_inc(exped, 1)
                        act.wait_ge(added, b * Q + q + 1)
                        act.activation(xp[:, 0, 1 + q * QR:1 + (q + 1) * QR, 1:1 + IMG], ex[:, q % 2], ACT.Copy
                                       ).then_inc(x_high, 1)

                def store(b, t):
                    act.wait_ge(gated, b * GT + t + 1 + 2)
                    act.dma_start(cv[:, b, t, :], co[:, t % 2, :]).then_inc(stored[t % 2], 16)

                def batch(b, more):
                    for t in range(GT):
                        act.wait_ge(c1_mm, b * GT + t + 1 + GT)
                        act.activation(interior(0, t), image(p1[:, t % 2, :]), ACT.Identity, bias=bias[:, 0:1]
                                       ).then_inc(c1_high, 1)
                    for t in range(GT):
                        if t == GT // 2 and more:
                            exps(b + 1)
                        act.wait_ge(c2_mm, b * GT + t + 1)
                        act.activation(sg[:, t % 2, :], pb[:, t % 2, :], ACT.Sigmoid, bias=bias[:, 2:3]
                                       ).then_inc(sig_done, 1)
                        if t:
                            store(b, t - 1)
                    store(b, GT - 1)

                act.wait_ge(w_in, 80)
                act.activation(w[:, 0], w_raw[:], ACT.Copy).then_inc(w_high, 1)
                act.wait_ge(bordered, 4)
                exps(0)
                with act.Fori(0, B - 1) as b:
                    batch(b, True)
                batch(B - 1, False)
                for k in range(2):
                    act.wait_ge(stored[k], 16 * (B * GT // 2 + 1))

            @block.vector
            def _(v):
                v.sem_inc(elu_done, 2)
                v.sem_inc(gated, 2)
                v.sem_inc(c1_evac, 2)
                for part in range(2):
                    v.memset(xp[:, part].bitcast(F32), 0.0).then_inc(bordered, 1)
                for part in range(2):
                    v.memset(c1[:, part].bitcast(F32), 0.0).then_inc(bordered, 1)
                v.wait_ge(bordered, 4)
                v.wait_ge(w_high, 1)
                low_part(v, w[:, 1], w_raw[:], w[:, 0]).then_inc(w_low, 1)

                def elus(b):
                    v.wait_ge(c1_mm, b * GT + GT)
                    for q in range(Q):
                        v.wait_ge(exped, b * Q + q + 1)
                        v.scalar_tensor_tensor(ex[:, q % 2], ex[:, q % 2], -1.0, pos[:, q % 2], ALU.add, ALU.add
                                               ).then_inc(added, 1)
                        v.wait_ge(x_high, b * Q + q + 1)
                        rows = slice(1 + q * QR, 1 + (q + 1) * QR)
                        low_part(v, xp[:, 1, rows, 1:1 + IMG], ex[:, q % 2], xp[:, 0, rows, 1:1 + IMG]
                                 ).then_inc(elu_done, 1)

                def batch(b, more):
                    for t in range(GT):
                        v.wait_ge(c1_high, b * GT + t + 1)
                        v.scalar_tensor_tensor(interior(1, t), image(p1[:, t % 2, :]), bias[:, 0:1],
                                               interior(0, t).bitcast(F32), ALU.add, ALU.subtract).then_inc(c1_evac, 1)
                    for t in range(GT):
                        if t == GT // 2 and more:
                            elus(b + 1)
                        v.wait_ge(sig_done, b * GT + t + 1)
                        v.wait_ge(stored[t % 2], b * (16 * GT // 2) + (t // 2) * 16 + 16)
                        v.scalar_tensor_tensor(co[:, t % 2, :], pa[:, t % 2, :], bias[:, 1:2], sg[:, t % 2, :],
                                               ALU.add, ALU.mult).then_inc(gated, 1)

                elus(0)
                with v.Fori(0, B - 1) as b:
                    batch(b, True)
                batch(B - 1, False)


def attention_constants():
    rows = np.arange(P)
    sel = np.zeros((P, 4), np.float32)
    for side in range(2):
        for i in range(PARTS):
            for j in range(PARTS):
                part = (i, j)[side]
                for d in range(DQK):
                    r = 64 * side + (i * PARTS + j) * DQK + d
                    sel[r, 0], sel[r, 1] = -float(part >= 1), -float(part >= 2)
    for part in range(PARTS):
        sel[MROW + part, 2], sel[MROW + part, 3] = -float(part >= 1), -float(part >= 2)
    mask = np.stack([np.where(rows[None, :] >= rows[:, None], MASK1, 0.0),
                     np.where(rows[:, None] >= rows[None, :], MASK2, 0.0)])
    fold = (rows[:, None] % DV == np.arange(DV)[None, :]).astype(np.float32)
    return {"c_sel": sel, "c_mask": mask.astype(np.float32), "c_ident": np.eye(P, dtype=np.float32),
            "c_fold": fold}


def attention(nc, sems, g, c3, t0):
    s = Scope(nc, sems, "att")
    NT = T // P
    items = [(G, kt) for G in range(GT) for kt in range(4 * G + 4)]
    NI = len(items)
    first = [2 * G * (G + 1) for G in range(GT + 1)]
    LAG, NS, NE = 1, 2, 4
    SLOTS = NI + LAG + 12
    units = [(i, k) for i in range(NT) for k in range(i // 4 + 1)]
    NU = len(units)
    SPLIT0, V_AT, UNIT0 = 2, 30, 8
    V_PARTS = [V_AT - 6, V_AT - 4, V_AT - 2, V_AT]
    M_AT = UNIT0 + NU * 3 // 4 + 2
    R_AT = M_AT + 6
    NORM = [first[G + 1] + LAG for G in range(GT)]
    AT, PROJ, RES, STORE = 4, 6, 8, 10

    def units_at(n):
        return [u for u in range(NU) if UNIT0 + u * 3 // 4 == n]

    def split_at(n):
        t, odd = divmod(n - SPLIT0, 2)
        return t if not odd and 0 <= t <= GT else None

    m_dram = nc.dram_tensor("row_max", (B, T), F32, kind="Internal").ap()
    MH = T // 2
    rows = slice(MROW, MROW + PARTS)
    with s.stack:
        qs = s.sb("qs", [MROW + PARTS, B, T], BF16)
        ks = s.sb("ks", [MROW + PARTS, B, T], BF16)
        va = s.sb("va", [P, B, NT, 48])
        vc = s.sb("vc", [P, NT, 48])
        ident = s.sb("ident", [P, P])
        identb = s.sb("identb", [P, P], BF16)
        mask = s.sb("mask", [P, 2, P], BF16)
        mk = s.sb("mk", [P, 2, P])
        sel = s.sb("sel", [P, 4])
        wqk = s.sb("wqk", [P, P])
        wv = s.sb("wv", [P, DV])
        bqk = s.sb("bqk", [P, 1])
        bv = s.sb("bv", [P, DV])
        fold = s.sb("fold", [P, DV])
        w3 = s.sb("w3", [P, P])
        w3s = s.sb("w3s", [DV, P])
        b3 = s.sb("b3", [P, 1])
        f = s.sb("f", [P, T])
        qf = s.sb("qf", [P, 2, BANK])
        h1 = s.sb("h1", [P, 2, BANK], BF16)
        r1 = s.sb("r1", [P, 2, BANK])
        h2 = s.sb("h2", [P, 2, BANK], BF16)
        mp = s.sb("mp", [P, NT, GT])
        mall = s.sb("mall", [P, NT])
        mt = s.sb("mt", [NT, P])
        m_row = s.sb("m_row", [MROW + PARTS, 2, MH])
        m_h = s.sb("m_h", [MROW + PARTS, 2, MH], BF16)
        m_r = s.sb("m_r", [MROW + PARTS, 2, MH])
        e = s.sb("e", [P, NE, BANK])
        xr = s.sb("xr", [P, 2, BANK])
        cr = s.sb("cr", [P, 2, BANK])
        den = s.sb("den", [DV, BANK])
        rec = s.sb("rec", [DV, BANK])
        at = s.sb("at", [DV, BANK])
        o1 = s.sb("o1", [P, BANK])
        o2 = s.sb("o2", [P, 2, BANK])
        pq = s.ps("pq", [P, BANK])
        pu = s.ps("pu", [P, 2, BANK])
        sc = s.ps("sc", [P, NS, BANK])
        po = s.ps("po", [64, 2, BANK])
        pm = s.ps("pm", [P, BANK])
        (w_in, ready, f_in, qk_mm, v_mm, qf_done, h1_done, r1_done, h2_done, split, v_done, unit_mm, maxed, m_done,
         mt_mm, mt_done, m_stored, mh_done, mr_done, mh2_done, row_split) = (s.sem(n) for n in (
             "w_in", "ready", "f_in", "qk_mm", "v_mm", "qf_done", "h1_done", "r1_done", "h2_done", "split", "v_done",
             "unit_mm", "maxed", "m_done", "mt_mm", "mt_done", "m_stored", "mh_done", "mr_done", "mh2_done",
             "row_split"))
        passed = s.sem("passed")
        (fold_mm, fold_done, vc_done, sc_mm, exped, pv_mm, den_done, rec_done, at_done, proj_mm, o1_done, o2_done) = (
            s.sem(n) for n in ("fold_mm", "fold_done", "vc_done", "sc_mm", "exped", "pv_mm", "den_done", "rec_done",
                               "at_done", "proj_mm", "o1_done", "o2_done"))
        m_in, r_in, stored = ([s.sem(f"{n}{k}") for k in range(2)] for n in ("m_in", "r_in", "stored"))
        cb = c3.rearrange("p (b n) -> p b n", b=B)
        xv, cv, tv = (a.rearrange("p (b g n) -> p b g n", b=B, g=GT) for a in (g["x"], c3, t0))
        NW = 10 * 16
        READY = 7

        def batches(eng, values, coming):
            for n in range(SLOTS):
                coming(0, n)
            with eng.Fori(0, B - 1) as b:
                for n in range(SLOTS):
                    values(b, n)
                    coming(b + 1, n)
            for n in range(SLOTS):
                values(B - 1, n)

        with nc.Block() as block:

            @block.sync
            def _(sp):
                for dst, name in ((wqk, "Wqk"), (wv, "Wv"), (bqk, "bqk"), (bv, "bv"), (ident, "c_ident"), (sel, "c_sel"),
                                  (mk, "c_mask"), (fold, "c_fold"), (w3, "W3"), (b3, "b3")):
                    src = g[name].rearrange("m p n -> p m n") if name == "c_mask" else g[name]
                    sp.dma_start(dst[:], src).then_inc(w_in, 16)

                def values(b, n):
                    for G in range(GT):
                        if n == first[G]:
                            sp.wait_ge(o2_done, b * GT + G + 1)
                            sp.dma_start(xr[:, G % 2, :], xv[:, b, G, :]).then_inc(r_in[G % 2], 16)
                            sp.dma_start(cr[:, G % 2, :], cv[:, b, G, :]).then_inc(r_in[G % 2], 16)

                def coming(m, n):
                    if n == 0:
                        sp.wait_ge(v_mm, m + 1)
                        sp.dma_start(f[:], cb[:, m, :]).then_inc(f_in, 16)
                    if n == M_AT:
                        sp.wait_ge(m_stored, m * 16 + 32)
                        for k in range(2):
                            sp.wait_ge(row_split, m * 2 + k + 1)
                            for r0 in range(PARTS):
                                src = m_dram[m:m + 1] if isinstance(m, int) else m_dram[bass.ds(m, 1)]
                                sp.dma_start(m_row[MROW + r0:MROW + r0 + 1, k, :], src[:, k * MH:(k + 1) * MH]
                                             ).then_inc(m_in[k], 16)

                batches(sp, values, coming)

            @block.gpsimd
            def _(pool):
                pool.wait_ge(w_in, NW)
                pool.tensor_copy(identb[:], ident[:]).then_inc(ready, 1)
                pool.tensor_copy(mask[:], mk[:]).then_inc(ready, 1)
                pool.memset(va[:, :, :, DV:2 * DV], 0.0).then_inc(ready, 1)
                pool.memset(va[:, :, :, 2 * DV:3 * DV], 1.0).then_inc(ready, 1)
                pool.wait_ge(ready, READY)
                with pool.Fori(0, B) as b:
                    pool.wait_ge(pv_mm, b * NI + NI)
                    pool.wait_ge(v_done, b + 2)
                    hold(pool, passed)
                    pool.tensor_copy(vc[:], va[:, b]).then_inc(vc_done, 1)

            @block.tensor
            def _(pe):
                pe.sem_inc(v_mm, 1)
                pe.sem_inc(pv_mm, NI)
                pe.wait_ge(w_in, NW)
                pe.matmul(pm[0:DV, 0:P], fold[:], w3[:], start=True, stop=True).then_inc(fold_mm, 1)
                pe.wait_ge(fold_done, 1)
                pe.wait_ge(ready, READY)

                def scores(b, n):
                    G, kt = items[n]
                    c0 = max(0, kt - 4 * G) * P
                    diag = kt >= 4 * G
                    pe.wait_ge(exped, b * NI + n + 1)
                    if n == 0:
                        pe.wait_ge(row_split, b * 2 + 4)
                    mm = pe.matmul(sc[:, n % NS, c0:], ks[:, b, kt * P:(kt + 1) * P],
                                   qs[:, b, G * BANK + c0:(G + 1) * BANK], start=True, stop=not diag)
                    if diag:
                        mm = pe.matmul(sc[:, n % NS, c0:c0 + P], identb[:], mask[:, 1, :], start=False, stop=True)
                    mm.then_inc(sc_mm, 1)

                def weigh(b, n):
                    G, kt = items[n]
                    c0 = max(0, kt - 4 * G) * P
                    if n == 0:
                        pe.wait_ge(vc_done, b + 1)
                    if kt == 0:
                        pe.wait_ge(at_done, b * GT + G + 1)
                    pe.wait_ge(exped, b * NI + n + 1 + NS)
                    pe.matmul(po[0:48, G % 2, c0:], vc[:, kt, :], e[:, n % NE, c0:], start=(kt == 0),
                              stop=(kt == 4 * G + 3)).then_inc(pv_mm, 1)

                def values(b, n):
                    if n < NI:
                        scores(b, n)
                    if LAG <= n < NI + LAG:
                        weigh(b, n - LAG)
                    for G in range(GT):
                        if n == NORM[G] + PROJ:
                            pe.wait_ge(at_done, b * GT + G + 3)
                            pe.wait_ge(o1_done, b * GT + G + 1)
                            pe.matmul(pm[:], w3s[:], at[:], start=True, stop=True).then_inc(proj_mm, 1)

                def coming(m, n):
                    t = split_at(n)
                    if t is not None and t < GT:
                        if t == 0:
                            pe.wait_ge(f_in, m * 16 + 16)
                            pe.wait_ge(mt_done, m + 1)
                        else:
                            pe.wait_ge(qf_done, m * GT + t)
                        pe.matmul(pq[:], wqk[:], f[:, t * BANK:(t + 1) * BANK], start=True, stop=True
                                  ).then_inc(qk_mm, 1)
                    if n in V_PARTS:
                        quarter = V_PARTS.index(n)
                        if quarter == 0:
                            pe.wait_ge(qf_done, m * GT + GT)
                        for k in range(quarter * NT // 4, (quarter + 1) * NT // 4):
                            mm = pe.matmul(pq[:, k * DV:(k + 1) * DV], f[:, k * P:(k + 1) * P], wv[:], start=True,
                                           stop=True, skip_group_check=True)
                        if quarter == 3:
                            mm.then_inc(v_mm, 1)
                    for u in units_at(n):
                        i, k = units[u]
                        if k == 0 and i % 4 == 0:
                            pe.wait_ge(split, m * (2 * GT) + 2 * (i // 4 + 1) + 4)
                        pe.wait_ge(maxed, m * NU + u + 1)
                        diag = k == i // 4
                        wid = (i % 4 + 1) * P if diag else BANK
                        mm = pe.matmul(pu[:, u % 2, 0:wid], qs[:, m, i * P:(i + 1) * P],
                                       ks[:, m, k * BANK:k * BANK + wid], start=True, stop=not diag,
                                       skip_group_check=True)
                        if diag:
                            mm = pe.matmul(pu[:, u % 2, wid - P:wid], identb[:], mask[:, 0, :],
                                           start=False, stop=True, skip_group_check=True)
                        mm.then_inc(unit_mm, 1)
                    if n == M_AT:
                        pe.wait_ge(m_done, m + 1)
                        pe.wait_ge(v_done, m + 2)
                        pe.transpose(pq[0:NT, 0:P], mall[:], ident[:]).then_inc(mt_mm, 1)

                batches(pe, values, coming)

            @block.scalar
            def _(act):
                act.sem_inc(mt_done, 1)
                act.sem_inc(m_stored, 16)
                act.sem_inc(exped, NS)
                for k in range(2):
                    act.sem_inc(stored[k], 16)
                act.wait_ge(w_in, NW)
                act.wait_ge(fold_mm, 1)
                act.activation(w3s[:], pm[0:DV, 0:P], ACT.Copy).then_inc(fold_done, 1)

                def values(b, n):
                    if n < NI:
                        G, kt = items[n]
                        c0 = max(0, kt - 4 * G) * P
                        act.wait_ge(sc_mm, b * NI + n + 1)
                        act.wait_ge(pv_mm, b * NI + n + 1 + NI - NE)
                        act.activation(e[:, n % NE, c0:], sc[:, n % NS, c0:], ACT.Exp, scale=1.0 / float(np.sqrt(P // 8))
                                       ).then_inc(exped, 1)
                    for G in range(GT):
                        if n == NORM[G] + STORE:
                            act.wait_ge(o2_done, b * GT + G + 1 + 2)
                            act.dma_start(tv[:, b, G, :], o2[:, G % 2, :]).then_inc(stored[G % 2], 16)

                def coming(m, n):
                    t = split_at(n)
                    if t is not None and t < GT:
                        act.wait_ge(qk_mm, m * GT + t + 1)
                        act.wait_ge(split, m * (2 * GT) + 2 * t + 2)
                        act.activation(qf[:, t % 2, :], pq[:], ACT.Identity, bias=bqk[:, 0:1]).then_inc(qf_done, 1)
                        act.wait_ge(qf_done, m * GT + t + 1)
                        act.activation(h1[:, t % 2, :], qf[:, t % 2, :], ACT.Copy).then_inc(h1_done, 1)
                    if t:
                        act.wait_ge(r1_done, m * GT + t)
                        act.activation(h2[:, (t - 1) % 2, :], r1[:, (t - 1) % 2, :], ACT.Copy).then_inc(h2_done, 1)
                    if n == M_AT:
                        act.wait_ge(mt_mm, m + 1)
                        act.wait_ge(m_stored, m * 16 + 16)
                        act.activation(mt[:], pq[0:NT, 0:P], ACT.Copy).then_inc(mt_done, 1)
                        act.wait_ge(mt_done, m + 2)
                        dst = m_dram[m:m + 1] if isinstance(m, int) else m_dram[bass.ds(m, 1)]
                        act.dma_start(dst.rearrange("o (t q) -> (o t) q", q=P), mt[:]).then_inc(m_stored, 16)
                    if n == R_AT:
                        for k in range(2):
                            act.wait_ge(m_in[k], m * (16 * PARTS) + 16 * PARTS)
                            act.wait_ge(row_split, m * 2 + k + 1)
                            act.activation(m_h[rows, k], m_row[rows, k], ACT.Copy).then_inc(mh_done, 1)
                    if n == R_AT + 4:
                        for k in range(2):
                            act.wait_ge(mr_done, m * 2 + k + 1)
                            act.activation(m_h[rows, k], m_r[rows, k], ACT.Copy).then_inc(mh2_done, 1)

                batches(act, values, coming)
                act.wait_ge(m_stored, 16 * (B + 1))
                for k in range(2):
                    act.wait_ge(stored[k], 16 * (B * GT // 2 + 1))

            @block.vector
            def _(v):
                v.memset(ks[rows], -1.0).then_inc(ready, 1)
                v.memset(qs[rows], 0.0).then_inc(ready, 1)
                v.memset(mp[:], MASK2).then_inc(ready, 1)
                for sem, credit in ((v_done, 1), (maxed, 2), (split, 4), (row_split, 2), (at_done, 2), (o1_done, 1),
                                    (o2_done, 2)):
                    v.sem_inc(sem, credit)
                v.wait_ge(w_in, NW)
                v.wait_ge(ready, READY)

                def values(b, n):
                    for G in range(GT):
                        if n == NORM[G]:
                            v.wait_ge(pv_mm, b * NI + first[G + 1] + NI)
                            v.tensor_scalar(den[:], po[32:48, G % 2, :], 1e-10, None, ALU.add).then_inc(den_done, 1)
                        for j in range(4):
                            if n == NORM[G] + j:
                                v.wait_ge(den_done, b * GT + G + 1)
                                sl = slice(j * P, (j + 1) * P)
                                v.reciprocal(rec[:, sl], den[:, sl]).then_inc(rec_done, 1)
                        if n == NORM[G] + AT:
                            v.wait_ge(rec_done, b * (4 * GT) + 4 * G + 4)
                            if G:
                                v.wait_ge(proj_mm, b * GT + G)
                            v.tensor_tensor(at[:], po[0:DV, G % 2, :], rec[:], ALU.mult).then_inc(at_done, 1)
                        if n == NORM[G] + RES:
                            v.wait_ge(proj_mm, b * GT + G + 1)
                            v.wait_ge(r_in[G % 2], b * (32 * GT // 2) + (G // 2) * 32 + 32)
                            v.wait_ge(o2_done, b * GT + G + 2)
                            v.scalar_tensor_tensor(o1[:], pm[:], b3[:, 0:1], cr[:, G % 2, :], ALU.add, ALU.add
                                                   ).then_inc(o1_done, 1)
                            v.wait_ge(o1_done, b * GT + G + 2)
                            v.wait_ge(stored[G % 2], b * (16 * GT // 2) + (G // 2) * 16 + 16)
                            v.tensor_tensor(o2[:, G % 2, :], o1[:], xr[:, G % 2, :], ALU.add).then_inc(o2_done, 1)

                def coming(m, n):
                    t = split_at(n)
                    if t is not None and t < GT:
                        v.wait_ge(h1_done, m * GT + t + 1)
                        v.scalar_tensor_tensor(r1[:, t % 2, :], h1[:, t % 2, :], sel[:, 0:1], qf[:, t % 2, :],
                                               ALU.mult, ALU.add).then_inc(r1_done, 1)
                    if t:
                        k = t - 1
                        v.wait_ge(h2_done, m * GT + t)
                        for dst, p0 in ((qs, 0), (ks, 64)):
                            v.scalar_tensor_tensor(dst[0:64, m, k * BANK:(k + 1) * BANK],
                                                   h2[p0:p0 + 64, k % 2, :], sel[p0:p0 + 64, 1:2],
                                                   r1[p0:p0 + 64, k % 2, :], ALU.mult, ALU.add).then_inc(split, 1)
                    if n == V_AT:
                        v.wait_ge(v_mm, m + 2)
                        v.tensor_tensor(va[:, m, :, 0:DV], pq[:].rearrange("p (t d) -> p t d", d=DV),
                                        bv[:].unsqueeze(1).broadcast_to((P, NT, DV)), ALU.add).then_inc(v_done, 1)
                    for u in units_at(n):
                        i, k = units[u]
                        v.wait_ge(unit_mm, m * NU + u + 1)
                        wid = (i % 4 + 1) * P if k == i // 4 else BANK
                        v.tensor_reduce(mp[:, i, k:k + 1], pu[:, u % 2, 0:wid], AX.X, ALU.max).then_inc(maxed, 1)
                    if n == M_AT:
                        v.wait_ge(maxed, m * NU + NU + 2)
                        v.wait_ge(mt_done, m + 1)
                        v.tensor_reduce(mall[:], mp[:], AX.X, ALU.max).then_inc(m_done, 1)
                    if n == R_AT + 2:
                        for k in range(2):
                            v.wait_ge(mh_done, m * 2 + k + 1)
                            v.scalar_tensor_tensor(m_r[rows, k], m_h[rows, k], sel[rows, 2:3], m_row[rows, k],
                                                   ALU.mult, ALU.add).then_inc(mr_done, 1)
                    if n == R_AT + 6:
                        for k in range(2):
                            v.wait_ge(mh2_done, m * 2 + k + 1)
                            v.scalar_tensor_tensor(qs[rows, m, k * MH:(k + 1) * MH], m_h[rows, k], sel[rows, 3:4],
                                                   m_r[rows, k], ALU.mult, ALU.add).then_inc(row_split, 1)

                batches(v, values, coming)


class Signal:

    def __init__(self, sem, per):
        self.sem, self.per = sem, per

    def credit(self, eng):
        eng.sem_inc(self.sem, self.per)

    def now(self, eng, it, k):
        eng.wait_ge(self.sem, it * self.per + (self.per + k))

    def before(self, eng, it, k):
        eng.wait_ge(self.sem, it * self.per + k)


def mamba_constants():
    r = np.arange(P)
    upto = (r[:, None] <= r[None, :]).astype(np.float32)
    after = (r[:, None] > r[None, :]).astype(np.float32)
    return {"c_tri": np.stack([upto, after, np.ones((P, P), np.float32)], 1),
            "c_pick": np.tile(np.eye(2 * B * NH, dtype=np.float32), (2, 1)),
            "c_flip": np.ascontiguousarray(np.eye(P, dtype=np.float32)[::-1]),
            "c_causal": np.tile(np.where(r[:, None] > r[None, :], MASK1, 0.0).astype(np.float32), (1, NH))}


def mamba(nc, sems, g, hn, outs):
    s = Scope(nc, sems, "mb")
    with s.stack:
        step = {n: s.sb(n, [P, 2, NCH, B * NH]) for n in ("dt", "nacs", "eacs", "dtdec", "etot")}
        step["rows"] = s.sb("rows", [4 * B * NH, T], F32R)
        mamba_steps(nc, sems, g, hn, step)
        mamba_scan(nc, sems, g, hn, step, outs)


def mamba_steps(nc, sems, g, hn, st):
    s = Scope(nc, sems, "ms")
    W = NCH * B * NH
    with s.stack:
        wdt = s.sb("wdt", [P, 2 * NH])
        bias = s.sb("bias", [P, 2, NH])
        alog = s.sb("alog", [P, 2, NH])
        aneg = s.sb("aneg", [P, 2, NH])
        tri = s.sb("tri", [P, 3, P])
        flip = s.sb("flip", [P, P])
        h = s.sb("h", [P, 2, T])
        raw = s.sb("raw", [P, 2, NCH, B, NH])
        x = s.sb("x", [P, 2, W])
        ax = s.sb("ax", [P, 2, W])
        ex = s.sb("ex", [P, 2, W])
        lg = s.sb("lg", [P, 2, W])
        dec = s.sb("dec", [P, 2, W])
        da = s.sb("da", [P, NCH, 2, B * NH])
        NR = 2 * B * NH
        pd = s.ps("pd", [P, 2, BANK])
        pf = s.ps("pf", [P, BANK])
        pc = s.ps("pc", [P, 5, BANK])
        w_in, dt_mm, gathered, flip_mm, step, exp_done, sum_mm, sum_exp, dec_done, row_mm, row_high, row_low = (
            s.sem(n) for n in ("w_in", "dt_mm", "gathered", "flip_mm", "step", "exp_done", "sum_mm", "sum_exp",
                               "dec_done", "row_mm", "row_high", "row_low"))
        h_in = [s.sem(f"h_in{k}") for k in range(2)]
        hv = hn.rearrange("p (b n) -> p b n", b=B)
        with nc.Block() as block:

            @block.sync
            def _(sp):
                for dst, name in ((wdt, "Wdt"), (bias, "dt_bias"), (alog, "A_log"), (tri, "c_tri"), (flip, "c_flip")):
                    sp.dma_start(dst[:], g[name]).then_inc(w_in, 16)
                with sp.Fori(0, B // 2) as i:
                    for k in range(2):
                        sp.wait_ge(dt_mm, i * 2 + k + 1)
                        sp.dma_start(h[:, k], hv[:, i * 2 + k, :]).then_inc(h_in[k], 16)

            @block.tensor
            def _(pe):
                pe.sem_inc(dt_mm, 2)
                pe.wait_ge(w_in, 80)
                with pe.Fori(0, B // 2) as i:
                    for k in range(2):
                        pe.wait_ge(h_in[k], i * 16 + 16)
                        pe.wait_ge(gathered, i * 2 + k + 1)
                        for c in range(NCH):
                            mm = pe.matmul(pd[:, k, c * 2 * NH:(c + 1) * 2 * NH], h[:, k, c * P:(c + 1) * P], wdt[:],
                                           start=True, stop=True, skip_group_check=True)
                        mm.then_inc(dt_mm, 1)
                pe.wait_ge(gathered, B + 2)
                pe.matmul(pf[:], flip[:], raw[:, 1].rearrange("p c b h -> p (c b h)"), start=True, stop=True
                          ).then_inc(flip_mm, 1)
                pe.wait_ge(dec_done, 1)
                for d in range(2):
                    for k in range(3):
                        n = 3 * d + k
                        if n == 5:
                            pe.wait_ge(sum_exp, 2)
                        pe.matmul(pc[:, n % 5, :], tri[:, k, :], da[:, :, d, :], start=True, stop=True
                                  ).then_inc(sum_mm, 1)
                for r in range(NCH // 4):
                    if r >= 2:
                        pe.wait_ge(row_low, r - 1)
                    for c in range(4):
                        mm = pe.matmul(pd[0:NR, r % 2, c * CH:(c + 1) * CH],
                                       da[:, 4 * r + c].rearrange("p d n -> p (d n)"), tri[:, 0, :], start=True,
                                       stop=True, skip_group_check=True)
                    mm.then_inc(row_mm, 1)

            @block.scalar
            def _(act):
                act.wait_ge(step, 3)
                act.activation(ex[:].rearrange("p d n -> p (d n)"), ax[:].rearrange("p d n -> p (d n)"), ACT.Exp,
                               scale=-1.0).then_inc(exp_done, 1)
                act.wait_ge(w_in, 80)
                act.activation(aneg[:].rearrange("p d n -> p (d n)"), alog[:].rearrange("p d n -> p (d n)"), ACT.Exp
                               ).then_inc(exp_done, 1)
                act.wait_ge(exp_done, 2)
                act.activation(lg[:].rearrange("p d n -> p (d n)"), ex[:].rearrange("p d n -> p (d n)"), ACT.Ln,
                               bias=1.0).then_inc(exp_done, 1)
                for d in range(2):
                    for k in range(3):
                        n = 3 * d + k
                        act.wait_ge(sum_mm, n + 1)
                        if k == 0:
                            act.activation(st["nacs"][:, d].rearrange("p c n -> p (c n)"), pc[:, n % 5, :], ACT.Copy,
                                           scale=-1.0).then_inc(sum_exp, 1)
                        dst = (st["eacs"][:, d].rearrange("p c n -> p (c n)"), dec[:, d, :],
                               st["etot"][:, d].rearrange("p c n -> p (c n)"))[k]
                        act.activation(dst, pc[:, n % 5, :], ACT.Exp).then_inc(sum_exp, 1)
                for r in range(NCH // 4):
                    act.wait_ge(row_mm, r + 1)
                    act.activation(st["rows"][0:NR, r * BANK:(r + 1) * BANK], pd[0:NR, r % 2, :], ACT.Copy
                                   ).then_inc(row_high, 1)

            @block.vector
            def _(v):
                v.sem_inc(gathered, 2)
                with v.Fori(0, B // 2) as i:
                    for k in range(2):
                        v.wait_ge(dt_mm, i * 2 + k + 3)
                        v.tensor_copy(raw[:, :, :, i * 2 + k, :],
                                      pd[:, k, 0:2 * NH * NCH].rearrange("p (c d h) -> p d c h", d=2, h=NH)
                                      ).then_inc(gathered, 1)
                v.wait_ge(w_in, 80)
                v.wait_ge(gathered, B + 2)
                v.tensor_tensor(x[:, 0].rearrange("p (n h) -> p n h", h=NH),
                                raw[:, 0].rearrange("p c b h -> p (c b) h"),
                                bias[:, 0].unsqueeze(1).broadcast_to((P, NCH * B, NH)), ALU.add).then_inc(step, 1)
                v.wait_ge(flip_mm, 1)
                v.tensor_tensor(x[:, 1].rearrange("p (c b h) -> p c b h", b=B, h=NH),
                                pf[:].rearrange("p (c b h) -> p c b h", b=B, h=NH)[:, ::-1],
                                bias[:, 1].unsqueeze(1).unsqueeze(1).broadcast_to((P, NCH, B, NH)), ALU.add
                                ).then_inc(step, 1)
                v.wait_ge(step, 2)
                v.scalar_tensor_tensor(ax[:], x[:], -1.0, x[:], ALU.mult, ALU.max).then_inc(step, 1)
                v.wait_ge(exp_done, 3)
                dtf = st["dt"][:].rearrange("p d c n -> p d (c n)")
                v.scalar_tensor_tensor(dtf, x[:], 0.0, lg[:], ALU.max, ALU.add).then_inc(step, 1)
                v.wait_ge(step, 4)
                for d in range(2):
                    for b in range(B):
                        hs = slice(b * NH, (b + 1) * NH)
                        v.scalar_tensor_tensor(da[:, :, d, hs], st["dt"][:, d, :, hs], -1.0,
                                               aneg[:, d].unsqueeze(1).broadcast_to((P, NCH, NH)),
                                               ALU.mult, ALU.mult).then_inc(step, 1)
                v.wait_ge(step, 4 + 2 * B)
                v.sem_inc(dec_done, 1)
                for r in range(NCH // 4):
                    v.wait_ge(row_high, r + 1)
                    sl = slice(r * BANK, (r + 1) * BANK)
                    low_part(v, st["rows"][NR:2 * NR, sl], pd[0:NR, r % 2, :], st["rows"][0:NR, sl]
                             ).then_inc(row_low, 1)
                v.wait_ge(sum_exp, 8)
                v.tensor_tensor(st["dtdec"][:].rearrange("p d c n -> p d (c n)"), dtf, dec[:], ALU.mult
                                ).then_inc(step, 1)


def mamba_scan(nc, sems, g, hn, st, outs):
    s = Scope(nc, sems, "mm")
    XB = 3
    H2 = B // 2
    PER = dict(xin=16, xc=1, halo=1, proj=3, evac=6, zmm=2, thz=2, zs=2, lmm=4, lexp=16, taps=9, th=3, silu=4,
               gmm=1, w=4, xtmm=2, btmm=1, bt=1, xd=4, yomm=2, ydmm=2, y=2, yadd=2, gate=2, stmm=2, stmp=1,
               st=2, sq=4, rs1=1, rs=1, yn=4, ytmm=2, yta=1, ytv=1, omm=1, ob=1, stored=16)
    FROM = dict(scalar="evac thz lexp th bt sq yn yta ob stored", vector="taps zs silu w xd y yadd st ytv",
                tensor="proj zmm lmm gmm xtmm btmm yomm ydmm stmm ytmm omm", gpsimd="xc halo gate stmp rs1 rs",
                sync="xin")
    with s.stack:
        identb = s.sb("identb", [P, P], BF16)
        ident = s.sb("ident", [P, P])
        cm = s.sb("cm", [P, NH * P])
        cmb = s.sb("cmb", [P, NH * P], BF16)
        pick_in = s.sb("pick_in", [4 * B * NH, 2 * B * NH])
        pick = s.sb("pick", [4 * B * NH, 2 * B * NH], F32R)
        nhalf = s.sb("nhalf", [P, B])
        D = []
        for d in range(2):
            t = {n: s.sb(f"{n}{d}", shape) for n, shape in (
                ("wi", [P, 2 * DI + 2 * DS]), ("cw", [P, XB, TAPS]), ("cb", [P, XB]), ("dcol", [P, 2]),
                ("nw", [P, 2]), ("dg", [P, 2, P]), ("wo", [P, 2, P]),
                ("xin", [P, B, CH]), ("xc", [P, B, CH]), ("raw", [P, XB, B, CH + TAPS - 1]),
                ("acc", [P, XB, B, CH]), ("th", [P, XB, B, CH]), ("xs", [P, 2, B, CH]), ("bs", [DS, B, CH]),
                ("cs", [DS, B, CH]), ("L", [P, B, NH, CH]), ("xdt", [P, B, NH, HD]), ("xdd", [P, B, NH, HD]),
                ("bt", [P, B, DS]), ("state", [DS, B, DI]), ("stmp", [DS, B, DI]), ("zs", [P, B, DI]),
                ("y", [P, B, DI]), ("yn", [P, B, DI]), ("yt", [P, 2, B, CH]), ("ob", [P, B, CH]),
                ("ssq", [P, B]), ("rs", [P, B]))}
            for n in "ABCD":
                t[n] = s.ps(f"{n}{d}", [P, BANK])
            t["sig"] = {n: Signal(s.sem(f"{n}{d}"), per) for n, per in PER.items()}
            D.append(t)
        w_in, ready, passed_sp, passed_pool, passed_pe = (
            s.sem(n) for n in ("w_in", "ready", "passed_sp", "passed_pool", "passed_pe"))
        hv = hn.rearrange("p (b c n) -> p b c n", b=B, n=CH)
        ov = [o.rearrange("p (b c n) -> p b c n", b=B, n=CH) for o in outs]
        DMAS = 3 + 2 * 6
        READY = 4 + 2 * 9

        def credits(eng, name):
            for t in D:
                for n in FROM[name].split():
                    t["sig"][n].credit(eng)

        def run(stage, at, *more):
            it, d = at
            stage(it, d, D[d], D[d]["sig"], *more)

        def halves(eng, half):
            half(None, None, (0, 0))
            half((0, 0), None, (0, 1))
            with eng.Fori(0, NCH - 1) as it:
                half((it, 1), (it, 0), (it + 1, 0))
                half((it + 1, 0), (it, 1), (it + 1, 1))
            half((NCH - 1, 1), (NCH - 1, 0), None)
            half(None, (NCH - 1, 1), None)

        def chunk(it, d):
            return it if d == 0 else (NCH - 1) - it

        with nc.Block() as block:

            @block.sync
            def _(sp):
                sp.dma_start(ident[:], g["c_ident"]).then_inc(w_in, 16)
                sp.dma_start(cm[:], g["c_causal"]).then_inc(w_in, 16)
                sp.dma_start(pick_in[:], g["c_pick"]).then_inc(w_in, 16)
                for d, t in enumerate(D):
                    for n, name in (("wi", "in_proj"), ("cw", "conv_w"), ("cb", "conv_b"), ("dcol", "D"), ("nw", "norm_w"),
                                    ("wo", "out_proj")):
                        sp.dma_start(t[n][:], g[f"{name}{d}"]).then_inc(w_in, 16)
                credits(sp, "sync")
                with sp.Fori(0, NCH) as it:
                    for d, t in enumerate(D):
                        t["sig"]["xc"].before(sp, it, 1)
                        hold(sp, passed_sp)
                        sp.dma_start(t["xin"][:], hv[:, :, chunk(it, d), :]).then_inc(t["sig"]["xin"].sem, 16)

            @block.gpsimd
            def _(pool):
                pool.wait_ge(w_in, 16 * DMAS)
                pool.tensor_copy(identb[:], ident[:]).then_inc(ready, 1)
                pool.tensor_copy(cmb[:], cm[:]).then_inc(ready, 1)
                pool.memset(nhalf[:], -0.5).then_inc(ready, 1)
                pool.tensor_copy(pick[:], pick_in[:]).then_inc(ready, 1)
                for t in D:
                    pool.memset(t["raw"][:], 0.0).then_inc(ready, 1)
                    pool.memset(t["state"][:], 0.0).then_inc(ready, 1)
                    for k in range(2):
                        pool.tensor_scalar(t["dg"][:, k, :], ident[:], t["dcol"][:, k:k + 1], None, ALU.mult
                                           ).then_inc(ready, 1)
                        pool.tensor_scalar(t["wo"][:, k, :], t["wo"][:, k, :], t["nw"][:, k:k + 1], None, ALU.mult
                                           ).then_inc(ready, 1)
                    pool.tensor_scalar(t["wi"][:, 0:DI], t["wi"][:, 0:DI], 0.5, None, ALU.mult).then_inc(ready, 1)
                    pool.tensor_scalar(t["cw"][:], t["cw"][:], 0.5, None, ALU.mult).then_inc(ready, 1)
                    pool.tensor_scalar(t["cb"][:], t["cb"][:], 0.5, None, ALU.mult).then_inc(ready, 1)
                credits(pool, "gpsimd")
                pool.wait_ge(ready, READY)

                def copy_in(it, d, t, S):
                    S["xin"].now(pool, it, 16)
                    S["zmm"].before(pool, it, 2)
                    hold(pool, passed_pool)
                    pool.tensor_copy(t["xc"][:], t["xin"][:] if d == 0 else t["xin"][:, :, ::-1]
                                     ).then_inc(S["xc"].sem, 1)

                def halo(it, d, t, S):
                    S["taps"].now(pool, it, 9)
                    hold(pool, passed_pool)
                    pool.tensor_copy(t["raw"][:, :, :, 0:TAPS - 1].rearrange("p x b n -> p (x b) n"),
                                     t["raw"][:, :, :, CH:CH + TAPS - 1].rearrange("p x b n -> p (x b) n")
                                     ).then_inc(S["halo"].sem, 1)

                def decayed_state(it, d, t, S):
                    S["st"].before(pool, it, 2)
                    pool.tensor_tensor(t["stmp"][:].rearrange("p b (h e) -> p (b h) e", h=NH),
                                       t["state"][:].rearrange("p b (h e) -> p (b h) e", h=NH),
                                       st["etot"][0:DS, d, it, :].unsqueeze(2).broadcast_to((DS, B * NH, HD)),
                                       ALU.mult).then_inc(S["stmp"].sem, 1)

                def gates(it, d, t, S):
                    for k in range(2):
                        S["yadd"].now(pool, it, k + 1)
                        S["zs"].now(pool, it, k + 1)
                        sl = slice(k * H2, (k + 1) * H2)
                        pool.tensor_tensor(t["y"][:, sl], t["y"][:, sl], t["zs"][:, sl], ALU.mult
                                           ).then_inc(S["gate"].sem, 1)

                def norms(it, d, t, S):
                    S["sq"].now(pool, it, 4)
                    hold(pool, passed_pool)
                    pool.tensor_scalar(t["rs"][:], t["ssq"][:], 1.0 / DI, 1e-5, ALU.mult, ALU.add
                                       ).then_inc(S["rs1"].sem, 1)
                    S["rs1"].now(pool, it, 1)
                    pool.tensor_tensor(t["rs"][:], t["rs"][:], nhalf[:], ALU.pow).then_inc(S["rs"].sem, 1)

                def half(front, back, coming):
                    if coming:
                        run(copy_in, coming)
                    if back:
                        run(decayed_state, back)
                        run(gates, back)
                        run(norms, back)
                    if front:
                        run(halo, front)

                halves(pool, half)

            @block.tensor
            def _(pe):
                credits(pe, "tensor")
                pe.wait_ge(w_in, 16 * DMAS)
                pe.wait_ge(ready, READY)

                def flat(ap):
                    return ap.rearrange("p b n -> p (b n)")

                def project(it, d, t, S, tiles):
                    S["xc"].now(pe, it, 1)
                    for k in tiles:
                        free, cnt = (("st", 1), ("st", 2), ("yta", 1))[k]
                        S[free].before(pe, it, cnt)
                        pe.matmul(t["BAC"[k]][:], t["wi"][:, DI + k * P:DI + (k + 1) * P], flat(t["xc"][:]), start=True,
                                  stop=True).then_inc(S["proj"].sem, 1)

                def gate(it, d, t, S, k):
                    if k == 0:
                        S["ob"].before(pe, it, 1)
                    else:
                        S["zs"].now(pe, it, 1)
                    for j in range(2):
                        mm = pe.matmul(t["D"][:, j * DI:(j + 1) * DI], t["xc"][:, 2 * k + j, :], t["wi"][:, 0:DI],
                                       start=True, stop=True, skip_group_check=True)
                    mm.then_inc(S["zmm"].sem, 1)

                def decay(it, d, t, S, b):
                    if b < 2:
                        S["evac"].now(pe, it, (2, 4)[b])
                    else:
                        S["lexp"].now(pe, it, NH * (b - 1))
                    bank = t["BA"[b % 2]]
                    pe.matmul(bank[:], identb[:], cmb[:], start=True, stop=False, skip_group_check=True)
                    for h in range(NH):
                        n = b * NH + h
                        n += d * B * NH
                        mm = pe.matmul(bank[:, h * P:(h + 1) * P], pick[:, n:n + 1].broadcast_to((4 * B * NH, P)),
                                       st["rows"][:, bass.ds(it * CH, CH)] if not isinstance(it, int) else
                                       st["rows"][:, it * CH:(it + 1) * CH], start=False, stop=(h == NH - 1), skip_group_check=True)
                    mm.then_inc(S["lmm"].sem, 1)

                def b_times_c(it, d, t, S):
                    S["silu"].now(pe, it, 4)
                    S["evac"].now(pe, it, 6)
                    for b in range(B):
                        mm = pe.matmul(t["C"][:, b * P:(b + 1) * P], t["bs"][:, b, :], t["cs"][:, b, :], start=True,
                                       stop=True, skip_group_check=True)
                    mm.then_inc(S["gmm"].sem, 1)

                def turn_b(it, d, t, S):
                    S["silu"].now(pe, it, 3)
                    S["zs"].now(pe, it, 2)
                    hold(pe, passed_pe)
                    for b in range(B):
                        mm = pe.transpose(t["D"][:, b * DS:(b + 1) * DS], t["bs"][:, b, :], ident[0:DS, 0:DS])
                    mm.then_inc(S["btmm"].sem, 1)

                def turn_x(it, d, t, S, k):
                    S["silu"].now(pe, it, 2)
                    S["lexp"].now(pe, it, 12 + 4 * k)
                    for j in range(2):
                        for x in range(2):
                            mm = pe.transpose(t["BA"[k]][:, (2 * j + x) * P:(2 * j + x + 1) * P],
                                              t["xs"][:, x, 2 * k + j, :], ident[:])
                    mm.then_inc(S["xtmm"].sem, 1)

                def from_state(it, d, t, S, k):
                    S["st"].before(pe, it, 2)
                    S["xd"].now(pe, it, 2 * k + 2)
                    for j in range(2):
                        mm = pe.matmul(t["BA"[k]][:, j * DI:(j + 1) * DI], t["cs"][:, 2 * k + j, :],
                                       t["state"][:, 2 * k + j, :], start=True, stop=True, skip_group_check=True)
                    mm.then_inc(S["yomm"].sem, 1)

                def from_chunk(it, d, t, S, k):
                    S["w"].now(pe, it, 4)
                    if k == 1:
                        S["bt"].now(pe, it, 1)
                    bank = t["CD"[k]]
                    for j in range(2):
                        b = 2 * k + j
                        for x in range(2):
                            o = j * DI + x * P
                            pe.matmul(bank[:, o:o + P], t["xs"][:, x, b, :], t["dg"][:, x, :], start=(x == 0),
                                      stop=False, skip_group_check=True)
                        for h in range(NH):
                            o = j * DI + h * HD
                            mm = pe.matmul(bank[:, o:o + HD], t["L"][:, b, h, :], t["xdt"][:, b, h, :],
                                           start=False, stop=(h == NH - 1), skip_group_check=True)
                    mm.then_inc(S["ydmm"].sem, 1)

                def states(it, d, t, S, k):
                    S["y"].now(pe, it, k + 1)
                    for j in range(2):
                        b = 2 * k + j
                        mm = pe.matmul(t["BA"[k]][0:DS, j * DI:(j + 1) * DI], t["bt"][:, b, :],
                                       t["xdd"][:, b].rearrange("p h e -> p (h e)"), start=True, stop=True,
                                       skip_group_check=True)
                    mm.then_inc(S["stmm"].sem, 1)

                def turn_back(it, d, t, S, x):
                    S["yn"].now(pe, it, 4)
                    S["yadd"].now(pe, it, x + 1)
                    for b in range(B):
                        mm = pe.transpose(t["CD"[x]][:, b * P:(b + 1) * P], t["yn"][:, b, x * P:(x + 1) * P],
                                          ident[:])
                    mm.then_inc(S["ytmm"].sem, 1)

                def project_out(it, d, t, S):
                    S["yta"].now(pe, it, 1)
                    S["ytv"].now(pe, it, 1)
                    for x in range(2):
                        mm = pe.matmul(t["D"][:], t["wo"][:, x, :], flat(t["yt"][:, x]), start=(x == 0), stop=(x == 1))
                    mm.then_inc(S["omm"].sem, 1)

                def half(front, back, coming):
                    if back:
                        run(from_state, back, 0)
                        run(from_state, back, 1)
                    if front:
                        run(gate, front, 0)
                    if back:
                        run(from_chunk, back, 0)
                        run(from_chunk, back, 1)
                    if front:
                        run(decay, front, 0)
                        run(decay, front, 1)
                    if back:
                        run(states, back, 0)
                        run(states, back, 1)
                    if front:
                        run(gate, front, 1)
                        run(decay, front, 2)
                    if coming:
                        run(project, coming, (0, 1))
                    if front:
                        run(decay, front, 3)
                        run(turn_x, front, 0)
                        run(turn_x, front, 1)
                        run(b_times_c, front)
                        run(turn_b, front)
                    if back:
                        run(turn_back, back, 0)
                        run(turn_back, back, 1)
                    if coming:
                        run(project, coming, (2,))
                    if back:
                        run(project_out, back)

                halves(pe, half)

            @block.scalar
            def _(act):
                credits(act, "scalar")
                act.wait_ge(w_in, 16 * DMAS)
                act.wait_ge(ready, READY)

                def flat(ap):
                    return ap.rearrange("p b n -> p (b n)")

                def raws(it, d, t, S, tiles):
                    S["halo"].before(act, it, 1)
                    S["silu"].before(act, it, 4)
                    for k in tiles:
                        S["proj"].now(act, it, k + 1)
                        pj = t["BAC"[k]][:].rearrange("p (b n) -> p b n", b=B)
                        act.activation(t["raw"][:, k, :, TAPS - 1:], pj, ACT.Copy).then_inc(S["evac"].sem, 1)
                        act.activation(t["acc"][:, k], pj, ACT.Identity, bias=t["cb"][:, k:k + 1],
                                       scale=t["cw"][:, k, TAPS - 1:TAPS]).then_inc(S["evac"].sem, 1)

                def z_tanh(it, d, t, S, k):
                    S["zmm"].now(act, it, k + 1)
                    S["gate"].before(act, it, 2)
                    act.activation(flat(t["zs"][:, k * H2:(k + 1) * H2]), t["D"][:], ACT.Tanh).then_inc(S["thz"].sem, 1)

                def decays(it, d, t, S, b):
                    S["lmm"].now(act, it, b + 1)
                    S["ydmm"].before(act, it, 2)
                    for h in range(NH):
                        n = b * NH + h
                        act.activation(t["L"][:, b, h, :], t["BA"[b % 2]][:, h * P:(h + 1) * P], ACT.Exp,
                                       bias=st["nacs"][:, d, it, n:n + 1]).then_inc(S["lexp"].sem, 1)

                def tanhs(it, d, t, S, k):
                    S["taps"].now(act, it, (5, 6, 9)[k])
                    act.activation(t["th"][:, k], t["acc"][:, k], ACT.Tanh).then_inc(S["th"].sem, 1)

                def b_tokens(it, d, t, S):
                    S["btmm"].now(act, it, 1)
                    S["stmm"].before(act, it, 2)
                    act.activation(flat(t["bt"][:]), t["D"][:, 0:B * DS], ACT.Copy).then_inc(S["bt"].sem, 1)

                def squares(it, d, t, S, k):
                    S["ytmm"].before(act, it, 2)
                    S["gate"].now(act, it, k + 1)
                    for b in range(k * H2, (k + 1) * H2):
                        act.activation(t["yn"][:, b, :], t["y"][:, b, :], ACT.Square, accum_out=t["ssq"][:, b:b + 1]
                                       ).then_inc(S["sq"].sem, 1)

                def norms(it, d, t, S):
                    S["rs"].now(act, it, 1)
                    for b in range(B):
                        act.activation(t["yn"][:, b, :], t["y"][:, b, :], ACT.Copy, scale=t["rs"][:, b:b + 1]
                                       ).then_inc(S["yn"].sem, 1)

                def turned(it, d, t, S):
                    S["ytmm"].now(act, it, 1)
                    S["omm"].before(act, it, 1)
                    act.activation(flat(t["yt"][:, 0]), t["C"][:], ACT.Copy).then_inc(S["yta"].sem, 1)

                def result(it, d, t, S):
                    S["omm"].now(act, it, 1)
                    S["stored"].before(act, it, 16)
                    dst = t["ob"][:] if d == 0 else t["ob"][:, :, ::-1]
                    act.activation(dst, t["D"][:].rearrange("p (b n) -> p b n", b=B), ACT.Copy).then_inc(S["ob"].sem, 1)
                    S["ob"].now(act, it, 1)
                    act.dma_start(ov[d][:, :, chunk(it, d), :], t["ob"][:]).then_inc(S["stored"].sem, 16)

                def half(front, back, coming):
                    if front:
                        run(z_tanh, front, 0)
                        run(tanhs, front, 0)
                        run(tanhs, front, 1)
                        run(tanhs, front, 2)
                        run(decays, front, 0)
                        run(decays, front, 1)
                    if back:
                        run(squares, back, 0)
                    if front:
                        run(z_tanh, front, 1)
                    if back:
                        run(squares, back, 1)
                    if front:
                        run(decays, front, 2)
                    if coming:
                        run(raws, coming, (0, 1))
                    if front:
                        run(decays, front, 3)
                    if back:
                        run(norms, back)
                    if front:
                        run(b_tokens, front)
                    if back:
                        run(turned, back)
                    if coming:
                        run(raws, coming, (2,))
                    if back:
                        run(result, back)

                halves(act, half)
                for t in D:
                    act.wait_ge(t["sig"]["stored"].sem, 16 * (NCH + 1))

            @block.vector
            def _(v):
                credits(v, "vector")
                v.wait_ge(w_in, 16 * DMAS)
                v.wait_ge(ready, READY)

                def taps(it, d, t, S, tiles):
                    for i in range(TAPS - 1):
                        for n, k in enumerate(tiles):
                            S["evac"].now(v, it, 2 * k + 2)
                            if i:
                                S["taps"].now(v, it, 3 * tiles[0] + (i - 1) * len(tiles) + n + 1)
                            v.scalar_tensor_tensor(t["acc"][:, k], t["raw"][:, k, :, i:i + CH], t["cw"][:, k, i:i + 1],
                                                   t["acc"][:, k], ALU.mult, ALU.add).then_inc(S["taps"].sem, 1)

                def z_silu(it, d, t, S, k):
                    S["thz"].now(v, it, k + 1)
                    zf = t["zs"][:, k * H2:(k + 1) * H2].rearrange("p b n -> p (b n)")
                    v.scalar_tensor_tensor(zf, zf, 1.0, t["D"][:], ALU.add, ALU.mult).then_inc(S["zs"].sem, 1)

                def silus(it, d, t, S, n):
                    S["ydmm"].before(v, it, 2)
                    S["stmm"].before(v, it, 2)
                    dst, k, p0, p1 = ((t["xs"][:, 0], 0, 0, P), (t["xs"][:, 1], 1, 0, P), (t["bs"][:], 2, 0, DS),
                                      (t["cs"][:], 2, DS, 2 * DS))[n]
                    S["th"].now(v, it, k + 1)
                    v.scalar_tensor_tensor(dst, t["th"][p0:p1, k], 1.0, t["acc"][p0:p1, k], ALU.add, ALU.mult
                                           ).then_inc(S["silu"].sem, 1)

                def weights(it, d, t, S, b):
                    S["gmm"].now(v, it, 1)
                    S["lexp"].now(v, it, NH * (b + 1))
                    v.tensor_tensor(t["L"][:, b], t["L"][:, b],
                                    t["C"][:, b * P:(b + 1) * P].unsqueeze(1).broadcast_to((P, NH, P)), ALU.mult
                                    ).then_inc(S["w"].sem, 1)

                def spread(ap, it, d, k):
                    return ap[:, d, it, k * H2 * NH:(k + 1) * H2 * NH].unsqueeze(2).broadcast_to((P, H2 * NH, HD))

                def heads(ap):
                    return ap.rearrange("p (n e) -> p n e", e=HD)

                def steps(it, d, t, S, k):
                    S["xtmm"].now(v, it, k + 1)
                    for n, f in (("xdt", "dt"), ("xdd", "dtdec")):
                        v.tensor_tensor(t[n][:, k * H2:(k + 1) * H2].rearrange("p b h e -> p (b h) e"),
                                        heads(t["BA"[k]][:]), spread(st[f], it, d, k), ALU.mult
                                        ).then_inc(S["xd"].sem, 1)

                def decayed(it, d, t, S, k):
                    S["yn"].before(v, it, 4)
                    S["yomm"].now(v, it, k + 1)
                    v.tensor_tensor(t["y"][:, k * H2:(k + 1) * H2].rearrange("p b (h e) -> p (b h) e", e=HD),
                                    heads(t["BA"[k]][:]), spread(st["eacs"], it, d, k), ALU.mult
                                    ).then_inc(S["y"].sem, 1)

                def add_chunk(it, d, t, S, k):
                    S["ydmm"].now(v, it, k + 1)
                    S["y"].now(v, it, k + 1)
                    yf = t["y"][:, k * H2:(k + 1) * H2].rearrange("p b n -> p (b n)")
                    v.tensor_tensor(yf, yf, t["CD"[k]][:], ALU.add).then_inc(S["yadd"].sem, 1)

                def states(it, d, t, S, k):
                    S["stmp"].now(v, it, 1)
                    S["yomm"].now(v, it, 2)
                    S["stmm"].now(v, it, k + 1)
                    sl = slice(k * H2, (k + 1) * H2)
                    v.tensor_tensor(t["state"][:, sl].rearrange("p b n -> p (b n)"),
                                    t["stmp"][:, sl].rearrange("p b n -> p (b n)"), t["BA"[k]][0:DS, :], ALU.add
                                    ).then_inc(S["st"].sem, 1)

                def turned(it, d, t, S):
                    S["ytmm"].now(v, it, 2)
                    S["omm"].before(v, it, 1)
                    v.tensor_copy(t["yt"][:, 1].rearrange("p b n -> p (b n)"), t["D"][:]).then_inc(S["ytv"].sem, 1)

                def half(front, back, coming):
                    if front:
                        run(taps, front, (2,))
                    if back:
                        run(decayed, back, 0)
                    if front:
                        run(z_silu, front, 0)
                    if back:
                        run(decayed, back, 1)
                        run(add_chunk, back, 0)
                        run(add_chunk, back, 1)
                        run(states, back, 0)
                    if front:
                        run(z_silu, front, 1)
                    if back:
                        run(states, back, 1)
                    if front:
                        run(silus, front, 0)
                        run(silus, front, 1)
                        run(silus, front, 2)
                        run(silus, front, 3)
                    if coming:
                        run(taps, coming, (0, 1))
                    if front:
                        run(steps, front, 0)
                    if back:
                        run(turned, back)
                    if front:
                        run(steps, front, 1)
                        run(weights, front, 0)
                        run(weights, front, 1)
                        run(weights, front, 2)
                        run(weights, front, 3)

                halves(v, half)


def stu_constants():
    a = np.arange(NB)
    ang = 2 * np.pi * np.outer(a, np.arange(NB)) / NF
    re, im = np.cos(ang), -np.sin(ang)
    alt = (-1.0) ** a
    fwd = np.stack([re, im], 1)
    fwd[:, 1, 0] = alt
    dft_u = np.zeros((2, B, NB, 2, 2, NB))
    for b in range(B):
        dft_u[b // 2, b, :, :, b % 2, :] = fwd
    blk = np.zeros((NB, 2, NB, 2))
    blk[:, 0, :, 0], blk[:, 1, :, 0], blk[:, 0, :, 1], blk[:, 1, :, 1] = re, im, -im, re
    blk[:, 1, 0, 0] = blk[:, 0, 0, 1] = 0
    blk[:, 1, 0, 1] = alt
    inv = np.stack([2 * re, 2 * im], 2).transpose(2, 1, 0) / NF
    inv[0, 0], inv[1, 0] = 1 / NF, alt / NF
    f = lambda m, *shape: np.ascontiguousarray(m.reshape(shape), np.float32)
    return {"c_dft_u": f(dft_u, 2, P, P), "c_dft_phi": f(blk, NB, P), "c_idft": f(inv, 2 * NB, NB)}


def spectral(nc, sems, g, hn, t1, out):
    s0 = Scope(nc, sems, "stu")
    u_hat = nc.dram_tensor("u_hat", (2, NB, 2, B, 2, P, HALF), F32, kind="Internal").ap()
    g_hat = nc.dram_tensor("g_hat", (2, NB, 2, K, 2, BL, 2), F32, kind="Internal").ap()
    y_hat = nc.dram_tensor("y_hat", (2, B, NB, HALF, 2, P), F32, kind="Internal").ap()
    with s0.stack:
        me = s0.sb("me", [P, 2, 2, K, P], F32R)
        mu = s0.sb("mu", [P, 3, P])
        seg = s0.sb("seg", [P, 4])
        stu_matrices(nc, sems, g, me, mu, seg)
        stu_transforms(nc, sems, g, hn, u_hat, g_hat)
        stu_convolve(nc, sems, me, u_hat, g_hat, y_hat)
        stu_finish(nc, sems, g, mu, seg, y_hat, hn, t1, out)


def stu_matrices(nc, sems, g, me, mu, seg):
    s = Scope(nc, sems, "mat")
    with s.stack:
        lw = s.sb("lw", [P, 4])
        gum = s.sb("gum", [P, 4])
        sig = s.sb("sig", [P, K])
        quarter = s.sb("quarter", [P, K])
        sk = s.sb("sk", [P, K])
        z = s.sb("z", [P, 4])
        e = s.sb("e", [P, 4])
        soft = s.sb("soft", [P, 4])
        eq = s.sb("eq", [P, 4])
        hard = s.sb("hard", [P, 4])
        left = s.sb("left", [P, 4])
        w = s.sb("w", [P, 4])
        one = s.sb("one", [P, 4])
        raw = s.sb("raw", [P, 2, 4, K * P])
        rmu = s.sb("rmu", [P, 4, 3 * P])
        acc = s.sb("acc", [P, 2, K * P])
        small_in, big_in, mu_in, z_done, e_done, step, pow_done = (
            s.sem(n) for n in ("small_in", "big_in", "mu_in", "z_done", "e_done", "step", "pow_done"))
        with nc.Block() as block:

            @block.sync
            def _(sp):
                sp.dma_start(lw[:], g["log_weights"]).then_inc(small_in, 16)
                sp.dma_start(gum[:], g["gumbel"]).then_inc(small_in, 16)
                sp.dma_start(sig[:], g["sigma"]).then_inc(small_in, 16)
                for i in range(4):
                    for m, name in enumerate(("M_phi_plus", "M_phi_minus")):
                        sp.dma_start(raw[:, m, i, :].rearrange("d (k e) -> d k e", e=P),
                                     g[name][i].rearrange("k d e -> d k e")).then_inc(big_in, 16)
                for i in range(4):
                    sp.dma_start(rmu[:, i, :].rearrange("d (k e) -> d k e", e=P),
                                 g["M_u"][i].rearrange("k d e -> d k e")).then_inc(mu_in, 16)

            @block.gpsimd
            def _(pool):
                pool.memset(quarter[:], 0.25).then_inc(pow_done, 1)
                pool.wait_ge(pow_done, 1)
                pool.wait_ge(small_in, 48)
                pool.tensor_tensor(sk[:], sig[:], quarter[:], ALU.pow).then_inc(pow_done, 1)

            @block.scalar
            def _(act):
                act.wait_ge(z_done, 1)
                act.activation(e[:], z[:], ACT.Exp).then_inc(e_done, 1)

            @block.vector
            def _(v):
                done = [0]

                def then(ins):
                    done[0] += 1
                    ins.then_inc(step, 1)
                    v.wait_ge(step, done[0])

                then(v.memset(one[:], 1.0))
                v.wait_ge(small_in, 48)
                then(v.tensor_tensor(z[:], lw[:], gum[:], ALU.add))
                then(v.tensor_reduce(w[:, 0:1], z[:], AX.X, ALU.max))
                v.tensor_scalar(z[:], z[:], w[:, 0:1], None, ALU.subtract).then_inc(z_done, 1)
                v.wait_ge(e_done, 1)
                then(v.tensor_reduce(w[:, 0:1], e[:], AX.X, ALU.add))
                then(v.reciprocal(w[:, 1:2], w[:, 0:1]))
                then(v.tensor_scalar(soft[:], e[:], w[:, 1:2], None, ALU.mult))
                then(v.tensor_reduce(w[:, 0:1], soft[:], AX.X, ALU.max))
                then(v.tensor_scalar(eq[:], soft[:], w[:, 0:1], None, ALU.is_ge))
                then(v.tensor_copy(hard[:, 0:1], eq[:, 0:1]))
                then(v.tensor_tensor(left[:, 0:1], one[:, 0:1], eq[:, 0:1], ALU.subtract))
                for i in range(1, 4):
                    then(v.tensor_tensor(hard[:, i:i + 1], eq[:, i:i + 1], left[:, i - 1:i], ALU.mult))
                    then(v.tensor_tensor(left[:, i:i + 1], left[:, i - 1:i], hard[:, i:i + 1], ALU.subtract))
                then(v.tensor_tensor(w[:], hard[:], soft[:], ALU.subtract))
                then(v.tensor_tensor(w[:], w[:], soft[:], ALU.add))
                then(v.tensor_copy(seg[:, 3:4], hard[:, 0:1]))
                for j in (2, 1, 0):
                    then(v.tensor_tensor(seg[:, j:j + 1], seg[:, j + 1:j + 2], hard[:, 3 - j:4 - j], ALU.add))
                v.wait_ge(mu_in, 64)
                mu_f = mu[:].rearrange("d k e -> d (k e)")
                then(v.tensor_scalar(mu_f, rmu[:, 0, :], w[:, 0:1], None, ALU.mult))
                for i in range(1, 4):
                    then(v.scalar_tensor_tensor(mu_f, rmu[:, i, :], w[:, i:i + 1], mu_f, ALU.mult, ALU.add))
                v.wait_ge(big_in, 128)
                for m in range(2):
                    then(v.tensor_scalar(acc[:, m, :], raw[:, m, 0, :], w[:, 0:1], None, ALU.mult))
                    for i in range(1, 4):
                        then(v.scalar_tensor_tensor(acc[:, m, :], raw[:, m, i, :], w[:, i:i + 1], acc[:, m, :],
                                                    ALU.mult, ALU.add))
                v.wait_ge(pow_done, 2)
                for m, op in enumerate((ALU.add, ALU.subtract)):
                    then(v.tensor_tensor(raw[:, m, 0, :], acc[:, 0, :], acc[:, 1, :], op))
                    full = raw[:, m, 1, :].rearrange("d (k e) -> d k e", e=P)
                    then(v.tensor_tensor(full, raw[:, m, 0, :].rearrange("d (k e) -> d k e", e=P),
                                         sk[:].unsqueeze(2).broadcast_to((P, K, P)), ALU.mult))
                    then(v.tensor_copy(me[:, 0, m], full))
                    then(low_part(v, me[:, 1, m], full, me[:, 0, m]))


def stu_transforms(nc, sems, g, hn, u_hat, g_hat):
    DC = 16
    STEPS = P // DC
    s = Scope(nc, sems, "dft")
    with s.stack:
        wp = s.sb("wp", [NB, P])
        wu = s.sb("wu", [P, 2, P])
        ph = s.sb("ph", [NB, K, 2 * BL])
        gs = s.sb("gs", [2 * NB, 2, K, 2, BL, 2], F32R)
        u = s.sb("u", [P, 2, DC, BL])
        uo = s.sb("uo", [P, 2, 2, 2, 2, DC, HALF], F32R)
        pp = s.ps("pp", [P, 2, BANK])
        pu = s.ps("pu", [P, 4, BANK])
        w_in, ph_in, ph_mm, ph_high, ph_out, g_stored, u_mm, u_high, u_low, u_used = (
            s.sem(n) for n in ("w_in", "ph_in", "ph_mm", "ph_high", "ph_out", "g_stored", "u_mm", "u_high", "u_low",
                               "u_used"))
        u_in = [s.sem(f"u_in{k}") for k in range(2)]
        u_stored = [s.sem(f"u_stored{k}") for k in range(2)]
        NP = K * 2 * BL // BANK
        MM = DC * BL // BANK
        hv = hn.rearrange("d (ba n) -> ba d n", n=BL)
        with nc.Block() as block:

            @block.sync
            def _(sp):
                sp.dma_start(wp[:], g["c_dft_phi"]).then_inc(w_in, 16)
                sp.dma_start(wu[:], g["c_dft_u"].rearrange("r p m -> p r m")).then_inc(w_in, 16)
                for half in range(2):
                    sp.dma_start(ph[:, :, half * BL:(half + 1) * BL],
                                 g["phi"][:, half * BL:half * BL + T].rearrange("k (a m) -> a k m", m=BL)
                                 ).then_inc(ph_in, 16)
                for c in range(STEPS):
                    if c >= 2:
                        sp.wait_ge(u_used, c - 1)
                    sp.dma_start(u[:, c % 2], hv[:, c * DC:(c + 1) * DC, :]).then_inc(u_in[c % 2], 16)
                sp.wait_ge(ph_out, 4 * NP)
                for part in range(2):
                    sp.dma_start(g_hat[part].rearrange("w x k r m y -> (w x) (k r m y)"),
                                 gs[:, part].rearrange("p k r m y -> p (k r m y)").bitcast(F32)).then_inc(g_stored, 16)
                sp.wait_ge(g_stored, 32)
                for k in range(2):
                    sp.wait_ge(u_stored[k], 256 * (STEPS // 2))

            @block.tensor
            def _(pe):
                pe.wait_ge(w_in, 32)
                pe.wait_ge(ph_in, 32)
                phf = ph[:].rearrange("a k m -> a (k m)")
                for n in range(NP):
                    for y in range(2):
                        if n >= 1:
                            pe.wait_ge(ph_out, 2 * (2 * n + y - 1))
                        pe.matmul(pp[0:2 * NB, y, :], wp[:, y * 2 * NB:(y + 1) * 2 * NB],
                                  phf[:, n * BANK:(n + 1) * BANK], start=True, stop=True).then_inc(ph_mm, 1)
                for c in range(STEPS):
                    pe.wait_ge(u_in[c % 2], 16 * (c // 2 + 1))
                    uf = u[:, c % 2].rearrange("p d n -> p (d n)")
                    for n in range(2 * MM):
                        tot = c * 2 * MM + n
                        if tot >= 4:
                            pe.wait_ge(u_low, tot - 3)
                        mm = pe.matmul(pu[:, tot % 4, :], wu[:, n // MM, :], uf[:, n % MM * BANK:(n % MM + 1) * BANK],
                                       start=True, stop=True)
                        mm.then_inc(u_mm, 1)
                    mm = None
                    pe.wait_ge(u_mm, (c + 1) * 2 * MM)
                    pe.sem_inc(u_used, 1)

            def tokens(eng, step):
                for c in range(STEPS):
                    if c >= 2:
                        eng.wait_ge(u_stored[c % 2], 256 * (c // 2))
                    for n in range(2 * MM):
                        d0 = n % MM * (BANK // BL)
                        tot = c * 2 * MM + n
                        for q in range(2):
                            src = pu[:, tot % 4, :].rearrange("p (d j q) -> p q d j", q=2, j=HALF)[:, q, :, ::-1]
                            step(tot, q, src, *(uo[:, c % 2, part, n // MM, q, d0:d0 + BANK // BL, :]
                                                for part in range(2)))

            @block.vector
            def _(v):
                for n in range(NP):
                    for y in range(2):
                        v.wait_ge(ph_mm, 2 * n + y + 1)
                        full = pp[0:2 * NB, y, :].rearrange("p (k m r) -> p k r m", k=2, r=2)
                        high, low = (gs[:, part, 2 * n:2 * n + 2, :, :, y] for part in range(2))
                        v.tensor_copy(high, full).then_inc(ph_high, 1)
                        v.wait_ge(ph_high, 2 * n + y + 1)
                        for k in range(2):
                            low_part(v, low[:, k], full[:, k], high[:, k]).then_inc(ph_out, 1)

                def low_tokens(tot, q, src, high, low):
                    v.wait_ge(u_high, 2 * tot + 2)
                    ins = low_part(v, low, src, high)
                    if q:
                        ins.then_inc(u_low, 1)

                tokens(v, low_tokens)

            @block.scalar
            def _(act):
                def high_tokens(tot, q, src, high, low):
                    act.wait_ge(u_mm, tot + 1)
                    act.activation(high, src, ACT.Copy).then_inc(u_high, 1)

                tokens(act, high_tokens)

            @block.gpsimd
            def _(pool):
                for c in range(STEPS):
                    pool.wait_ge(u_low, (c + 1) * 2 * MM)
                    for part in range(2):
                        for r in range(2):
                            for x in range(2):
                                for b2 in range(2):
                                    p0 = x * HALF + b2 * NB
                                    pool.dma_start(u_hat[part, :, x, 2 * r + b2, :, c * DC:(c + 1) * DC, :],
                                                   uo[p0:p0 + NB, c % 2, part, r].bitcast(F32)).then_inc(u_stored[c % 2], 16)


def stu_convolve(nc, sems, me, u_hat, g_hat, y_hat):
    s = Scope(nc, sems, "cv")
    NG = K // KG
    W = 2
    NI = NB // W
    GPB = W * NG
    with s.stack:
        u = s.sb("u", [P, W, 2, B, 2, 2, HALF], F32R)
        tp = s.sb("tp", [P, 2, 2, KG, 2, 2 * (HALF + 1)], F32R)
        vb = s.sb("vb", [P, 2, 2, 4, KG, B, P], F32R)
        yo = s.sb("yo", [P, 2, B, P])
        pv = s.ps("pv", [P, 4, BANK])
        py = s.ps("py", [P, 4, BANK])
        u_in = [s.sem(f"u_in{k}") for k in range(W)]
        t_in = [s.sem(f"t_in{k}") for k in range(2)]
        y_stored = [s.sem(f"y_stored{k}") for k in range(2)]
        v_mm, v_high, v_low, g_done, y_evac, yo_free = (
            s.sem(n) for n in ("v_mm", "v_high", "v_low", "g_done", "y_evac", "yo_free"))
        VT = 16
        with nc.Block() as block:

            @block.sync
            def _(sp):
                with sp.Fori(0, NI) as i:
                    for gg in range(GPB):
                        w, kg = divmod(gg, NG)
                        if kg == 0:
                            sp.wait_ge(v_mm, (i * GPB + (w + 1) * NG) * VT)
                            for part in range(2):
                                for x in range(2):
                                    sp.dma_start(u[:, w, part, :, :, x, :].rearrange("d b q j -> d (b q) j").bitcast(F32),
                                                 u_hat[part, i * W + w, x].rearrange("b q d j -> d (b q) j")
                                                 ).then_inc(u_in[w], 16)
                        sp.wait_ge(g_done, i * GPB + gg + 1)
                        for part in range(2):
                            for x in range(2):
                                row = g_hat[part, i * W + w, x, kg * KG:(kg + 1) * KG]
                                src = bass.AP(row.tensor, row.offset,
                                              ap=[[2, HALF], [2 * BL, KG * 2], [1, 2 * HALF + 2]])
                                sp.dma_start(tp[x * HALF:(x + 1) * HALF, gg % 2, part].rearrange("p k r m -> p (k r) m").bitcast(F32),
                                             src).then_inc(t_in[gg % 2], 16)

            @block.tensor
            def _(pe):
                pe.sem_inc(v_mm, GPB * VT)
                pe.sem_inc(g_done, 2)
                with pe.Fori(0, NI) as i:

                    def make_v(gg):
                        w, kg = divmod(gg, NG)
                        if kg == 0:
                            pe.wait_ge(u_in[w], i * 64 + 64)
                        for n in range(VT):
                            qt, b = divmod(n, B)
                            q, ty = divmod(qt, 2)
                            pe.wait_ge(v_low, (i * GPB + gg) * VT + n + 1)
                            product(pe, pv[:, n % 4, :], [u[:, w, part, b, q] for part in range(2)],
                                    [me[:, part, ty, kg * KG:(kg + 1) * KG, :] for part in range(2)],
                                    start=True, stop=True).then_inc(v_mm, 1)

                    def toeplitz(gg):
                        w, kg = divmod(gg, NG)
                        pe.wait_ge(t_in[gg % 2], i * (32 * GPB) + (gg // 2 + 1) * 64)
                        pe.wait_ge(v_low, (i * GPB + gg + 1) * VT + 4)
                        for p in range(2):
                            if kg == 0:
                                pe.wait_ge(y_evac, i * (2 * W) + 2 * w + p + 1)
                            for k in range(KG):
                                for q in range(2):
                                    par = p ^ q
                                    off = 0 if (p, q) == (0, 1) else 1
                                    mm = product(pe, py[:, 2 * w + p, :],
                                                 [tp[:, gg % 2, part, k, par, 2 * off:2 * off + P] for part in range(2)],
                                                 [vb[:, gg % 2, part, 2 * q + par, k] for part in range(2)],
                                                 start=(kg == 0 and k == 0 and q == 0),
                                                 stop=(kg == NG - 1 and k == KG - 1 and q == 1))
                        mm.then_inc(g_done, 1)

                    make_v(0)
                    for gg in range(GPB):
                        if gg + 1 < GPB:
                            make_v(gg + 1)
                        toeplitz(gg)

            def split_v(eng, step, i, gg):
                eng.wait_ge(g_done, i * GPB + gg + 1)
                for n in range(VT):
                    qt, b = divmod(n, B)
                    step(n, pv[:, n % 4, :].rearrange("p (k e) -> p k e", e=P),
                         *(vb[:, gg % 2, part, qt, :, b, :] for part in range(2)))

            @block.gpsimd
            def _(pool):
                pool.sem_inc(yo_free, 2)
                with pool.Fori(0, NI) as i:
                    for w in range(W):
                        for p in range(2):
                            pool.wait_ge(y_evac, i * (2 * W) + 2 * w + p + 1 + 2 * W)
                            pool.dma_start(y_hat[p, :, i * W + w].rearrange("b j y e -> (j y) b e"),
                                           yo[:, p]).then_inc(y_stored[p], 16)
                        for p in range(2):
                            pool.wait_ge(y_stored[p], i * (16 * W) + w * 16 + 16)
                            pool.sem_inc(yo_free, 1)

            @block.scalar
            def _(act):
                with act.Fori(0, NI) as i:
                    for gg in range(GPB):

                        def high_v(n, full, high, low):
                            act.wait_ge(v_mm, (i * GPB + gg + GPB) * VT + n + 1)
                            act.activation(high, full, ACT.Copy).then_inc(v_high, 1)

                        split_v(act, high_v, i, gg)

            @block.vector
            def _(v):
                v.sem_inc(v_low, 4)
                v.sem_inc(y_evac, 2 * W)

                def copy_y(i, w):
                    v.wait_ge(g_done, (i * GPB + (w + 1) * NG) + 2)
                    for p in range(2):
                        v.wait_ge(yo_free, i * (2 * W) + 2 * w + 2)
                        v.tensor_copy(yo[:, p].rearrange("p b e -> p (b e)"), py[:, 2 * w + p, :]).then_inc(y_evac, 1)

                with v.Fori(0, NI) as i:
                    for gg in range(GPB):

                        def low_v(n, full, high, low):
                            v.wait_ge(v_high, (i * GPB + gg) * VT + n + 1)
                            low_part(v, low, full, high).then_inc(v_low, 1)

                        split_v(v, low_v, i, gg)
                        if gg % NG == 1 and gg > NG:
                            copy_y(i, gg // NG - 1)
                    copy_y(i, W - 1)


def stu_finish(nc, sems, g, mu, seg, y_hat, hn, t1, out):
    s = Scope(nc, sems, "fin")
    JB = BANK // NB
    with s.stack:
        wi = s.sb("wi", [2 * NB, NB])
        yh = s.sb("yh", [2 * NB, 2, HALF, P])
        ys = s.sb("ys", [P, NB, HALF, 2])
        h = s.sb("h", [P, 2 + T])
        t = s.sb("t", [P, T])
        o = s.sb("o", [P, T])
        py = s.ps("py", [P, 2, BANK])
        pa = s.ps("pa", [P, 2, BANK])
        yh_in = [s.sem(f"yh_in{k}") for k in range(2)]
        w_in, h_in, t_in, yh_used, y_mm, y_evac, ar_mm, summed, kept, o_stored, zeroed = (
            s.sem(n) for n in ("w_in", "h_in", "t_in", "yh_used", "y_mm", "y_evac", "ar_mm", "summed", "kept",
                               "o_stored", "zeroed"))
        NT = T // BANK
        NJ = 2 * HALF // JB
        SEG = (0, 1, 2, 2, 3, 3, 3, 3)
        hv, tv, ov = (a.rearrange("p (b n) -> p b n", b=B) for a in (hn, t1, out))
        with nc.Block() as block:

            @block.sync
            def _(sp):
                sp.dma_start(wi[:], g["c_idft"]).then_inc(w_in, 16)
                with sp.Fori(0, B) as b:
                    sp.wait_ge(ar_mm, b * NT + NT)
                    sp.wait_ge(kept, b * NT + NT)
                    sp.dma_start(h[:, 2:], hv[:, b, :]).then_inc(h_in, 16)
                    sp.dma_start(t[:], tv[:, b, :]).then_inc(t_in, 16)
                    for p in range(2):
                        sp.wait_ge(yh_used, b * 2 + p + 1)
                        for x in range(2):
                            sp.dma_start(yh[x * NB:(x + 1) * NB, p], y_hat[p, b, :, :, x, :]).then_inc(yh_in[p], 16)

            @block.gpsimd
            def _(pool):
                pool.memset(h[:, 0:2], 0.0).then_inc(zeroed, 1)

            @block.tensor
            def _(pe):
                pe.sem_inc(ar_mm, NT)
                pe.sem_inc(yh_used, 2)
                pe.wait_ge(w_in, 16)
                pe.wait_ge(zeroed, 1)
                with pe.Fori(0, B) as b:
                    for p in range(2):
                        pe.wait_ge(yh_in[p], b * 32 + 32)
                        for c in range(NJ // 2):
                            n = p * (NJ // 2) + c
                            pe.wait_ge(y_evac, b * NJ + n + 1)
                            for jj in range(JB):
                                mm = pe.matmul(py[:, n % 2, jj * NB:(jj + 1) * NB], yh[:, p, c * JB + jj, :], wi[:],
                                               start=True, stop=True, skip_group_check=True)
                            mm.then_inc(y_mm, 1)
                        pe.wait_ge(y_mm, b * NJ + (p + 1) * (NJ // 2))
                        pe.sem_inc(yh_used, 1)
                    pe.wait_ge(h_in, b * 16 + 16)
                    for c in range(NT):
                        pe.wait_ge(summed, b * NT + c + 1)
                        for d in range(3):
                            mm = pe.matmul(pa[:, c % 2, :], mu[:, d, :], h[:, 2 - d + c * BANK:2 - d + (c + 1) * BANK],
                                           start=(d == 0), stop=(d == 2))
                        mm.then_inc(ar_mm, 1)

            @block.vector
            def _(v):
                v.sem_inc(y_evac, 2)
                v.sem_inc(summed, 2)
                v.sem_inc(kept, NT)
                with v.Fori(0, B) as b:
                    v.wait_ge(kept, b * NT + NT)
                    for n in range(NJ):
                        p, c = divmod(n, NJ // 2)
                        v.wait_ge(y_mm, b * NJ + n + 1)
                        v.tensor_copy(ys[:, :, c * JB:(c + 1) * JB, p],
                                      py[:, n % 2, :].rearrange("e (j a) -> e a j", a=NB)).then_inc(y_evac, 1)
                    v.wait_ge(y_evac, b * NJ + NJ + 2)
                    v.wait_ge(t_in, b * 16 + 16)
                    v.wait_ge(o_stored, b * 16 + 16)
                    yf = ys[:].rearrange("e a j q -> e (a j q)")
                    for c in range(NT):
                        sl = slice(c * BANK, (c + 1) * BANK)
                        v.wait_ge(ar_mm, b * NT + c + 1 + NT)
                        v.tensor_tensor(yf[:, sl], yf[:, sl], pa[:, c % 2, :], ALU.add).then_inc(summed, 1)
                        v.wait_ge(summed, b * NT + c + 3)
                        v.scalar_tensor_tensor(o[:, sl], yf[:, sl], seg[:, SEG[c]:SEG[c] + 1], t[:, sl],
                                               ALU.mult, ALU.add).then_inc(kept, 1)

            @block.scalar
            def _(act):
                act.sem_inc(o_stored, 16)
                with act.Fori(0, B) as b:
                    act.wait_ge(kept, b * NT + 2 * NT)
                    act.dma_start(ov[:, b, :], o[:]).then_inc(o_stored, 16)
                act.wait_ge(o_stored, 16 * (B + 1))


def program(nc, g, out):
    def scratch(name):
        return nc.dram_tensor(name, (P, N), F32, kind="Internal").ap()

    c3, t0, t1, hn1, hn2, hf, hb = (scratch(n) for n in ("c3", "t0", "t1", "hn1", "hn2", "h_forward", "h_backward"))
    sems = []
    conv_block(nc, sems, g, c3)
    attention(nc, sems, g, c3, t0)
    layer_norm(nc, sems, "ln1", [t0], None, hn1, g["c_mean"])
    release(nc, sems)
    mamba(nc, sems, g, hn1, (hf, hb))
    release(nc, sems)
    layer_norm(nc, sems, "ln2", [t0, hf, hb], t1, hn2, g["c_mean"])
    spectral(nc, sems, g, hn2, t1, out)


def laid_out(inputs):
    i = {k: np.asarray(v) for k, v in inputs.items()}
    col = lambda a: a[:, None]
    rep = lambda a: np.broadcast_to(a, (P,) + a.shape)
    c = {k[8:]: v for k, v in i.items() if k.startswith("L0_conv_")}
    m = [{k[12:]: v for k, v in i.items() if k.startswith(f"L1_attn_{p}")} for p in ("fwd", "bwd")]
    f = {k[7:]: v for k, v in i.items() if k.startswith("L1_ffn_")}
    a = {"x": i["x"].reshape(N, P).T, "W1": c["W1"], "W2": c["W2"], "b1": col(c["b1"]), "b2a": col(c["b2"][:P]),
         "b2b": col(c["b2"][P:]), "Wv": c["Wv"], "bv": rep(c["bv"]), "W3": c["W3"], "b3": col(c["b3"])}
    a["Wqk"], a["bqk"] = np.zeros((P, P), np.float32), np.zeros((P, 1), np.float32)
    for n in range(PARTS * PARTS):
        for at, w, b in ((0, "Wq", "bq"), (64, "Wk", "bk")):
            a["Wqk"][:, at + n * DQK:at + (n + 1) * DQK] = c[w]
            a["bqk"][at + n * DQK:at + (n + 1) * DQK, 0] = c[b]
    nz = 2 * DI + 2 * DS
    a["Wdt"] = np.concatenate([d["in_proj"][:, nz:] for d in m], 1)
    a["dt_bias"] = rep(np.stack([d["dt_bias"] for d in m]))
    a["A_log"] = rep(np.stack([d["A_log"] for d in m]))
    for n, d in enumerate(m):
        a[f"in_proj{n}"] = d["in_proj"][:, :nz]
        a[f"conv_w{n}"] = d["conv_w"].reshape(3, P, TAPS).transpose(1, 0, 2)
        a[f"conv_b{n}"] = d["conv_b"].reshape(3, P).T
        a[f"D{n}"] = np.repeat(d["D"], HD).reshape(2, P).T
        a[f"norm_w{n}"] = d["norm_w"].reshape(2, P).T
        a[f"out_proj{n}"] = d["out_proj"].reshape(2, P, P).transpose(1, 0, 2)
    a["phi"] = np.zeros((K, BL + T), np.float32)
    a["phi"][:, BL:] = f["phi"].T
    a.update(M_u=f["M_u"], M_phi_plus=f["M_phi_plus"], M_phi_minus=f["M_phi_minus"], sigma=rep(f["sigma"]),
             log_weights=rep(f["log_weights"]), gumbel=rep(f["gumbel"]), c_mean=np.full((P, P), 1 / P, np.float32))
    for constants in (attention_constants(), mamba_constants(), stu_constants()):
        a.update(constants)
    return {k: np.ascontiguousarray(v) for k, v in a.items()}


def kernel(**inputs):
    import concourse.bacc as bacc
    from concourse.bass_utils import run_bass_kernel_spmd

    arrays = laid_out(inputs)
    nc = bacc.Bacc("TRN2", target_bir_lowering=False, num_devices=1)
    g = {k: nc.dram_tensor(f"in_{k}", v.shape, F32, kind="ExternalInput").ap() for k, v in arrays.items()}
    out = nc.dram_tensor("out", (P, N), F32, kind="ExternalOutput").ap()
    program(nc, g, out)
    r = run_bass_kernel_spmd(nc, [{f"in_{k}": v for k, v in arrays.items()}], core_ids=[0])
    return r.results[0]["out"].T.reshape(B, IMG, IMG, P)
```

```python
from contextlib import ExitStack

import numpy as np

import concourse.bass as bass
from concourse import mybir

F32 = mybir.dt.float32
BF16 = mybir.dt.bfloat16
F32R = mybir.dt.float32r
ALU = mybir.AluOpType
ACT = mybir.ActivationFunctionType
AX = mybir.AxisListType

P = 128
B, IMG = 4, 64
T = IMG * IMG
N = B * T
BANK = 512
TILES = N // BANK

DQK, DV, HEADS = 4, 16, 8
PARTS = 3
PAIRS = PARTS * PARTS * DQK
MROW = 64
MASK1, MASK2 = -1.0e30, -2.0e38

CH = 128
NCH = T // CH
NH, HD, DS, DI = 4, 64, 64, 256
TAPS = 4

K = 16
BL, NB, HALF = 128, 32, 64
NF = 2 * NB
KG = 4
FRACS = (1, 2, 4, 8)


class Scope:

    def __init__(self, nc, sems, name):
        self.nc, self.sems, self.name, self.stack = nc, sems, name, ExitStack()

    def sb(self, name, shape, dt=F32):
        return self.stack.enter_context(self.nc.sbuf_tensor(f"{self.name}_{name}", shape, dt))

    def ps(self, name, shape, dt=F32):
        return self.stack.enter_context(self.nc.psum_tensor(f"{self.name}_{name}", shape, dt))

    def sem(self, name):
        self.sems.append(self.nc.alloc_semaphore(name=f"{self.name}_{name}"))
        return self.sems[-1]


def product(pe, out, stationary, moving, start, stop, **kw):
    for n, (a, b) in enumerate(((0, 0), (0, 1), (1, 0))):
        mm = pe.matmul(out, stationary[a], moving[b], start=start and n == 0, stop=stop and n == 2, **kw)
    return mm


def low_part(v, out, full, high):
    return v.tensor_tensor(out, full, high.bitcast(F32), ALU.subtract)


def hold(eng, passed):
    eng.sem_inc(passed, 1)


def release(nc, sems):
    nc.clear_and_free_semaphores(sems)
    nc.all_engine_barrier()
    sems.clear()


def layer_norm(nc, sems, name, addends, total, out, c_mean):
    s = Scope(nc, sems, name)
    na = len(addends)
    G, ITER = 4, TILES // 8
    with s.stack:
        mean_w = s.sb("mean_w", [P, P])
        eps = s.sb("eps", [P, 1])
        x = s.sb("x", [P, 2, na, G, BANK])
        xc = s.sb("xc", [P, 2, G, BANK])
        sq = s.sb("sq", [P, G, BANK])
        rs = s.sb("rs", [P, G, BANK])
        y = s.sb("y", [P, 2, G, BANK])
        mean = s.ps("mean", [P, G, BANK])
        var = s.ps("var", [P, G, BANK])
        loaded, stored, sum_stored = ([s.sem(f"{n}{k}") for k in range(2)] for n in ("loaded", "stored", "sum_stored"))
        w_in, summed, mean_done, centred, squared, var_done, logged, rooted, normed, eps_set = (
            s.sem(n) for n in ("w_in", "summed", "mean_done", "centred", "squared", "var_done", "logged", "rooted",
                               "normed", "eps_set"))
        views = [a.rearrange("p (t n) -> p t n", n=G * BANK) for a in addends]
        out_v = out.rearrange("p (t n) -> p t n", n=G * BANK)
        tot_v = total.rearrange("p (t n) -> p t n", n=G * BANK) if total is not None else None
        flat = lambda ap: ap.rearrange("p g n -> p (g n)")
        with nc.Block() as block:

            @block.sync
            def _(sp):
                sp.dma_start(mean_w[:], c_mean).then_inc(w_in, 16)
                with sp.Fori(0, ITER) as i:
                    for k in range(2):
                        sp.wait_ge(centred, i * (2 * G) + (k + 1) * G)
                        if total is not None:
                            sp.wait_ge(sum_stored[k], i * 16 + 16)
                        for a in range(na):
                            sp.dma_start(flat(x[:, k, a]), views[a][:, i * 2 + k, :]).then_inc(loaded[k], 16)

            @block.vector
            def _(v):
                v.memset(eps[:], 1e-5).then_inc(eps_set, 1)
                v.sem_inc(normed, G)
                v.sem_inc(centred, 2 * G)

                def centre(i, k):
                    v.wait_ge(loaded[k], i * (16 * na) + 16 * na)
                    for a in range(1, na):
                        for t in range(G):
                            if a > 1:
                                v.wait_ge(summed, (i * 2 + k) * ((na - 1) * G) + (a - 2) * G + t + 1)
                            v.tensor_tensor(x[:, k, 0, t], x[:, k, 0, t], x[:, k, a, t], ALU.add
                                            ).then_inc(summed, 1)
                    for t in range(G):
                        v.wait_ge(mean_done, (i * 2 + k) * G + t + 1)
                        v.tensor_tensor(xc[:, k, t], x[:, k, 0, t], mean[:, t], ALU.subtract).then_inc(centred, 1)

                def scale(i, k):
                    v.wait_ge(stored[k], i * 16 + 16)
                    for t in range(G):
                        v.wait_ge(rooted, (i * 2 + k) * G + t + 1)
                        v.tensor_tensor(y[:, k, t], xc[:, k, t], rs[:, t], ALU.mult).then_inc(normed, 1)

                centre(0, 0)
                with v.Fori(0, ITER - 1) as i:
                    centre(i, 1)
                    scale(i, 0)
                    centre(i + 1, 0)
                    scale(i, 1)
                centre(ITER - 1, 1)
                scale(ITER - 1, 0)
                scale(ITER - 1, 1)

            @block.tensor
            def _(pe):
                pe.wait_ge(w_in, 16)
                with pe.Fori(0, ITER) as i:
                    for k in range(2):
                        pe.wait_ge(loaded[k], i * (16 * na) + 16 * na)
                        for t in range(G):
                            if na > 1:
                                pe.wait_ge(summed, (i * 2 + k) * ((na - 1) * G) + (na - 2) * G + t + 1)
                            pe.wait_ge(centred, (i * 2 + k) * G + t + 1 + G)
                            pe.matmul(mean[:, t], mean_w[:], x[:, k, 0, t], start=True, stop=True
                                      ).then_inc(mean_done, 1)
                        for t in range(G):
                            pe.wait_ge(squared, (i * 2 + k) * G + t + 1)
                            pe.matmul(var[:, t], mean_w[:], sq[:, t], start=True, stop=True).then_inc(var_done, 1)

            @block.scalar
            def _(act):
                for k in range(2):
                    act.sem_inc(stored[k], 16)
                    act.sem_inc(sum_stored[k], 16)
                act.wait_ge(eps_set, 1)
                with act.Fori(0, ITER) as i:
                    for k in range(2):
                        for t in range(G):
                            act.wait_ge(centred, (i * 2 + k) * G + t + 1 + 2 * G)
                            act.activation(sq[:, t], xc[:, k, t], ACT.Square).then_inc(squared, 1)
                        if total is not None:
                            act.dma_start(tot_v[:, i * 2 + k, :], flat(x[:, k, 0])).then_inc(sum_stored[k], 16)
                        for t in range(G):
                            act.wait_ge(var_done, (i * 2 + k) * G + t + 1)
                            act.wait_ge(normed, (i * 2 + k) * G + t + 1)
                            act.activation(rs[:, t], var[:, t], ACT.Ln, bias=eps[:, 0:1]).then_inc(logged, 1)
                        for t in range(G):
                            act.wait_ge(logged, (i * 2 + k) * G + t + 1)
                            act.activation(rs[:, t], rs[:, t], ACT.Exp, scale=-0.5).then_inc(rooted, 1)
                        act.wait_ge(normed, (i * 2 + k) * G + 2 * G)
                        act.dma_start(out_v[:, i * 2 + k, :], flat(y[:, k])).then_inc(stored[k], 16)
                for k in range(2):
                    act.wait_ge(stored[k], 16 * (ITER + 1))
                    if total is not None:
                        act.wait_ge(sum_stored[k], 16 * (ITER + 1))


PW = IMG + 2
ROWS = BANK // IMG
GT = T // BANK


def conv_block(nc, sems, g, c3):
    s = Scope(nc, sems, "conv")
    Q = 4
    QR = IMG // Q
    with s.stack:
        w_raw = s.sb("w_raw", [P, 27 * P])
        w = s.sb("w", [P, 2, 27 * P], F32R)
        bias = s.sb("bias", [P, 3])
        x = s.sb("x", [P, IMG, IMG])
        neg = s.sb("neg", [P, 2, QR, IMG])
        pos = s.sb("pos", [P, 2, QR, IMG])
        ex = s.sb("ex", [P, 2, QR, IMG])
        xp = s.sb("xp", [P, 2, PW, PW], F32R)
        c1 = s.sb("c1", [P, 2, PW, PW], F32R)
        sg = s.sb("sg", [P, 2, BANK])
        co = s.sb("co", [P, 2, BANK])
        p1 = s.ps("p1", [P, 2, BANK])
        pa = s.ps("pa", [P, 2, BANK])
        pb = s.ps("pb", [P, 2, BANK])
        w_in, w_high, w_low, x_in, halves, exped, added, x_high, elu_done, c1_mm, c1_high, c1_evac, c2_mm, gated, \
            sig_done, bordered, passed = (s.sem(n) for n in (
                "w_in", "w_high", "w_low", "x_in", "halves", "exped", "added", "x_high", "elu_done", "c1_mm", "c1_high",
                "c1_evac", "c2_mm", "gated", "sig_done", "bordered", "passed"))
        w1 = [w[:, part, 0:9 * P].rearrange("i (k o) -> i k o", o=P) for part in range(2)]
        w2 = [w[:, part, 9 * P:].rearrange("i (k o) -> i k o", o=2 * P) for part in range(2)]
        stored = [s.sem(f"stored{k}") for k in range(2)]
        xv = g["x"].rearrange("p (b h w) -> p b h w", b=B, h=IMG)
        cv = c3.rearrange("p (b g n) -> p b g n", b=B, g=GT)

        def interior(part, t):
            return c1[:, part, 1 + t * ROWS:1 + (t + 1) * ROWS, 1:1 + IMG]

        def image(ap):
            return ap.rearrange("p (r c) -> p r c", c=IMG)

        with nc.Block() as block:

            @block.sync
            def _(sp):
                sp.dma_start(x[:], xv[:, 0]).then_inc(x_in, 16)
                sp.dma_start(w_raw[:, 0:9 * P].rearrange("i (k o) -> i k o", o=P),
                             g["W1"].rearrange("h w i o -> i (h w) o")).then_inc(w_in, 16)
                sp.dma_start(w_raw[:, 9 * P:].rearrange("i (k o) -> i k o", o=2 * P),
                             g["W2"].rearrange("h w i o -> i (h w) o")).then_inc(w_in, 16)
                for k, name in enumerate(("b1", "b2a", "b2b")):
                    sp.dma_start(bias[:, k:k + 1], g[name]).then_inc(w_in, 16)
                with sp.Fori(0, B - 1) as b:
                    sp.wait_ge(halves, b * (2 * Q) + 2 * Q)
                    sp.dma_start(x[:], xv[:, b + 1]).then_inc(x_in, 16)

            @block.gpsimd
            def _(pool):
                with pool.Fori(0, B) as b:
                    pool.wait_ge(x_in, b * 16 + 16)
                    for q in range(Q):
                        pool.wait_ge(elu_done, b * Q + q + 1)
                        hold(pool, passed)
                        rows = x[:, q * QR:(q + 1) * QR, :]
                        pool.tensor_scalar(neg[:, q % 2], rows, 0.0, None, ALU.min).then_inc(halves, 1)
                        pool.tensor_scalar(pos[:, q % 2], rows, 0.0, None, ALU.max).then_inc(halves, 1)

            @block.tensor
            def _(pe):
                pe.sem_inc(c1_mm, GT)
                pe.wait_ge(w_low, 1)
                pe.wait_ge(bordered, 4)
                with pe.Fori(0, B) as b:
                    for t in range(GT):
                        pe.wait_ge(elu_done, b * Q + min(ROWS * (t + 1), IMG - 1) // QR + 1 + 2)
                        pe.wait_ge(c1_evac, b * GT + t + 1)
                        for k in range(9):
                            dy, dx = divmod(k, 3)
                            mm = product(pe, p1[:, t % 2, :], [w1[part][:, k, :] for part in range(2)],
                                         [xp[:, part, t * ROWS + dy:t * ROWS + dy + ROWS, dx:dx + IMG]
                                          for part in range(2)], start=(k == 0), stop=(k == 8))
                        mm.then_inc(c1_mm, 1)
                    for t in range(GT):
                        pe.wait_ge(c1_evac, b * GT + min(t + 2, GT) + 2)
                        pe.wait_ge(gated, b * GT + t + 1)
                        for half, bank in enumerate((pa, pb)):
                            for k in range(9):
                                dy, dx = divmod(k, 3)
                                mm = product(pe, bank[:, t % 2, :],
                                             [w2[part][:, k, half * P:(half + 1) * P] for part in range(2)],
                                             [c1[:, part, t * ROWS + dy:t * ROWS + dy + ROWS, dx:dx + IMG]
                                              for part in range(2)], start=(k == 0), stop=(k == 8))
                        mm.then_inc(c2_mm, 1)

            @block.scalar
            def _(act):
                for k in range(2):
                    act.sem_inc(stored[k], 16)

                def exps(b):
                    for q in range(Q):
                        act.wait_ge(halves, b * (2 * Q) + 2 * q + 2)
                        act.activation(ex[:, q % 2], neg[:, q % 2], ACT.Exp).then_inc(exped, 1)
                        act.wait_ge(added, b * Q + q + 1)
                        act.activation(xp[:, 0, 1 + q * QR:1 + (q + 1) * QR, 1:1 + IMG], ex[:, q % 2], ACT.Copy
                                       ).then_inc(x_high, 1)

                def store(b, t):
                    act.wait_ge(gated, b * GT + t + 1 + 2)
                    act.dma_start(cv[:, b, t, :], co[:, t % 2, :]).then_inc(stored[t % 2], 16)

                def batch(b, more):
                    for t in range(GT):
                        act.wait_ge(c1_mm, b * GT + t + 1 + GT)
                        act.activation(interior(0, t), image(p1[:, t % 2, :]), ACT.Identity, bias=bias[:, 0:1]
                                       ).then_inc(c1_high, 1)
                    for t in range(GT):
                        if t == GT // 2 and more:
                            exps(b + 1)
                        act.wait_ge(c2_mm, b * GT + t + 1)
                        act.activation(sg[:, t % 2, :], pb[:, t % 2, :], ACT.Sigmoid, bias=bias[:, 2:3]
                                       ).then_inc(sig_done, 1)
                        if t:
                            store(b, t - 1)
                    store(b, GT - 1)

                act.wait_ge(w_in, 80)
                act.activation(w[:, 0], w_raw[:], ACT.Copy).then_inc(w_high, 1)
                act.wait_ge(bordered, 4)
                exps(0)
                with act.Fori(0, B - 1) as b:
                    batch(b, True)
                batch(B - 1, False)
                for k in range(2):
                    act.wait_ge(stored[k], 16 * (B * GT // 2 + 1))

            @block.vector
            def _(v):
                v.sem_inc(elu_done, 2)
                v.sem_inc(gated, 2)
                v.sem_inc(c1_evac, 2)
                for part in range(2):
                    v.memset(xp[:, part].bitcast(F32), 0.0).then_inc(bordered, 1)
                for part in range(2):
                    v.memset(c1[:, part].bitcast(F32), 0.0).then_inc(bordered, 1)
                v.wait_ge(bordered, 4)
                v.wait_ge(w_high, 1)
                low_part(v, w[:, 1], w_raw[:], w[:, 0]).then_inc(w_low, 1)

                def elus(b):
                    v.wait_ge(c1_mm, b * GT + GT)
                    for q in range(Q):
                        v.wait_ge(exped, b * Q + q + 1)
                        v.scalar_tensor_tensor(ex[:, q % 2], ex[:, q % 2], -1.0, pos[:, q % 2], ALU.add, ALU.add
                                               ).then_inc(added, 1)
                        v.wait_ge(x_high, b * Q + q + 1)
                        rows = slice(1 + q * QR, 1 + (q + 1) * QR)
                        low_part(v, xp[:, 1, rows, 1:1 + IMG], ex[:, q % 2], xp[:, 0, rows, 1:1 + IMG]
                                 ).then_inc(elu_done, 1)

                def batch(b, more):
                    for t in range(GT):
                        v.wait_ge(c1_high, b * GT + t + 1)
                        v.scalar_tensor_tensor(interior(1, t), image(p1[:, t % 2, :]), bias[:, 0:1],
                                               interior(0, t).bitcast(F32), ALU.add, ALU.subtract).then_inc(c1_evac, 1)
                    for t in range(GT):
                        if t == GT // 2 and more:
                            elus(b + 1)
                        v.wait_ge(sig_done, b * GT + t + 1)
                        v.wait_ge(stored[t % 2], b * (16 * GT // 2) + (t // 2) * 16 + 16)
                        v.scalar_tensor_tensor(co[:, t % 2, :], pa[:, t % 2, :], bias[:, 1:2], sg[:, t % 2, :],
                                               ALU.add, ALU.mult).then_inc(gated, 1)

                elus(0)
                with v.Fori(0, B - 1) as b:
                    batch(b, True)
                batch(B - 1, False)


def attention_constants():
    rows = np.arange(P)
    sel = np.zeros((P, 4), np.float32)
    for side in range(2):
        for i in range(PARTS):
            for j in range(PARTS):
                part = (i, j)[side]
                for d in range(DQK):
                    r = 64 * side + (i * PARTS + j) * DQK + d
                    sel[r, 0], sel[r, 1] = -float(part >= 1), -float(part >= 2)
    for part in range(PARTS):
        sel[MROW + part, 2], sel[MROW + part, 3] = -float(part >= 1), -float(part >= 2)
    mask = np.stack([np.where(rows[None, :] >= rows[:, None], MASK1, 0.0),
                     np.where(rows[:, None] >= rows[None, :], MASK2, 0.0)])
    fold = (rows[:, None] % DV == np.arange(DV)[None, :]).astype(np.float32)
    return {"c_sel": sel, "c_mask": mask.astype(np.float32), "c_ident": np.eye(P, dtype=np.float32),
            "c_fold": fold}


def attention(nc, sems, g, c3, t0):
    s = Scope(nc, sems, "att")
    NT = T // P
    items = [(G, kt) for G in range(GT) for kt in range(4 * G + 4)]
    NI = len(items)
    first = [2 * G * (G + 1) for G in range(GT + 1)]
    LAG, NS, NE = 2, 2, 4
    SLOTS = NI + LAG + 12
    units = [(i, k) for i in range(NT) for k in range(i // 4 + 1)]
    NU = len(units)
    SPLIT0, SPACE, UNIT0 = 2, 4, 10
    V_AT = SPLIT0 + GT * SPACE + 6
    V_PARTS = [V_AT - 6, V_AT - 4, V_AT - 2, V_AT]
    M_AT = UNIT0 + NU * 5 // 6 + 1
    R_AT = M_AT + 5
    NORM = [first[G + 1] + LAG for G in range(GT)]
    AT, PROJ, RES, STORE = 4, 6, 8, 10

    def units_at(n):
        return [u for u in range(NU) if UNIT0 + u * 5 // 6 == n]

    def split_at(n, stage=0):
        t, off = divmod(n - SPLIT0 - stage, SPACE)
        return t if not off and 0 <= t < GT else None

    m_dram = nc.dram_tensor("row_max", (B, T), F32, kind="Internal").ap()
    MH = T // 2
    rows = slice(MROW, MROW + PARTS)
    with s.stack:
        qs = s.sb("qs", [MROW + PARTS, B, T], BF16)
        ks = s.sb("ks", [MROW + PARTS, B, T], BF16)
        va = s.sb("va", [P, B, NT, DV])
        vc = s.sb("vc", [P, NT, 3 * DV])
        ident = s.sb("ident", [P, P])
        identb = s.sb("identb", [P, P], BF16)
        mask = s.sb("mask", [P, 2, P], BF16)
        mk = s.sb("mk", [P, 2, P])
        sel = s.sb("sel", [P, 4])
        wqk = s.sb("wqk", [P, P])
        wv = s.sb("wv", [P, DV])
        bqk = s.sb("bqk", [P, 1])
        bv = s.sb("bv", [P, DV])
        fold = s.sb("fold", [P, DV])
        w3 = s.sb("w3", [P, P])
        w3s = s.sb("w3s", [DV, P])
        b3 = s.sb("b3", [P, 1])
        f = s.sb("f", [P, T])
        qf = s.sb("qf", [P, 2, BANK])
        h1 = s.sb("h1", [P, 2, BANK], BF16)
        r1 = s.sb("r1", [P, 2, BANK])
        h2 = s.sb("h2", [P, 2, BANK], BF16)
        mp = s.sb("mp", [P, NT, GT])
        mall = s.sb("mall", [P, NT])
        mt = s.sb("mt", [NT, P])
        m_row = s.sb("m_row", [MROW + PARTS, 2, MH])
        m_h = s.sb("m_h", [MROW + PARTS, 2, MH], BF16)
        m_r = s.sb("m_r", [MROW + PARTS, 2, MH])
        e = s.sb("e", [P, NE, BANK])
        xr = s.sb("xr", [P, 2, BANK])
        cr = s.sb("cr", [P, 2, BANK])
        den = s.sb("den", [DV, BANK])
        rec = s.sb("rec", [DV, BANK])
        at = s.sb("at", [DV, BANK])
        o1 = s.sb("o1", [P, BANK])
        o2 = s.sb("o2", [P, 2, BANK])
        pq = s.ps("pq", [P, BANK])
        pu = s.ps("pu", [P, 2, BANK])
        sc = s.ps("sc", [P, NS, BANK])
        po = s.ps("po", [64, 2, BANK])
        pm = s.ps("pm", [P, BANK])
        (w_in, ready, f_in, qk_mm, v_mm, qf_done, h1_done, r1_done, h2_done, split, v_done, unit_mm, maxed, m_done,
         mt_mm, mt_done, m_stored, mh_done, mr_done, mh2_done, row_split) = (s.sem(n) for n in (
             "w_in", "ready", "f_in", "qk_mm", "v_mm", "qf_done", "h1_done", "r1_done", "h2_done", "split", "v_done",
             "unit_mm", "maxed", "m_done", "mt_mm", "mt_done", "m_stored", "mh_done", "mr_done", "mh2_done",
             "row_split"))
        passed = s.sem("passed")
        (fold_mm, fold_done, vc_done, sc_mm, exped, pv_mm, den_done, rec_done, at_done, proj_mm, o1_done, o2_done) = (
            s.sem(n) for n in ("fold_mm", "fold_done", "vc_done", "sc_mm", "exped", "pv_mm", "den_done", "rec_done",
                               "at_done", "proj_mm", "o1_done", "o2_done"))
        m_in, r_in, stored = ([s.sem(f"{n}{k}") for k in range(2)] for n in ("m_in", "r_in", "stored"))
        cb = c3.rearrange("p (b n) -> p b n", b=B)
        xv, cv, tv = (a.rearrange("p (b g n) -> p b g n", b=B, g=GT) for a in (g["x"], c3, t0))
        NW = 10 * 16
        READY = 7

        def batches(eng, values, coming):
            for n in range(SLOTS):
                coming(0, n)
            with eng.Fori(0, B - 1) as b:
                for n in range(SLOTS):
                    values(b, n)
                    coming(b + 1, n)
            for n in range(SLOTS):
                values(B - 1, n)

        with nc.Block() as block:

            @block.sync
            def _(sp):
                for dst, name in ((wqk, "Wqk"), (wv, "Wv"), (bqk, "bqk"), (bv, "bv"), (ident, "c_ident"), (sel, "c_sel"),
                                  (mk, "c_mask"), (fold, "c_fold"), (w3, "W3"), (b3, "b3")):
                    src = g[name].rearrange("m p n -> p m n") if name == "c_mask" else g[name]
                    sp.dma_start(dst[:], src).then_inc(w_in, 16)

                def values(b, n):
                    for G in range(GT):
                        if n == first[G]:
                            sp.wait_ge(o2_done, b * GT + G + 1)
                            sp.dma_start(xr[:, G % 2, :], xv[:, b, G, :]).then_inc(r_in[G % 2], 16)
                            sp.dma_start(cr[:, G % 2, :], cv[:, b, G, :]).then_inc(r_in[G % 2], 16)

                def coming(m, n):
                    if n == 0:
                        sp.wait_ge(v_mm, m + 1)
                        sp.dma_start(f[:], cb[:, m, :]).then_inc(f_in, 16)
                    if n == M_AT:
                        sp.wait_ge(m_stored, m * 16 + 32)
                        for k in range(2):
                            sp.wait_ge(row_split, m * 2 + k + 1)
                            for r0 in range(PARTS):
                                src = m_dram[m:m + 1] if isinstance(m, int) else m_dram[bass.ds(m, 1)]
                                sp.dma_start(m_row[MROW + r0:MROW + r0 + 1, k, :], src[:, k * MH:(k + 1) * MH]
                                             ).then_inc(m_in[k], 16)

                batches(sp, values, coming)

            @block.gpsimd
            def _(pool):
                pool.wait_ge(w_in, NW)
                pool.tensor_copy(identb[:], ident[:]).then_inc(ready, 1)
                pool.tensor_copy(mask[:], mk[:]).then_inc(ready, 1)
                pool.memset(vc[:, :, DV:2 * DV], 0.0).then_inc(ready, 1)
                pool.memset(vc[:, :, 2 * DV:3 * DV], 1.0).then_inc(ready, 1)
                pool.wait_ge(ready, READY)
                with pool.Fori(0, B) as b:
                    pool.wait_ge(pv_mm, b * NI + NI)
                    pool.wait_ge(v_done, b + 2)
                    hold(pool, passed)
                    pool.tensor_copy(vc[:, :, 0:DV], va[:, b]).then_inc(vc_done, 1)

            @block.tensor
            def _(pe):
                pe.sem_inc(v_mm, 1)
                pe.sem_inc(pv_mm, NI)
                pe.wait_ge(w_in, NW)
                pe.matmul(pm[0:DV, 0:P], fold[:], w3[:], start=True, stop=True).then_inc(fold_mm, 1)
                pe.wait_ge(fold_done, 1)
                pe.wait_ge(ready, READY)

                def scores(b, n):
                    G, kt = items[n]
                    c0 = max(0, kt - 4 * G) * P
                    diag = kt >= 4 * G
                    pe.wait_ge(exped, b * NI + n + 1)
                    if n == 0:
                        pe.wait_ge(row_split, b * 2 + 4)
                    mm = pe.matmul(sc[:, n % NS, c0:], ks[:, b, kt * P:(kt + 1) * P],
                                   qs[:, b, G * BANK + c0:(G + 1) * BANK], start=True, stop=not diag)
                    if diag:
                        mm = pe.matmul(sc[:, n % NS, c0:c0 + P], identb[:], mask[:, 1, :], start=False, stop=True)
                    mm.then_inc(sc_mm, 1)

                def weigh(b, n):
                    G, kt = items[n]
                    c0 = max(0, kt - 4 * G) * P
                    if n == 0:
                        pe.wait_ge(vc_done, b + 1)
                    if kt == 0:
                        pe.wait_ge(at_done, b * GT + G + 1)
                    pe.wait_ge(exped, b * NI + n + 1 + NS)
                    pe.matmul(po[0:48, G % 2, c0:], vc[:, kt, :], e[:, n % NE, c0:], start=(kt == 0),
                              stop=(kt == 4 * G + 3)).then_inc(pv_mm, 1)

                def values(b, n):
                    if n < NI:
                        scores(b, n)
                    if LAG <= n < NI + LAG:
                        weigh(b, n - LAG)
                    for G in range(GT):
                        if n == NORM[G] + PROJ:
                            pe.wait_ge(at_done, b * GT + G + 3)
                            pe.wait_ge(o1_done, b * GT + G + 1)
                            pe.matmul(pm[:], w3s[:], at[:], start=True, stop=True).then_inc(proj_mm, 1)

                def coming(m, n):
                    t = split_at(n)
                    if t is not None:
                        if t == 0:
                            pe.wait_ge(f_in, m * 16 + 16)
                            pe.wait_ge(mt_done, m + 1)
                        else:
                            pe.wait_ge(qf_done, m * GT + t)
                        pe.matmul(pq[:], wqk[:], f[:, t * BANK:(t + 1) * BANK], start=True, stop=True
                                  ).then_inc(qk_mm, 1)
                    if n in V_PARTS:
                        quarter = V_PARTS.index(n)
                        if quarter == 0:
                            pe.wait_ge(qf_done, m * GT + GT)
                        for k in range(quarter * NT // 4, (quarter + 1) * NT // 4):
                            mm = pe.matmul(pq[:, k * DV:(k + 1) * DV], f[:, k * P:(k + 1) * P], wv[:], start=True,
                                           stop=True, skip_group_check=True)
                        if quarter == 3:
                            mm.then_inc(v_mm, 1)
                    for u in units_at(n):
                        i, k = units[u]
                        if k == 0 and i % 4 == 0:
                            pe.wait_ge(split, m * (2 * GT) + 2 * (i // 4 + 1) + 4)
                        pe.wait_ge(maxed, m * NU + u + 1)
                        diag = k == i // 4
                        wid = (i % 4 + 1) * P if diag else BANK
                        mm = pe.matmul(pu[:, u % 2, 0:wid], qs[:, m, i * P:(i + 1) * P],
                                       ks[:, m, k * BANK:k * BANK + wid], start=True, stop=not diag,
                                       skip_group_check=True)
                        if diag:
                            mm = pe.matmul(pu[:, u % 2, wid - P:wid], identb[:], mask[:, 0, :],
                                           start=False, stop=True, skip_group_check=True)
                        mm.then_inc(unit_mm, 1)
                    if n == M_AT:
                        pe.wait_ge(m_done, m + 1)
                        pe.wait_ge(v_done, m + 2)
                        pe.transpose(pq[0:NT, 0:P], mall[:], ident[:]).then_inc(mt_mm, 1)

                batches(pe, values, coming)

            @block.scalar
            def _(act):
                act.sem_inc(mt_done, 1)
                act.sem_inc(m_stored, 16)
                act.sem_inc(exped, NS)
                for k in range(2):
                    act.sem_inc(stored[k], 16)
                act.wait_ge(w_in, NW)
                act.wait_ge(fold_mm, 1)
                act.activation(w3s[:], pm[0:DV, 0:P], ACT.Copy).then_inc(fold_done, 1)

                def values(b, n):
                    if n < NI:
                        G, kt = items[n]
                        c0 = max(0, kt - 4 * G) * P
                        act.wait_ge(sc_mm, b * NI + n + 1)
                        act.wait_ge(pv_mm, b * NI + n + 1 + NI - NE)
                        act.activation(e[:, n % NE, c0:], sc[:, n % NS, c0:], ACT.Exp, scale=1.0 / float(np.sqrt(P // 8))
                                       ).then_inc(exped, 1)
                    for G in range(GT):
                        if n == NORM[G] + STORE:
                            act.wait_ge(o2_done, b * GT + G + 1 + 2)
                            act.dma_start(tv[:, b, G, :], o2[:, G % 2, :]).then_inc(stored[G % 2], 16)

                def coming(m, n):
                    t = split_at(n)
                    if t is not None:
                        act.wait_ge(qk_mm, m * GT + t + 1)
                        act.wait_ge(split, m * (2 * GT) + 2 * t + 2)
                        act.activation(qf[:, t % 2, :], pq[:], ACT.Identity, bias=bqk[:, 0:1]).then_inc(qf_done, 1)
                        act.wait_ge(qf_done, m * GT + t + 1)
                        act.activation(h1[:, t % 2, :], qf[:, t % 2, :], ACT.Copy).then_inc(h1_done, 1)
                    t = split_at(n, 2)
                    if t is not None:
                        act.wait_ge(r1_done, m * GT + t + 1)
                        act.activation(h2[:, t % 2, :], r1[:, t % 2, :], ACT.Copy).then_inc(h2_done, 1)
                    if n == M_AT:
                        act.wait_ge(mt_mm, m + 1)
                        act.wait_ge(m_stored, m * 16 + 16)
                        act.activation(mt[:], pq[0:NT, 0:P], ACT.Copy).then_inc(mt_done, 1)
                        act.wait_ge(mt_done, m + 2)
                        dst = m_dram[m:m + 1] if isinstance(m, int) else m_dram[bass.ds(m, 1)]
                        act.dma_start(dst.rearrange("o (t q) -> (o t) q", q=P), mt[:]).then_inc(m_stored, 16)
                    for k in range(2):
                        if n == R_AT + k:
                            act.wait_ge(m_in[k], m * (16 * PARTS) + 16 * PARTS)
                            act.wait_ge(row_split, m * 2 + k + 1)
                            act.activation(m_h[rows, k], m_row[rows, k], ACT.Copy).then_inc(mh_done, 1)
                    for k in range(2):
                        if n == R_AT + 3 + k:
                            act.wait_ge(mr_done, m * 2 + k + 1)
                            act.activation(m_h[rows, k], m_r[rows, k], ACT.Copy).then_inc(mh2_done, 1)

                batches(act, values, coming)
                act.wait_ge(m_stored, 16 * (B + 1))
                for k in range(2):
                    act.wait_ge(stored[k], 16 * (B * GT // 2 + 1))

            @block.vector
            def _(v):
                v.memset(ks[rows], -1.0).then_inc(ready, 1)
                v.memset(qs[rows], 0.0).then_inc(ready, 1)
                v.memset(mp[:], MASK2).then_inc(ready, 1)
                for sem, credit in ((v_done, 1), (maxed, 2), (split, 4), (row_split, 2), (at_done, 2), (o1_done, 1),
                                    (o2_done, 2)):
                    v.sem_inc(sem, credit)
                v.wait_ge(w_in, NW)
                v.wait_ge(ready, READY)

                def values(b, n):
                    for G in range(GT):
                        if n == NORM[G]:
                            v.wait_ge(pv_mm, b * NI + first[G + 1] + NI)
                            v.tensor_scalar(den[:], po[32:48, G % 2, :], 1e-10, None, ALU.add).then_inc(den_done, 1)
                        for j in range(4):
                            if n == NORM[G] + j:
                                v.wait_ge(den_done, b * GT + G + 1)
                                sl = slice(j * P, (j + 1) * P)
                                v.reciprocal(rec[:, sl], den[:, sl]).then_inc(rec_done, 1)
                        if n == NORM[G] + AT:
                            v.wait_ge(rec_done, b * (4 * GT) + 4 * G + 4)
                            if G:
                                v.wait_ge(proj_mm, b * GT + G)
                            v.tensor_tensor(at[:], po[0:DV, G % 2, :], rec[:], ALU.mult).then_inc(at_done, 1)
                        if n == NORM[G] + RES:
                            v.wait_ge(proj_mm, b * GT + G + 1)
                            v.wait_ge(r_in[G % 2], b * (32 * GT // 2) + (G // 2) * 32 + 32)
                            v.wait_ge(o2_done, b * GT + G + 2)
                            v.scalar_tensor_tensor(o1[:], pm[:], b3[:, 0:1], cr[:, G % 2, :], ALU.add, ALU.add
                                                   ).then_inc(o1_done, 1)
                            v.wait_ge(o1_done, b * GT + G + 2)
                            v.wait_ge(stored[G % 2], b * (16 * GT // 2) + (G // 2) * 16 + 16)
                            v.tensor_tensor(o2[:, G % 2, :], o1[:], xr[:, G % 2, :], ALU.add).then_inc(o2_done, 1)

                def coming(m, n):
                    t = split_at(n, 1)
                    if t is not None:
                        v.wait_ge(h1_done, m * GT + t + 1)
                        v.scalar_tensor_tensor(r1[:, t % 2, :], h1[:, t % 2, :], sel[:, 0:1], qf[:, t % 2, :],
                                               ALU.mult, ALU.add).then_inc(r1_done, 1)
                    k = split_at(n, 3)
                    if k is not None:
                        v.wait_ge(h2_done, m * GT + k + 1)
                        for dst, p0 in ((qs, 0), (ks, 64)):
                            v.scalar_tensor_tensor(dst[0:64, m, k * BANK:(k + 1) * BANK],
                                                   h2[p0:p0 + 64, k % 2, :], sel[p0:p0 + 64, 1:2],
                                                   r1[p0:p0 + 64, k % 2, :], ALU.mult, ALU.add).then_inc(split, 1)
                    if n == V_AT:
                        v.wait_ge(v_mm, m + 2)
                        v.tensor_tensor(va[:, m], pq[:].rearrange("p (t d) -> p t d", d=DV),
                                        bv[:].unsqueeze(1).broadcast_to((P, NT, DV)), ALU.add).then_inc(v_done, 1)
                    for u in units_at(n):
                        i, k = units[u]
                        v.wait_ge(unit_mm, m * NU + u + 1)
                        wid = (i % 4 + 1) * P if k == i // 4 else BANK
                        v.tensor_reduce(mp[:, i, k:k + 1], pu[:, u % 2, 0:wid], AX.X, ALU.max).then_inc(maxed, 1)
                    if n == M_AT:
                        v.wait_ge(maxed, m * NU + NU + 2)
                        v.wait_ge(mt_done, m + 1)
                        v.tensor_reduce(mall[:], mp[:], AX.X, ALU.max).then_inc(m_done, 1)
                    for k in range(2):
                        if n == R_AT + 1 + k:
                            v.wait_ge(mh_done, m * 2 + k + 1)
                            v.scalar_tensor_tensor(m_r[rows, k], m_h[rows, k], sel[rows, 2:3], m_row[rows, k],
                                                   ALU.mult, ALU.add).then_inc(mr_done, 1)
                    for k in range(2):
                        if n == R_AT + 4 + k:
                            v.wait_ge(mh2_done, m * 2 + k + 1)
                            v.scalar_tensor_tensor(qs[rows, m, k * MH:(k + 1) * MH], m_h[rows, k], sel[rows, 3:4],
                                                   m_r[rows, k], ALU.mult, ALU.add).then_inc(row_split, 1)

                batches(v, values, coming)


class Signal:

    def __init__(self, sem, per):
        self.sem, self.per = sem, per

    def credit(self, eng):
        eng.sem_inc(self.sem, self.per)

    def now(self, eng, it, k):
        eng.wait_ge(self.sem, it * self.per + (self.per + k))

    def before(self, eng, it, k):
        eng.wait_ge(self.sem, it * self.per + k)


def mamba_constants():
    r = np.arange(P)
    upto = (r[:, None] <= r[None, :]).astype(np.float32)
    after = (r[:, None] > r[None, :]).astype(np.float32)
    return {"c_tri": np.stack([upto, after, np.ones((P, P), np.float32)], 1),
            "c_pick": np.tile(np.eye(2 * B * NH, dtype=np.float32), (2, 1)),
            "c_flip": np.ascontiguousarray(np.eye(P, dtype=np.float32)[::-1]),
            "c_causal": np.tile(np.where(r[:, None] > r[None, :], MASK1, 0.0).astype(np.float32), (1, NH))}


def mamba(nc, sems, g, hn, outs):
    s = Scope(nc, sems, "mb")
    with s.stack:
        step = {n: s.sb(n, [P, 2, NCH, B * NH]) for n in ("dt", "nacs", "eacs", "dec", "etot")}
        step["rows"] = s.sb("rows", [4 * B * NH, T], F32R)
        mamba_steps(nc, sems, g, hn, step)
        mamba_scan(nc, sems, g, hn, step, outs)


def mamba_steps(nc, sems, g, hn, st):
    s = Scope(nc, sems, "ms")
    W = NCH * B * NH
    with s.stack:
        wdt = s.sb("wdt", [P, 2 * NH])
        bias = s.sb("bias", [P, 2, NH])
        alog = s.sb("alog", [P, 2, NH])
        aneg = s.sb("aneg", [P, 2, NH])
        tri = s.sb("tri", [P, 3, P])
        flip = s.sb("flip", [P, P])
        h = s.sb("h", [P, 2, T])
        raw = s.sb("raw", [P, 2, NCH, B, NH])
        x = s.sb("x", [P, 2, W])
        ax = s.sb("ax", [P, 2, W])
        ex = s.sb("ex", [P, 2, W])
        lg = s.sb("lg", [P, 2, W])
        da = s.sb("da", [P, NCH, 2, B * NH])
        NR = 2 * B * NH
        pd = s.ps("pd", [P, 2, BANK])
        pf = s.ps("pf", [P, BANK])
        pc = s.ps("pc", [P, 5, BANK])
        w_in, dt_mm, gathered, flip_mm, step, exp_done, sum_mm, sum_exp, dec_done, row_mm, row_high, row_low = (
            s.sem(n) for n in ("w_in", "dt_mm", "gathered", "flip_mm", "step", "exp_done", "sum_mm", "sum_exp",
                               "dec_done", "row_mm", "row_high", "row_low"))
        h_in = [s.sem(f"h_in{k}") for k in range(2)]
        hv = hn.rearrange("p (b n) -> p b n", b=B)
        with nc.Block() as block:

            @block.sync
            def _(sp):
                for dst, name in ((wdt, "Wdt"), (bias, "dt_bias"), (alog, "A_log"), (tri, "c_tri"), (flip, "c_flip")):
                    sp.dma_start(dst[:], g[name]).then_inc(w_in, 16)
                with sp.Fori(0, B // 2) as i:
                    for k in range(2):
                        sp.wait_ge(dt_mm, i * 2 + k + 1)
                        sp.dma_start(h[:, k], hv[:, i * 2 + k, :]).then_inc(h_in[k], 16)

            @block.tensor
            def _(pe):
                pe.sem_inc(dt_mm, 2)
                pe.wait_ge(w_in, 80)
                with pe.Fori(0, B // 2) as i:
                    for k in range(2):
                        pe.wait_ge(h_in[k], i * 16 + 16)
                        pe.wait_ge(gathered, i * 2 + k + 1)
                        for c in range(NCH):
                            mm = pe.matmul(pd[:, k, c * 2 * NH:(c + 1) * 2 * NH], h[:, k, c * P:(c + 1) * P], wdt[:],
                                           start=True, stop=True, skip_group_check=True)
                        mm.then_inc(dt_mm, 1)
                pe.wait_ge(gathered, B + 2)
                pe.matmul(pf[:], flip[:], raw[:, 1].rearrange("p c b h -> p (c b h)"), start=True, stop=True
                          ).then_inc(flip_mm, 1)
                pe.wait_ge(dec_done, 1)
                for d in range(2):
                    for k in range(3):
                        n = 3 * d + k
                        if n == 5:
                            pe.wait_ge(sum_exp, 2)
                        pe.matmul(pc[:, n % 5, :], tri[:, k, :], da[:, :, d, :], start=True, stop=True
                                  ).then_inc(sum_mm, 1)
                for r in range(NCH // 4):
                    if r >= 2:
                        pe.wait_ge(row_low, r - 1)
                    for c in range(4):
                        mm = pe.matmul(pd[0:NR, r % 2, c * CH:(c + 1) * CH],
                                       da[:, 4 * r + c].rearrange("p d n -> p (d n)"), tri[:, 0, :], start=True,
                                       stop=True, skip_group_check=True)
                    mm.then_inc(row_mm, 1)

            @block.scalar
            def _(act):
                act.wait_ge(step, 3)
                act.activation(ex[:].rearrange("p d n -> p (d n)"), ax[:].rearrange("p d n -> p (d n)"), ACT.Exp,
                               scale=-1.0).then_inc(exp_done, 1)
                act.wait_ge(w_in, 80)
                act.activation(aneg[:].rearrange("p d n -> p (d n)"), alog[:].rearrange("p d n -> p (d n)"), ACT.Exp
                               ).then_inc(exp_done, 1)
                act.wait_ge(exp_done, 2)
                act.activation(lg[:].rearrange("p d n -> p (d n)"), ex[:].rearrange("p d n -> p (d n)"), ACT.Ln,
                               bias=1.0).then_inc(exp_done, 1)
                for d in range(2):
                    for k in range(3):
                        n = 3 * d + k
                        act.wait_ge(sum_mm, n + 1)
                        if k == 0:
                            act.activation(st["nacs"][:, d].rearrange("p c n -> p (c n)"), pc[:, n % 5, :], ACT.Copy,
                                           scale=-1.0).then_inc(sum_exp, 1)
                        dst = (st["eacs"][:, d].rearrange("p c n -> p (c n)"), st["dec"][:, d].rearrange("p c n -> p (c n)"),
                               st["etot"][:, d].rearrange("p c n -> p (c n)"))[k]
                        act.activation(dst, pc[:, n % 5, :], ACT.Exp).then_inc(sum_exp, 1)
                for r in range(NCH // 4):
                    act.wait_ge(row_mm, r + 1)
                    act.activation(st["rows"][0:NR, r * BANK:(r + 1) * BANK], pd[0:NR, r % 2, :], ACT.Copy
                                   ).then_inc(row_high, 1)

            @block.vector
            def _(v):
                v.sem_inc(gathered, 2)
                with v.Fori(0, B // 2) as i:
                    for k in range(2):
                        v.wait_ge(dt_mm, i * 2 + k + 3)
                        v.tensor_copy(raw[:, :, :, i * 2 + k, :],
                                      pd[:, k, 0:2 * NH * NCH].rearrange("p (c d h) -> p d c h", d=2, h=NH)
                                      ).then_inc(gathered, 1)
                v.wait_ge(w_in, 80)
                v.wait_ge(gathered, B + 2)
                v.tensor_tensor(x[:, 0].rearrange("p (n h) -> p n h", h=NH),
                                raw[:, 0].rearrange("p c b h -> p (c b) h"),
                                bias[:, 0].unsqueeze(1).broadcast_to((P, NCH * B, NH)), ALU.add).then_inc(step, 1)
                v.wait_ge(flip_mm, 1)
                v.tensor_tensor(x[:, 1].rearrange("p (c b h) -> p c b h", b=B, h=NH),
                                pf[:].rearrange("p (c b h) -> p c b h", b=B, h=NH)[:, ::-1],
                                bias[:, 1].unsqueeze(1).unsqueeze(1).broadcast_to((P, NCH, B, NH)), ALU.add
                                ).then_inc(step, 1)
                v.wait_ge(step, 2)
                v.scalar_tensor_tensor(ax[:], x[:], -1.0, x[:], ALU.mult, ALU.max).then_inc(step, 1)
                v.wait_ge(exp_done, 3)
                dtf = st["dt"][:].rearrange("p d c n -> p d (c n)")
                v.scalar_tensor_tensor(dtf, x[:], 0.0, lg[:], ALU.max, ALU.add).then_inc(step, 1)
                v.wait_ge(step, 4)
                for d in range(2):
                    for b in range(B):
                        hs = slice(b * NH, (b + 1) * NH)
                        v.scalar_tensor_tensor(da[:, :, d, hs], st["dt"][:, d, :, hs], -1.0,
                                               aneg[:, d].unsqueeze(1).broadcast_to((P, NCH, NH)),
                                               ALU.mult, ALU.mult).then_inc(step, 1)
                v.wait_ge(step, 4 + 2 * B)
                v.sem_inc(dec_done, 1)
                for r in range(NCH // 4):
                    v.wait_ge(row_high, r + 1)
                    sl = slice(r * BANK, (r + 1) * BANK)
                    low_part(v, st["rows"][NR:2 * NR, sl], pd[0:NR, r % 2, :], st["rows"][0:NR, sl]
                             ).then_inc(row_low, 1)


def mamba_scan(nc, sems, g, hn, st, outs):
    s = Scope(nc, sems, "mm")
    XB = 3
    H2 = B // 2
    PER = dict(xin=16, xc=2, halo=1, proj=3, evac=6, zmm=2, thz=2, zs=2, lmm=4, lexp=16, taps=9, th=3, silu=4,
               gmm=1, w=4, xtmm=2, btmm=1, bt=1, xd=2, xdd=2, yomm=2, ydmm=2, y=2, yadd=2, gate=2, stmm=2, stmp=1,
               st=2, sq=4, rs1=1, rs=1, yn=4, ytmm=2, yta=2, omm=1, ob=1, stored=16)
    FROM = dict(scalar="evac thz lexp th bt sq yn yta ob stored", vector="taps zs silu w xd y yadd st",
                tensor="proj zmm lmm gmm xtmm btmm yomm ydmm stmm ytmm omm", gpsimd="xc halo xdd gate stmp rs1 rs",
                sync="xin")
    with s.stack:
        identb = s.sb("identb", [P, P], BF16)
        ident = s.sb("ident", [P, P])
        cm = s.sb("cm", [P, NH * P])
        cmb = s.sb("cmb", [P, NH * P], BF16)
        pick_in = s.sb("pick_in", [4 * B * NH, 2 * B * NH])
        pick = s.sb("pick", [4 * B * NH, 2 * B * NH], F32R)
        nhalf = s.sb("nhalf", [P, B])
        D = []
        for d in range(2):
            t = {n: s.sb(f"{n}{d}", shape) for n, shape in (
                ("cw", [P, XB, TAPS]), ("cb", [P, XB]), ("dcol", [P, 2]),
                ("nw", [P, 2]), ("dg", [P, 2, P]), ("wo", [P, 2, P]),
                ("xin", [P, B, CH]), ("raw", [P, XB, B, CH + TAPS - 1]),
                ("acc", [P, XB, B, CH]), ("th", [P, XB, B, CH]), ("xs", [P, 2, B, CH]), ("bs", [DS, B, CH]),
                ("cs", [DS, B, CH]), ("L", [P, B, NH, CH]), ("xdt", [P, B, NH, HD]), ("xdd", [P, B, NH, HD]),
                ("bt", [P, B, DS]), ("state", [DS, B, DI]), ("stmp", [DS, B, DI]), ("zs", [P, B, DI]),
                ("y", [P, B, DI]), ("yn", [P, B, DI]), ("yt", [P, 2, B, CH]), ("ob", [P, B, CH]),
                ("ssq", [P, B]), ("rs", [P, B]))}
            t["wi"] = t["L"][:].rearrange("p b h n -> p (b h n)")[:, 0:2 * DI + 2 * DS]
            t["wp"] = s.sb(f"wp{d}", [P, 2, 2 * DI + 2 * DS], F32R)
            t["xc"] = s.sb(f"xc{d}", [P, 2, B, CH], F32R)
            for n in "ABCD":
                t[n] = s.ps(f"{n}{d}", [P, BANK])
            t["sig"] = {n: Signal(s.sem(f"{n}{d}"), per) for n, per in PER.items()}
            D.append(t)
        w_in, ready, passed_sp, passed_pool, passed_pe = (
            s.sem(n) for n in ("w_in", "ready", "passed_sp", "passed_pool", "passed_pe"))
        hv = hn.rearrange("p (b c n) -> p b c n", b=B, n=CH)
        ov = [o.rearrange("p (b c n) -> p b c n", b=B, n=CH) for o in outs]
        DMAS = 3 + 2 * 6
        WEIGHTS = 4 + 2 * 9
        READY = WEIGHTS + 2 * 2

        def credits(eng, name):
            for t in D:
                for n in FROM[name].split():
                    t["sig"][n].credit(eng)

        def run(stage, at, *more):
            it, d = at
            stage(it, d, D[d], D[d]["sig"], *more)

        def halves(eng, half):
            half(None, None, (0, 0))
            half((0, 0), None, (0, 1))
            with eng.Fori(0, NCH - 1) as it:
                half((it, 1), (it, 0), (it + 1, 0))
                half((it + 1, 0), (it, 1), (it + 1, 1))
            half((NCH - 1, 1), (NCH - 1, 0), None)
            half(None, (NCH - 1, 1), None)

        def spread(ap, it, d, k):
            return ap[:, d, it, k * H2 * NH:(k + 1) * H2 * NH].unsqueeze(2).broadcast_to((P, H2 * NH, HD))

        def chunk(it, d):
            return it if d == 0 else (NCH - 1) - it

        with nc.Block() as block:

            @block.sync
            def _(sp):
                sp.dma_start(ident[:], g["c_ident"]).then_inc(w_in, 16)
                sp.dma_start(cm[:], g["c_causal"]).then_inc(w_in, 16)
                sp.dma_start(pick_in[:], g["c_pick"]).then_inc(w_in, 16)
                for d, t in enumerate(D):
                    for n, name in (("wi", "in_proj"), ("cw", "conv_w"), ("cb", "conv_b"), ("dcol", "D"), ("nw", "norm_w"),
                                    ("wo", "out_proj")):
                        sp.dma_start(t[n][:], g[f"{name}{d}"]).then_inc(w_in, 16)
                credits(sp, "sync")
                with sp.Fori(0, NCH) as it:
                    for d, t in enumerate(D):
                        t["sig"]["xc"].before(sp, it, 2)
                        hold(sp, passed_sp)
                        sp.dma_start(t["xin"][:], hv[:, :, chunk(it, d), :]).then_inc(t["sig"]["xin"].sem, 16)

            @block.gpsimd
            def _(pool):
                pool.wait_ge(w_in, 16 * DMAS)
                pool.tensor_copy(identb[:], ident[:]).then_inc(ready, 1)
                pool.tensor_copy(cmb[:], cm[:]).then_inc(ready, 1)
                pool.memset(nhalf[:], -0.5).then_inc(ready, 1)
                pool.tensor_copy(pick[:], pick_in[:]).then_inc(ready, 1)
                for t in D:
                    pool.memset(t["raw"][:], 0.0).then_inc(ready, 1)
                    pool.memset(t["state"][:], 0.0).then_inc(ready, 1)
                    for k in range(2):
                        pool.tensor_scalar(t["dg"][:, k, :], ident[:], t["dcol"][:, k:k + 1], None, ALU.mult
                                           ).then_inc(ready, 1)
                        pool.tensor_scalar(t["wo"][:, k, :], t["wo"][:, k, :], t["nw"][:, k:k + 1], None, ALU.mult
                                           ).then_inc(ready, 1)
                    pool.tensor_scalar(t["wi"][:, 0:DI], t["wi"][:, 0:DI], 0.5, None, ALU.mult).then_inc(ready, 1)
                    pool.tensor_scalar(t["cw"][:], t["cw"][:], 0.5, None, ALU.mult).then_inc(ready, 1)
                    pool.tensor_scalar(t["cb"][:], t["cb"][:], 0.5, None, ALU.mult).then_inc(ready, 1)
                pool.wait_ge(ready, WEIGHTS)
                for d, t in enumerate(D):
                    pool.tensor_copy(t["wp"][:, 0], t["wi"][:]).then_inc(ready, 1)
                    pool.wait_ge(ready, WEIGHTS + 2 * d + 1)
                    low_part(pool, t["wp"][:, 1], t["wi"][:], t["wp"][:, 0]).then_inc(ready, 1)
                credits(pool, "gpsimd")
                pool.wait_ge(ready, READY)

                def copy_in(it, d, t, S):
                    S["xin"].now(pool, it, 16)
                    S["zmm"].before(pool, it, 2)
                    hold(pool, passed_pool)
                    x = t["xin"][:] if d == 0 else t["xin"][:, :, ::-1]
                    pool.tensor_copy(t["xc"][:, 0], x).then_inc(S["xc"].sem, 1)
                    S["xc"].now(pool, it, 1)
                    low_part(pool, t["xc"][:, 1], x, t["xc"][:, 0]).then_inc(S["xc"].sem, 1)

                def halo(it, d, t, S):
                    S["taps"].now(pool, it, 9)
                    hold(pool, passed_pool)
                    pool.tensor_copy(t["raw"][:, :, :, 0:TAPS - 1].rearrange("p x b n -> p (x b) n"),
                                     t["raw"][:, :, :, CH:CH + TAPS - 1].rearrange("p x b n -> p (x b) n")
                                     ).then_inc(S["halo"].sem, 1)

                def decayed_state(it, d, t, S):
                    S["st"].before(pool, it, 2)
                    pool.tensor_tensor(t["stmp"][:].rearrange("p b (h e) -> p (b h) e", h=NH),
                                       t["state"][:].rearrange("p b (h e) -> p (b h) e", h=NH),
                                       st["etot"][0:DS, d, it, :].unsqueeze(2).broadcast_to((DS, B * NH, HD)),
                                       ALU.mult).then_inc(S["stmp"].sem, 1)

                def into_state(it, d, t, S, k):
                    S["xd"].now(pool, it, k + 1)
                    sl = slice(k * H2, (k + 1) * H2)
                    pool.tensor_tensor(t["xdd"][:, sl].rearrange("p b h e -> p (b h) e"),
                                       t["xdt"][:, sl].rearrange("p b h e -> p (b h) e"), spread(st["dec"], it, d, k),
                                       ALU.mult).then_inc(S["xdd"].sem, 1)

                def gates(it, d, t, S):
                    for k in range(2):
                        S["yadd"].now(pool, it, k + 1)
                        S["zs"].now(pool, it, k + 1)
                        sl = slice(k * H2, (k + 1) * H2)
                        pool.tensor_tensor(t["y"][:, sl], t["y"][:, sl], t["zs"][:, sl], ALU.mult
                                           ).then_inc(S["gate"].sem, 1)

                def norms(it, d, t, S):
                    S["sq"].now(pool, it, 4)
                    hold(pool, passed_pool)
                    pool.tensor_scalar(t["rs"][:], t["ssq"][:], 1.0 / DI, 1e-5, ALU.mult, ALU.add
                                       ).then_inc(S["rs1"].sem, 1)
                    S["rs1"].now(pool, it, 1)
                    pool.tensor_tensor(t["rs"][:], t["rs"][:], nhalf[:], ALU.pow).then_inc(S["rs"].sem, 1)

                def half(front, back, coming):
                    if coming:
                        run(copy_in, coming)
                    if back:
                        run(decayed_state, back)
                        run(gates, back)
                    if front:
                        run(halo, front)
                    if back:
                        run(norms, back)
                    if front:
                        run(into_state, front, 0)
                        run(into_state, front, 1)

                halves(pool, half)

            @block.tensor
            def _(pe):
                credits(pe, "tensor")
                pe.wait_ge(w_in, 16 * DMAS)
                pe.wait_ge(ready, READY)

                def flat(ap):
                    return ap.rearrange("p b n -> p (b n)")

                def project(it, d, t, S, tiles):
                    S["xc"].now(pe, it, 2)
                    for k in tiles:
                        free, cnt = (("st", 1), ("st", 2), ("yta", 1))[k]
                        S[free].before(pe, it, cnt)
                        product(pe, t["BAC"[k]][:],
                                [t["wp"][:, part, DI + k * P:DI + (k + 1) * P] for part in range(2)],
                                [flat(t["xc"][:, part]) for part in range(2)], start=True, stop=True
                                ).then_inc(S["proj"].sem, 1)

                def gate(it, d, t, S, k):
                    if k == 0:
                        S["ob"].before(pe, it, 1)
                    else:
                        S["zs"].now(pe, it, 1)
                    for j in range(2):
                        mm = product(pe, t["D"][:, j * DI:(j + 1) * DI],
                                     [t["xc"][:, part, 2 * k + j, :] for part in range(2)],
                                     [t["wp"][:, part, 0:DI] for part in range(2)], start=True, stop=True,
                                     skip_group_check=True)
                    mm.then_inc(S["zmm"].sem, 1)

                def decay(it, d, t, S, b):
                    if b < 2:
                        S["evac"].now(pe, it, (2, 4)[b])
                    else:
                        S["lexp"].now(pe, it, NH * (b - 1))
                    bank = t["BA"[b % 2]]
                    pe.matmul(bank[:], identb[:], cmb[:], start=True, stop=False, skip_group_check=True)
                    for h in range(NH):
                        n = b * NH + h
                        n += d * B * NH
                        mm = pe.matmul(bank[:, h * P:(h + 1) * P], pick[:, n:n + 1].broadcast_to((4 * B * NH, P)),
                                       st["rows"][:, bass.ds(it * CH, CH)] if not isinstance(it, int) else
                                       st["rows"][:, it * CH:(it + 1) * CH], start=False, stop=(h == NH - 1), skip_group_check=True)
                    mm.then_inc(S["lmm"].sem, 1)

                def b_times_c(it, d, t, S):
                    S["silu"].now(pe, it, 4)
                    S["evac"].now(pe, it, 6)
                    for b in range(B):
                        mm = pe.matmul(t["C"][:, b * P:(b + 1) * P], t["bs"][:, b, :], t["cs"][:, b, :], start=True,
                                       stop=True, skip_group_check=True)
                    mm.then_inc(S["gmm"].sem, 1)

                def turn_b(it, d, t, S):
                    S["silu"].now(pe, it, 3)
                    S["zs"].now(pe, it, 2)
                    hold(pe, passed_pe)
                    for b in range(B):
                        mm = pe.transpose(t["D"][:, b * DS:(b + 1) * DS], t["bs"][:, b, :], ident[0:DS, 0:DS])
                    mm.then_inc(S["btmm"].sem, 1)

                def turn_x(it, d, t, S, k):
                    S["silu"].now(pe, it, 2)
                    S["lexp"].now(pe, it, 12 + 4 * k)
                    for j in range(2):
                        for x in range(2):
                            mm = pe.transpose(t["BA"[k]][:, (2 * j + x) * P:(2 * j + x + 1) * P],
                                              t["xs"][:, x, 2 * k + j, :], ident[:])
                    mm.then_inc(S["xtmm"].sem, 1)

                def from_state(it, d, t, S, k):
                    S["st"].before(pe, it, 2)
                    S["xd"].now(pe, it, k + 1)
                    for j in range(2):
                        mm = pe.matmul(t["BA"[k]][:, j * DI:(j + 1) * DI], t["cs"][:, 2 * k + j, :],
                                       t["state"][:, 2 * k + j, :], start=True, stop=True, skip_group_check=True)
                    mm.then_inc(S["yomm"].sem, 1)

                def from_chunk(it, d, t, S, k):
                    S["w"].now(pe, it, 4)
                    if k == 1:
                        S["bt"].now(pe, it, 1)
                    bank = t["CD"[k]]
                    for j in range(2):
                        b = 2 * k + j
                        for x in range(2):
                            o = j * DI + x * P
                            pe.matmul(bank[:, o:o + P], t["xs"][:, x, b, :], t["dg"][:, x, :], start=(x == 0),
                                      stop=False, skip_group_check=True)
                        for h in range(NH):
                            o = j * DI + h * HD
                            mm = pe.matmul(bank[:, o:o + HD], t["L"][:, b, h, :], t["xdt"][:, b, h, :],
                                           start=False, stop=(h == NH - 1), skip_group_check=True)
                    mm.then_inc(S["ydmm"].sem, 1)

                def states(it, d, t, S, k):
                    S["y"].now(pe, it, k + 1)
                    S["xdd"].now(pe, it, k + 1)
                    for j in range(2):
                        b = 2 * k + j
                        mm = pe.matmul(t["BA"[k]][0:DS, j * DI:(j + 1) * DI], t["bt"][:, b, :],
                                       t["xdd"][:, b].rearrange("p h e -> p (h e)"), start=True, stop=True,
                                       skip_group_check=True)
                    mm.then_inc(S["stmm"].sem, 1)

                def turn_back(it, d, t, S, x):
                    S["yn"].now(pe, it, 4)
                    S["yadd"].now(pe, it, x + 1)
                    for b in range(B):
                        mm = pe.transpose(t["CD"[x]][:, b * P:(b + 1) * P], t["yn"][:, b, x * P:(x + 1) * P],
                                          ident[:])
                    mm.then_inc(S["ytmm"].sem, 1)

                def project_out(it, d, t, S):
                    S["yta"].now(pe, it, 2)
                    for x in range(2):
                        mm = pe.matmul(t["D"][:], t["wo"][:, x, :], flat(t["yt"][:, x]), start=(x == 0), stop=(x == 1))
                    mm.then_inc(S["omm"].sem, 1)

                def half(front, back, coming):
                    if front:
                        run(decay, front, 0)
                    if back:
                        run(from_state, back, 0)
                    if front:
                        run(gate, front, 0)
                    if back:
                        run(from_state, back, 1)
                        run(from_chunk, back, 0)
                        run(from_chunk, back, 1)
                    if front:
                        run(decay, front, 1)
                    if back:
                        run(states, back, 0)
                        run(states, back, 1)
                    if front:
                        run(gate, front, 1)
                        run(decay, front, 2)
                        run(decay, front, 3)
                    if coming:
                        run(project, coming, (0, 1))
                    if front:
                        run(turn_x, front, 0)
                        run(turn_x, front, 1)
                        run(b_times_c, front)
                        run(turn_b, front)
                    if back:
                        run(turn_back, back, 0)
                        run(turn_back, back, 1)
                    if coming:
                        run(project, coming, (2,))
                    if back:
                        run(project_out, back)

                halves(pe, half)

            @block.scalar
            def _(act):
                credits(act, "scalar")
                act.wait_ge(w_in, 16 * DMAS)
                act.wait_ge(ready, READY)

                def flat(ap):
                    return ap.rearrange("p b n -> p (b n)")

                def raws(it, d, t, S, tiles):
                    S["halo"].before(act, it, 1)
                    S["silu"].before(act, it, 4)
                    for k in tiles:
                        S["proj"].now(act, it, k + 1)
                        pj = t["BAC"[k]][:].rearrange("p (b n) -> p b n", b=B)
                        act.activation(t["raw"][:, k, :, TAPS - 1:], pj, ACT.Copy).then_inc(S["evac"].sem, 1)
                        act.activation(t["acc"][:, k], pj, ACT.Identity, bias=t["cb"][:, k:k + 1],
                                       scale=t["cw"][:, k, TAPS - 1:TAPS]).then_inc(S["evac"].sem, 1)

                def z_tanh(it, d, t, S, k):
                    S["zmm"].now(act, it, k + 1)
                    S["gate"].before(act, it, 2)
                    act.activation(flat(t["zs"][:, k * H2:(k + 1) * H2]), t["D"][:], ACT.Tanh).then_inc(S["thz"].sem, 1)

                def decays(it, d, t, S, b):
                    S["lmm"].now(act, it, b + 1)
                    S["ydmm"].before(act, it, 2)
                    for h in range(NH):
                        n = b * NH + h
                        act.activation(t["L"][:, b, h, :], t["BA"[b % 2]][:, h * P:(h + 1) * P], ACT.Exp,
                                       bias=st["nacs"][:, d, it, n:n + 1]).then_inc(S["lexp"].sem, 1)

                def tanhs(it, d, t, S, k):
                    S["taps"].now(act, it, (5, 6, 9)[k])
                    act.activation(t["th"][:, k], t["acc"][:, k], ACT.Tanh).then_inc(S["th"].sem, 1)

                def b_tokens(it, d, t, S):
                    S["btmm"].now(act, it, 1)
                    S["stmm"].before(act, it, 2)
                    act.activation(flat(t["bt"][:]), t["D"][:, 0:B * DS], ACT.Copy).then_inc(S["bt"].sem, 1)

                def squares(it, d, t, S, k):
                    S["ytmm"].before(act, it, 2)
                    S["gate"].now(act, it, k + 1)
                    for b in range(k * H2, (k + 1) * H2):
                        act.activation(t["yn"][:, b, :], t["y"][:, b, :], ACT.Square, accum_out=t["ssq"][:, b:b + 1]
                                       ).then_inc(S["sq"].sem, 1)

                def norms(it, d, t, S):
                    S["rs"].now(act, it, 1)
                    for b in range(B):
                        act.activation(t["yn"][:, b, :], t["y"][:, b, :], ACT.Copy, scale=t["rs"][:, b:b + 1]
                                       ).then_inc(S["yn"].sem, 1)

                def turned(it, d, t, S):
                    S["omm"].before(act, it, 1)
                    for x in range(2):
                        S["ytmm"].now(act, it, x + 1)
                        act.activation(flat(t["yt"][:, x]), t["CD"[x]][:], ACT.Copy).then_inc(S["yta"].sem, 1)

                def result(it, d, t, S):
                    S["omm"].now(act, it, 1)
                    S["stored"].before(act, it, 16)
                    dst = t["ob"][:] if d == 0 else t["ob"][:, :, ::-1]
                    act.activation(dst, t["D"][:].rearrange("p (b n) -> p b n", b=B), ACT.Copy).then_inc(S["ob"].sem, 1)
                    S["ob"].now(act, it, 1)
                    act.dma_start(ov[d][:, :, chunk(it, d), :], t["ob"][:]).then_inc(S["stored"].sem, 16)

                def half(front, back, coming):
                    if front:
                        run(tanhs, front, 0)
                        run(z_tanh, front, 0)
                        run(tanhs, front, 1)
                        run(tanhs, front, 2)
                        run(decays, front, 0)
                    if back:
                        run(squares, back, 0)
                    if front:
                        run(decays, front, 1)
                    if back:
                        run(squares, back, 1)
                    if front:
                        run(z_tanh, front, 1)
                        run(decays, front, 2)
                        run(decays, front, 3)
                    if back:
                        run(norms, back)
                        run(turned, back)
                    if coming:
                        run(raws, coming, (0, 1))
                    if back:
                        run(result, back)
                    if coming:
                        run(raws, coming, (2,))
                    if front:
                        run(b_tokens, front)

                halves(act, half)
                for t in D:
                    act.wait_ge(t["sig"]["stored"].sem, 16 * (NCH + 1))

            @block.vector
            def _(v):
                credits(v, "vector")
                v.wait_ge(w_in, 16 * DMAS)
                v.wait_ge(ready, READY)

                def taps(it, d, t, S, tiles):
                    for i in range(TAPS - 1):
                        for n, k in enumerate(tiles):
                            S["evac"].now(v, it, 2 * k + 2)
                            if i:
                                S["taps"].now(v, it, 3 * tiles[0] + (i - 1) * len(tiles) + n + 1)
                            v.scalar_tensor_tensor(t["acc"][:, k], t["raw"][:, k, :, i:i + CH], t["cw"][:, k, i:i + 1],
                                                   t["acc"][:, k], ALU.mult, ALU.add).then_inc(S["taps"].sem, 1)

                def z_silu(it, d, t, S, k):
                    S["thz"].now(v, it, k + 1)
                    zf = t["zs"][:, k * H2:(k + 1) * H2].rearrange("p b n -> p (b n)")
                    v.scalar_tensor_tensor(zf, zf, 1.0, t["D"][:], ALU.add, ALU.mult).then_inc(S["zs"].sem, 1)

                def silus(it, d, t, S, n):
                    S["ydmm"].before(v, it, 2)
                    S["stmm"].before(v, it, 2)
                    dst, k, p0, p1 = ((t["xs"][:, 0], 0, 0, P), (t["xs"][:, 1], 1, 0, P), (t["bs"][:], 2, 0, DS),
                                      (t["cs"][:], 2, DS, 2 * DS))[n]
                    S["th"].now(v, it, k + 1)
                    v.scalar_tensor_tensor(dst, t["th"][p0:p1, k], 1.0, t["acc"][p0:p1, k], ALU.add, ALU.mult
                                           ).then_inc(S["silu"].sem, 1)

                def weights(it, d, t, S, b):
                    S["gmm"].now(v, it, 1)
                    S["lexp"].now(v, it, NH * (b + 1))
                    v.tensor_tensor(t["L"][:, b], t["L"][:, b],
                                    t["C"][:, b * P:(b + 1) * P].unsqueeze(1).broadcast_to((P, NH, P)), ALU.mult
                                    ).then_inc(S["w"].sem, 1)

                def heads(ap):
                    return ap.rearrange("p (n e) -> p n e", e=HD)

                def steps(it, d, t, S, k):
                    S["xtmm"].now(v, it, k + 1)
                    v.tensor_tensor(t["xdt"][:, k * H2:(k + 1) * H2].rearrange("p b h e -> p (b h) e"),
                                    heads(t["BA"[k]][:]), spread(st["dt"], it, d, k), ALU.mult
                                    ).then_inc(S["xd"].sem, 1)

                def decayed(it, d, t, S, k):
                    S["yn"].before(v, it, 4)
                    S["yomm"].now(v, it, k + 1)
                    v.tensor_tensor(t["y"][:, k * H2:(k + 1) * H2].rearrange("p b (h e) -> p (b h) e", e=HD),
                                    heads(t["BA"[k]][:]), spread(st["eacs"], it, d, k), ALU.mult
                                    ).then_inc(S["y"].sem, 1)

                def add_chunk(it, d, t, S, k):
                    S["ydmm"].now(v, it, k + 1)
                    S["y"].now(v, it, k + 1)
                    yf = t["y"][:, k * H2:(k + 1) * H2].rearrange("p b n -> p (b n)")
                    v.tensor_tensor(yf, yf, t["CD"[k]][:], ALU.add).then_inc(S["yadd"].sem, 1)

                def states(it, d, t, S, k):
                    S["stmp"].now(v, it, 1)
                    S["yomm"].now(v, it, 2)
                    S["stmm"].now(v, it, k + 1)
                    sl = slice(k * H2, (k + 1) * H2)
                    v.tensor_tensor(t["state"][:, sl].rearrange("p b n -> p (b n)"),
                                    t["stmp"][:, sl].rearrange("p b n -> p (b n)"), t["BA"[k]][0:DS, :], ALU.add
                                    ).then_inc(S["st"].sem, 1)

                def half(front, back, coming):
                    if back:
                        run(decayed, back, 0)
                    if front:
                        run(taps, front, (2,))
                    if back:
                        run(add_chunk, back, 0)
                        run(decayed, back, 1)
                        run(add_chunk, back, 1)
                    if front:
                        run(z_silu, front, 0)
                    if back:
                        run(states, back, 0)
                        run(states, back, 1)
                    if front:
                        run(silus, front, 0)
                        run(silus, front, 1)
                        run(silus, front, 2)
                        run(z_silu, front, 1)
                        run(silus, front, 3)
                        run(steps, front, 0)
                        run(steps, front, 1)
                        run(weights, front, 0)
                        run(weights, front, 1)
                        run(weights, front, 2)
                        run(weights, front, 3)
                    if coming:
                        run(taps, coming, (0, 1))

                halves(v, half)


def stu_constants():
    a = np.arange(NB)
    ang = 2 * np.pi * np.outer(a, np.arange(NB)) / NF
    re, im = np.cos(ang), -np.sin(ang)
    alt = (-1.0) ** a
    fwd = np.stack([re, im], 1)
    fwd[:, 1, 0] = alt
    dft_u = np.zeros((2, B, NB, 2, 2, NB))
    for b in range(B):
        dft_u[b // 2, b, :, :, b % 2, :] = fwd
    blk = np.zeros((NB, 2, NB, 2))
    blk[:, 0, :, 0], blk[:, 1, :, 0], blk[:, 0, :, 1], blk[:, 1, :, 1] = re, im, -im, re
    blk[:, 1, 0, 0] = blk[:, 0, 0, 1] = 0
    blk[:, 1, 0, 1] = alt
    inv = np.stack([2 * re, 2 * im], 2).transpose(2, 1, 0) / NF
    inv[0, 0], inv[1, 0] = 1 / NF, alt / NF
    inv2 = np.zeros((2, NF, 2, NB))
    inv2[0, :, 0] = inv2[1, :, 1] = inv.reshape(NF, NB)
    f = lambda m, *shape: np.ascontiguousarray(m.reshape(shape), np.float32)
    return {"c_dft_u": f(dft_u, 2, P, P), "c_dft_phi": f(blk, NB, P), "c_idft": f(inv2, P, NF)}


def spectral(nc, sems, g, hn, t1, out):
    s0 = Scope(nc, sems, "stu")
    u_hat = nc.dram_tensor("u_hat", (NB, 2, B, 2, P, HALF), F32, kind="Internal").ap()
    g_hat = nc.dram_tensor("g_hat", (2, NB, 2, K, 2, BL, 2), F32, kind="Internal").ap()
    y_hat = nc.dram_tensor("y_hat", (2, B, NB, HALF, 2, P), F32, kind="Internal").ap()
    with s0.stack:
        me = s0.sb("me", [P, 2, 2, K, P], F32R)
        mu = s0.sb("mu", [P, 3, P])
        seg = s0.sb("seg", [P, 4])
        stu_prepare(nc, sems, g, hn, u_hat, g_hat, me, mu, seg)
        stu_convolve(nc, sems, me, u_hat, g_hat, y_hat)
        stu_finish(nc, sems, g, mu, seg, y_hat, hn, t1, out)


def stu_prepare(nc, sems, g, hn, u_hat, g_hat, me, mu, seg):
    DC = 16
    STEPS = P // DC
    s = Scope(nc, sems, "dft")
    with s.stack:
        wp = s.sb("wp", [NB, P])
        wu = s.sb("wu", [P, 2, P])
        ph = s.sb("ph", [NB, K, 2 * BL])
        gs = s.sb("gs", [2 * NB, 2, K, 2, BL, 2], F32R)
        u = s.sb("u", [P, 2, DC, BL])
        uo = s.sb("uo", [P, 2, 2, 2, DC, HALF])
        pp = s.ps("pp", [P, 2, BANK])
        pu = s.ps("pu", [P, 4, BANK])
        w_in, ph_in, ph_mm, ph_high, ph_out, g_stored, u_mm, u_out, u_used = (
            s.sem(n) for n in ("w_in", "ph_in", "ph_mm", "ph_high", "ph_out", "g_stored", "u_mm", "u_out", "u_used"))
        u_in = [s.sem(f"u_in{k}") for k in range(2)]
        u_stored = [s.sem(f"u_stored{k}") for k in range(2)]
        lw = s.sb("lw", [P, 4])
        gum = s.sb("gum", [P, 4])
        sig = s.sb("sig", [P, K])
        quarter = s.sb("quarter", [P, K])
        sk = s.sb("sk", [P, K])
        z = s.sb("z", [P, 4])
        e = s.sb("e", [P, 4])
        soft = s.sb("soft", [P, 4])
        eq = s.sb("eq", [P, 4])
        hard = s.sb("hard", [P, 4])
        left = s.sb("left", [P, 4])
        w = s.sb("w", [P, 4])
        one = s.sb("one", [P, 4])
        RING = 3
        raw = s.sb("raw", [P, RING, K * P])
        acc = s.sb("acc", [P, 2, K * P])
        rmu = acc[:, 1, 0:4 * 3 * P].rearrange("p (i n) -> p i n", i=4)
        small_in, mu_in, z_done, e_done, step, weighed, pow_done = (
            s.sem(n) for n in ("small_in", "mu_in", "z_done", "e_done", "step", "weighed", "pow_done"))
        raw_in = [s.sem(f"raw_in{i}") for i in range(RING)]
        NP = K * 2 * BL // BANK
        MM = DC * BL // BANK
        hv = hn.rearrange("d (ba n) -> ba d n", n=BL)

        def filters(n, y):
            return (pp[0:2 * NB, y, :].rearrange("p (k m r) -> p k r m", k=2, r=2),
                    *(gs[:, part, 2 * n:2 * n + 2, :, :, y] for part in range(2)))

        with nc.Block() as block:

            @block.sync
            def _(sp):
                sp.dma_start(lw[:], g["log_weights"]).then_inc(small_in, 16)
                sp.dma_start(gum[:], g["gumbel"]).then_inc(small_in, 16)
                sp.dma_start(sig[:], g["sigma"]).then_inc(small_in, 16)
                sp.dma_start(wp[:], g["c_dft_phi"]).then_inc(w_in, 16)
                sp.dma_start(wu[:], g["c_dft_u"].rearrange("r p m -> p r m")).then_inc(w_in, 16)
                for half in range(2):
                    sp.dma_start(ph[:, :, half * BL:(half + 1) * BL],
                                 g["phi"][:, half * BL:half * BL + T].rearrange("k (a m) -> a k m", m=BL)
                                 ).then_inc(ph_in, 16)
                for c in range(2):
                    sp.dma_start(u[:, c], hv[:, c * DC:(c + 1) * DC, :]).then_inc(u_in[c], 16)
                for c in range(STEPS):
                    if c + 2 < STEPS:
                        sp.wait_ge(u_used, c + 1)
                        sp.dma_start(u[:, c % 2], hv[:, (c + 2) * DC:(c + 3) * DC, :]).then_inc(u_in[c % 2], 16)
                    if c == 1:
                        sp.wait_ge(ph_out, 4 * NP)
                        for part in range(2):
                            sp.dma_start(g_hat[part].rearrange("w x k r m y -> (w x) (k r m y)"),
                                         gs[:, part].rearrange("p k r m y -> p (k r m y)").bitcast(F32)
                                         ).then_inc(g_stored, 16)
                    sp.wait_ge(u_out, (c + 1) * 2 * MM)
                    for r in range(2):
                        for x in range(2):
                            for b2 in range(2):
                                p0 = x * HALF + b2 * NB
                                sp.dma_start(u_hat[:, x, 2 * r + b2, :, c * DC:(c + 1) * DC, :],
                                             uo[p0:p0 + NB, c % 2, r]).then_inc(u_stored[c % 2], 16)
                sp.wait_ge(g_stored, 32)
                for k in range(2):
                    sp.wait_ge(u_stored[k], 128 * (STEPS // 2))

            @block.tensor
            def _(pe):
                pe.wait_ge(w_in, 32)
                pe.wait_ge(ph_in, 32)
                phf = ph[:].rearrange("a k m -> a (k m)")
                for n in range(NP):
                    for y in range(2):
                        if n >= 1:
                            pe.wait_ge(ph_out, 2 * (2 * n + y - 1))
                        pe.matmul(pp[0:2 * NB, y, :], wp[:, y * 2 * NB:(y + 1) * 2 * NB],
                                  phf[:, n * BANK:(n + 1) * BANK], start=True, stop=True).then_inc(ph_mm, 1)
                for c in range(STEPS):
                    pe.wait_ge(u_in[c % 2], 16 * (c // 2 + 1))
                    uf = u[:, c % 2].rearrange("p d n -> p (d n)")
                    for n in range(2 * MM):
                        tot = c * 2 * MM + n
                        if tot >= 4:
                            pe.wait_ge(u_out, tot - 3)
                        mm = pe.matmul(pu[:, tot % 4, :], wu[:, n // MM, :], uf[:, n % MM * BANK:(n % MM + 1) * BANK],
                                       start=True, stop=True)
                        mm.then_inc(u_mm, 1)
                    mm = None
                    pe.wait_ge(u_mm, (c + 1) * 2 * MM)
                    pe.sem_inc(u_used, 1)

            @block.vector
            def _(v):
                done = [0]

                def then(ins):
                    done[0] += 1
                    ins.then_inc(step, 1)
                    v.wait_ge(step, done[0])

                then(v.memset(one[:], 1.0))
                v.wait_ge(small_in, 48)
                then(v.tensor_tensor(z[:], lw[:], gum[:], ALU.add))
                then(v.tensor_reduce(w[:, 0:1], z[:], AX.X, ALU.max))
                v.tensor_scalar(z[:], z[:], w[:, 0:1], None, ALU.subtract).then_inc(z_done, 1)
                v.wait_ge(e_done, 1)
                then(v.tensor_reduce(w[:, 0:1], e[:], AX.X, ALU.add))
                then(v.reciprocal(w[:, 1:2], w[:, 0:1]))
                then(v.tensor_scalar(soft[:], e[:], w[:, 1:2], None, ALU.mult))
                then(v.tensor_reduce(w[:, 0:1], soft[:], AX.X, ALU.max))
                then(v.tensor_scalar(eq[:], soft[:], w[:, 0:1], None, ALU.is_ge))
                then(v.tensor_copy(hard[:, 0:1], eq[:, 0:1]))
                then(v.tensor_tensor(left[:, 0:1], one[:, 0:1], eq[:, 0:1], ALU.subtract))
                for i in range(1, 4):
                    then(v.tensor_tensor(hard[:, i:i + 1], eq[:, i:i + 1], left[:, i - 1:i], ALU.mult))
                    then(v.tensor_tensor(left[:, i:i + 1], left[:, i - 1:i], hard[:, i:i + 1], ALU.subtract))
                then(v.tensor_tensor(w[:], hard[:], soft[:], ALU.subtract))
                then(v.tensor_tensor(w[:], w[:], soft[:], ALU.add))
                then(v.tensor_copy(seg[:, 3:4], hard[:, 0:1]))
                for j in (2, 1, 0):
                    then(v.tensor_tensor(seg[:, j:j + 1], seg[:, j + 1:j + 2], hard[:, 3 - j:4 - j], ALU.add))
                for n in range(NP):
                    for y in range(2):
                        v.wait_ge(ph_high, 2 * n + y + 1)
                        full, high, low = filters(n, y)
                        for k in range(2):
                            low_part(v, low[:, k], full[:, k], high[:, k]).then_inc(ph_out, 1)
                v.wait_ge(mu_in, 64)
                mu_f = mu[:].rearrange("d k e -> d (k e)")
                then(v.tensor_scalar(mu_f, rmu[:, 0, :], w[:, 0:1], None, ALU.mult))
                for i in range(1, 4):
                    then(v.scalar_tensor_tensor(mu_f, rmu[:, i, :], w[:, i:i + 1], mu_f, ALU.mult, ALU.add))
                for m in range(2):
                    for i in range(4):
                        n = 4 * m + i
                        v.wait_ge(raw_in[n % RING], 16 * (n // RING + 1))
                        if i:
                            v.wait_ge(weighed, n)
                            v.scalar_tensor_tensor(acc[:, m, :], raw[:, n % RING, :], w[:, i:i + 1], acc[:, m, :],
                                                   ALU.mult, ALU.add).then_inc(weighed, 1)
                        else:
                            v.tensor_scalar(acc[:, m, :], raw[:, n % RING, :], w[:, 0:1], None, ALU.mult
                                            ).then_inc(weighed, 1)
                v.wait_ge(weighed, 8)
                v.wait_ge(pow_done, 2)
                for m, op in enumerate((ALU.add, ALU.subtract)):
                    then(v.tensor_tensor(raw[:, 2 * m, :], acc[:, 0, :], acc[:, 1, :], op))
                    full = raw[:, (2 * m + 1) % RING, :].rearrange("d (k e) -> d k e", e=P)
                    then(v.tensor_tensor(full, raw[:, 2 * m, :].rearrange("d (k e) -> d k e", e=P),
                                         sk[:].unsqueeze(2).broadcast_to((P, K, P)), ALU.mult))
                    then(v.tensor_copy(me[:, 0, m], full))
                    then(low_part(v, me[:, 1, m], full, me[:, 0, m]))

            @block.gpsimd
            def _(pool):
                for i in range(4):
                    pool.dma_start(rmu[:, i, :].rearrange("d (k e) -> d k e", e=P),
                                   g["M_u"][i].rearrange("k d e -> d k e")).then_inc(mu_in, 16)
                pool.memset(quarter[:], 0.25).then_inc(pow_done, 1)
                pool.wait_ge(pow_done, 1)
                pool.wait_ge(small_in, 48)
                pool.tensor_tensor(sk[:], sig[:], quarter[:], ALU.pow).then_inc(pow_done, 1)
                for m, name in enumerate(("M_phi_plus", "M_phi_minus")):
                    for i in range(4):
                        n = 4 * m + i
                        if n >= RING:
                            pool.wait_ge(weighed, n - RING + 1)
                        pool.dma_start(raw[:, n % RING, :].rearrange("d (k e) -> d k e", e=P),
                                       g[name][i].rearrange("k d e -> d k e")).then_inc(raw_in[n % RING], 16)

            @block.scalar
            def _(act):
                act.wait_ge(z_done, 1)
                act.activation(e[:], z[:], ACT.Exp).then_inc(e_done, 1)
                for n in range(NP):
                    for y in range(2):
                        act.wait_ge(ph_mm, 2 * n + y + 1)
                        full, high, low = filters(n, y)
                        for k in range(2):
                            ins = act.activation(high[:, k], full[:, k], ACT.Copy)
                        ins.then_inc(ph_high, 1)
                for c in range(STEPS):
                    if c >= 2:
                        act.wait_ge(u_stored[c % 2], 128 * (c // 2))
                    for n in range(2 * MM):
                        d0 = n % MM * (BANK // BL)
                        tot = c * 2 * MM + n
                        act.wait_ge(u_mm, tot + 1)
                        for q in range(2):
                            ins = act.activation(
                                uo[:, c % 2, n // MM, q, d0:d0 + BANK // BL, :],
                                pu[:, tot % 4, :].rearrange("p (d j q) -> p q d j", q=2, j=HALF)[:, q, :, ::-1], ACT.Copy)
                        ins.then_inc(u_out, 1)


def stu_convolve(nc, sems, me, u_hat, g_hat, y_hat):
    s = Scope(nc, sems, "cv")
    NG = K // KG
    W = 2
    NI = NB // W
    GPB = W * NG
    with s.stack:
        u_raw = s.sb("u_raw", [P, W, B, 2, 2, HALF])
        u = s.sb("u", [P, W, 2, B, 2, 2, HALF], F32R)
        tp = s.sb("tp", [P, 2, 2, KG, 2, 2 * (HALF + 1)], F32R)
        vb = s.sb("vb", [P, 2, 2, 4, KG, B, P], F32R)
        yo = s.sb("yo", [P, 2, B, P])
        pv = s.ps("pv", [P, 4, BANK])
        py = s.ps("py", [P, 4, BANK])
        u_in = [s.sem(f"u_in{k}") for k in range(W)]
        t_in = [s.sem(f"t_in{k}") for k in range(2)]
        y_stored = [s.sem(f"y_stored{k}") for k in range(2)]
        u_high, u_ready, v_mm, v_high, v_low, g_done, y_evac, yo_free = (
            s.sem(n) for n in ("u_high", "u_ready", "v_mm", "v_high", "v_low", "g_done", "y_evac", "yo_free"))

        def flat(ap):
            return ap.rearrange("d b q x j -> d (b q x j)")

        VT = 16
        with nc.Block() as block:

            @block.sync
            def _(sp):
                def load_u(i, w):
                    for x in range(2):
                        sp.dma_start(u_raw[:, w, :, :, x, :].rearrange("d b q j -> d (b q) j"),
                                     u_hat[i * W + w, x].rearrange("b q d j -> d (b q) j")).then_inc(u_in[w], 16)

                def groups(i, last):
                    for gg in range(GPB):
                        w, kg = divmod(gg, NG)
                        if kg == 1 and not last:
                            sp.wait_ge(u_ready, i * W + w + 1)
                            load_u(i + 1, w)
                        sp.wait_ge(g_done, i * GPB + gg + 1)
                        for part in range(2):
                            for x in range(2):
                                row = g_hat[part, i * W + w, x, kg * KG:(kg + 1) * KG]
                                src = bass.AP(row.tensor, row.offset,
                                              ap=[[2, HALF], [2 * BL, KG * 2], [1, 2 * HALF + 2]])
                                sp.dma_start(tp[x * HALF:(x + 1) * HALF, gg % 2, part].rearrange("p k r m -> p (k r) m").bitcast(F32),
                                             src).then_inc(t_in[gg % 2], 16)

                for w in range(W):
                    load_u(0, w)
                with sp.Fori(0, NI - 1) as i:
                    groups(i, False)
                groups(NI - 1, True)

            @block.tensor
            def _(pe):
                pe.sem_inc(v_mm, GPB * VT)
                pe.sem_inc(g_done, 2)
                with pe.Fori(0, NI) as i:

                    def make_v(gg):
                        w, kg = divmod(gg, NG)
                        if kg == 0:
                            pe.wait_ge(u_ready, i * W + w + 1)
                        for n in range(VT):
                            qt, b = divmod(n, B)
                            q, ty = divmod(qt, 2)
                            pe.wait_ge(v_low, (i * GPB + gg) * VT + n + 1)
                            product(pe, pv[:, n % 4, :], [u[:, w, part, b, q] for part in range(2)],
                                    [me[:, part, ty, kg * KG:(kg + 1) * KG, :] for part in range(2)],
                                    start=True, stop=True).then_inc(v_mm, 1)

                    def toeplitz(gg):
                        w, kg = divmod(gg, NG)
                        pe.wait_ge(t_in[gg % 2], i * (32 * GPB) + (gg // 2 + 1) * 64)
                        pe.wait_ge(v_low, (i * GPB + gg + 1) * VT + 4)
                        for p in range(2):
                            if kg == 0:
                                pe.wait_ge(y_evac, i * (2 * W) + 2 * w + p + 1)
                            for k in range(KG):
                                for q in range(2):
                                    par = p ^ q
                                    off = 0 if (p, q) == (0, 1) else 1
                                    mm = product(pe, py[:, 2 * w + p, :],
                                                 [tp[:, gg % 2, part, k, par, 2 * off:2 * off + P] for part in range(2)],
                                                 [vb[:, gg % 2, part, 2 * q + par, k] for part in range(2)],
                                                 start=(kg == 0 and k == 0 and q == 0),
                                                 stop=(kg == NG - 1 and k == KG - 1 and q == 1))
                        mm.then_inc(g_done, 1)

                    make_v(0)
                    for gg in range(GPB):
                        if gg + 1 < GPB:
                            make_v(gg + 1)
                        toeplitz(gg)


            def split_v(eng, step, i, gg):
                eng.wait_ge(g_done, i * GPB + gg + 1)
                for n in range(VT):
                    qt, b = divmod(n, B)
                    step(n, pv[:, n % 4, :].rearrange("p (k e) -> p k e", e=P),
                         *(vb[:, gg % 2, part, qt, :, b, :] for part in range(2)))

            @block.gpsimd
            def _(pool):
                pool.sem_inc(yo_free, 2)
                with pool.Fori(0, NI) as i:
                    for w in range(W):
                        for p in range(2):
                            pool.wait_ge(y_evac, i * (2 * W) + 2 * w + p + 1 + 2 * W)
                            pool.dma_start(y_hat[p, :, i * W + w].rearrange("b j y e -> (j y) b e"),
                                           yo[:, p]).then_inc(y_stored[p], 16)
                        for p in range(2):
                            pool.wait_ge(y_stored[p], i * (16 * W) + w * 16 + 16)
                            pool.sem_inc(yo_free, 1)

            @block.scalar
            def _(act):
                def high_u(i, w):
                    act.wait_ge(u_in[w], i * 32 + 32)
                    act.wait_ge(v_mm, (i * GPB + (w + 1) * NG) * VT)
                    act.activation(flat(u[:, w, 0]), flat(u_raw[:, w]), ACT.Copy).then_inc(u_high, 1)

                def groups(i, last):
                    for gg in range(GPB):

                        def high_v(n, full, high, low):
                            act.wait_ge(v_mm, (i * GPB + gg + GPB) * VT + n + 1)
                            act.activation(high, full, ACT.Copy).then_inc(v_high, 1)

                        split_v(act, high_v, i, gg)
                        if gg == 0:
                            high_u(i, 1)
                        if gg == NG and not last:
                            high_u(i + 1, 0)

                high_u(0, 0)
                with act.Fori(0, NI - 1) as i:
                    groups(i, False)
                groups(NI - 1, True)

            @block.vector
            def _(v):
                v.sem_inc(v_low, 4)
                v.sem_inc(y_evac, 2 * W)

                def copy_y(i, w):
                    v.wait_ge(g_done, (i * GPB + (w + 1) * NG) + 2)
                    for p in range(2):
                        v.wait_ge(yo_free, i * (2 * W) + 2 * w + 2)
                        v.tensor_copy(yo[:, p].rearrange("p b e -> p (b e)"), py[:, 2 * w + p, :]).then_inc(y_evac, 1)

                def low_u(i, w):
                    v.wait_ge(u_high, i * W + w + 1)
                    low_part(v, flat(u[:, w, 1]), flat(u_raw[:, w]), flat(u[:, w, 0])).then_inc(u_ready, 1)

                def groups(i, last):
                    for gg in range(GPB):

                        def low_v(n, full, high, low):
                            v.wait_ge(v_high, (i * GPB + gg) * VT + n + 1)
                            low_part(v, low, full, high).then_inc(v_low, 1)

                        split_v(v, low_v, i, gg)
                        if gg == 0:
                            low_u(i, 1)
                        if gg == NG and not last:
                            low_u(i + 1, 0)
                        if gg % NG == 1 and gg > NG:
                            copy_y(i, gg // NG - 1)
                    copy_y(i, W - 1)

                low_u(0, 0)
                with v.Fori(0, NI - 1) as i:
                    groups(i, False)
                groups(NI - 1, True)


def stu_finish(nc, sems, g, mu, seg, y_hat, hn, t1, out):
    s = Scope(nc, sems, "fin")
    JB = BANK // NB
    with s.stack:
        wi = s.sb("wi", [P, NF])
        yh = s.sb("yh", [P, 2, HALF // 2, P])
        ys = s.sb("ys", [P, NB, HALF, 2])
        h = s.sb("h", [P, 2, 2 + T])
        t = s.sb("t", [P, 2, T])
        o = s.sb("o", [P, T])
        py = s.ps("py", [P, 4, BANK])
        pa = s.ps("pa", [P, 2, BANK])
        yh_in, h_in, t_in = ([s.sem(f"{n}{k}") for k in range(2)] for n in ("yh_in", "h_in", "t_in"))
        w_in, yh_used, y_mm, y_evac, ar_mm, summed, kept, o_stored, zeroed = (
            s.sem(n) for n in ("w_in", "yh_used", "y_mm", "y_evac", "ar_mm", "summed", "kept", "o_stored", "zeroed"))
        NT = T // BANK
        NJ = 2 * HALF // JB
        SEG = (0, 1, 2, 2, 3, 3, 3, 3)
        hv, tv, ov = (a.rearrange("p (b n) -> p b n", b=B) for a in (hn, t1, out))

        def batches(eng, body):
            with eng.Fori(0, B // 2) as i:
                for k in range(2):
                    body(i * 2 + k, i, k)

        with nc.Block() as block:

            @block.sync
            def _(sp):
                sp.dma_start(wi[:], g["c_idft"]).then_inc(w_in, 16)

                def body(b, i, k):
                    for p in range(2):
                        sp.wait_ge(yh_used, b * 2 + p + 1)
                        for parity in range(2):
                            for x in range(2):
                                p0 = parity * NF + x * NB
                                sp.dma_start(yh[p0:p0 + NB, p], y_hat[p, b, :, parity::2, x, :]).then_inc(yh_in[p], 16)
                    sp.wait_ge(ar_mm, b * NT + NT)
                    sp.wait_ge(kept, b * NT + NT)
                    sp.dma_start(h[:, k, 2:], hv[:, b, :]).then_inc(h_in[k], 16)
                    sp.dma_start(t[:, k], tv[:, b, :]).then_inc(t_in[k], 16)

                batches(sp, body)

            @block.gpsimd
            def _(pool):
                pool.memset(h[:, :, 0:2], 0.0).then_inc(zeroed, 1)

            @block.tensor
            def _(pe):
                pe.sem_inc(ar_mm, 2 * NT)
                pe.sem_inc(yh_used, 2)
                pe.wait_ge(w_in, 16)
                pe.wait_ge(zeroed, 1)

                def body(b, i, k):
                    for p in range(2):
                        pe.wait_ge(yh_in[p], b * 64 + 64)
                        for c in range(NJ // 2):
                            n = p * (NJ // 2) + c
                            pe.wait_ge(y_evac, b * NJ + n + 1)
                            for jj in range(JB // 2):
                                mm = pe.matmul(py[:, n % 4, jj * NF:(jj + 1) * NF], yh[:, p, c * (JB // 2) + jj, :],
                                               wi[:], start=True, stop=True, skip_group_check=True)
                            mm.then_inc(y_mm, 1)
                        pe.wait_ge(y_mm, b * NJ + (p + 1) * (NJ // 2))
                        pe.sem_inc(yh_used, 1)
                    pe.wait_ge(h_in[k], i * 16 + 16)
                    for c in range(NT):
                        pe.wait_ge(summed, b * NT + c + 1)
                        for d in range(3):
                            mm = pe.matmul(pa[:, c % 2, :], mu[:, d, :],
                                           h[:, k, 2 - d + c * BANK:2 - d + (c + 1) * BANK],
                                           start=(d == 0), stop=(d == 2))
                        mm.then_inc(ar_mm, 1)

                batches(pe, body)

            @block.vector
            def _(v):
                v.sem_inc(y_evac, 4)
                v.sem_inc(summed, 2)
                v.sem_inc(kept, 2 * NT)

                def body(b, i, k):
                    v.wait_ge(kept, b * NT + 2 * NT)
                    for n in range(NJ):
                        p, c = divmod(n, NJ // 2)
                        v.wait_ge(y_mm, b * NJ + n + 1)
                        v.tensor_copy(ys[:, :, c * JB:(c + 1) * JB, p],
                                      py[:, n % 4, :].rearrange("e (j a) -> e a j", a=NB)).then_inc(y_evac, 1)
                    v.wait_ge(y_evac, b * NJ + NJ + 4)
                    v.wait_ge(t_in[k], i * 16 + 16)
                    v.wait_ge(o_stored, b * 16 + 16)
                    yf = ys[:].rearrange("e a j q -> e (a j q)")
                    for c in range(NT):
                        sl = slice(c * BANK, (c + 1) * BANK)
                        v.wait_ge(ar_mm, b * NT + c + 1 + 2 * NT)
                        v.tensor_tensor(yf[:, sl], yf[:, sl], pa[:, c % 2, :], ALU.add).then_inc(summed, 1)
                        v.wait_ge(summed, b * NT + c + 3)
                        v.scalar_tensor_tensor(o[:, sl], yf[:, sl], seg[:, SEG[c]:SEG[c] + 1], t[:, k, sl],
                                               ALU.mult, ALU.add).then_inc(kept, 1)

                batches(v, body)

            @block.scalar
            def _(act):
                act.sem_inc(o_stored, 16)

                def body(b, i, k):
                    act.wait_ge(kept, b * NT + 3 * NT)
                    act.dma_start(ov[:, b, :], o[:]).then_inc(o_stored, 16)

                batches(act, body)
                act.wait_ge(o_stored, 16 * (B + 1))


def program(nc, g, out):
    def scratch(name):
        return nc.dram_tensor(name, (P, N), F32, kind="Internal").ap()

    c3, t0, t1, hn1, hn2, hf, hb = (scratch(n) for n in ("c3", "t0", "t1", "hn1", "hn2", "h_forward", "h_backward"))
    sems = []
    conv_block(nc, sems, g, c3)
    attention(nc, sems, g, c3, t0)
    layer_norm(nc, sems, "ln1", [t0], None, hn1, g["c_mean"])
    release(nc, sems)
    mamba(nc, sems, g, hn1, (hf, hb))
    release(nc, sems)
    layer_norm(nc, sems, "ln2", [t0, hf, hb], t1, hn2, g["c_mean"])
    spectral(nc, sems, g, hn2, t1, out)


def laid_out(inputs):
    i = {k: np.asarray(v) for k, v in inputs.items()}
    col = lambda a: a[:, None]
    rep = lambda a: np.broadcast_to(a, (P,) + a.shape)
    c = {k[8:]: v for k, v in i.items() if k.startswith("L0_conv_")}
    m = [{k[12:]: v for k, v in i.items() if k.startswith(f"L1_attn_{p}")} for p in ("fwd", "bwd")]
    f = {k[7:]: v for k, v in i.items() if k.startswith("L1_ffn_")}
    a = {"x": i["x"].reshape(N, P).T, "W1": c["W1"], "W2": c["W2"], "b1": col(c["b1"]), "b2a": col(c["b2"][:P]),
         "b2b": col(c["b2"][P:]), "Wv": c["Wv"], "bv": rep(c["bv"]), "W3": c["W3"], "b3": col(c["b3"])}
    a["Wqk"], a["bqk"] = np.zeros((P, P), np.float32), np.zeros((P, 1), np.float32)
    for n in range(PARTS * PARTS):
        for at, w, b in ((0, "Wq", "bq"), (64, "Wk", "bk")):
            a["Wqk"][:, at + n * DQK:at + (n + 1) * DQK] = c[w]
            a["bqk"][at + n * DQK:at + (n + 1) * DQK, 0] = c[b]
    nz = 2 * DI + 2 * DS
    a["Wdt"] = np.concatenate([d["in_proj"][:, nz:] for d in m], 1)
    a["dt_bias"] = rep(np.stack([d["dt_bias"] for d in m]))
    a["A_log"] = rep(np.stack([d["A_log"] for d in m]))
    for n, d in enumerate(m):
        a[f"in_proj{n}"] = d["in_proj"][:, :nz]
        a[f"conv_w{n}"] = d["conv_w"].reshape(3, P, TAPS).transpose(1, 0, 2)
        a[f"conv_b{n}"] = d["conv_b"].reshape(3, P).T
        a[f"D{n}"] = np.repeat(d["D"], HD).reshape(2, P).T
        a[f"norm_w{n}"] = d["norm_w"].reshape(2, P).T
        a[f"out_proj{n}"] = d["out_proj"].reshape(2, P, P).transpose(1, 0, 2)
    a["phi"] = np.zeros((K, BL + T), np.float32)
    a["phi"][:, BL:] = f["phi"].T
    a.update(M_u=f["M_u"], M_phi_plus=f["M_phi_plus"], M_phi_minus=f["M_phi_minus"], sigma=rep(f["sigma"]),
             log_weights=rep(f["log_weights"]), gumbel=rep(f["gumbel"]), c_mean=np.full((P, P), 1 / P, np.float32))
    for constants in (attention_constants(), mamba_constants(), stu_constants()):
        a.update(constants)
    return {k: np.ascontiguousarray(v) for k, v in a.items()}


def kernel(**inputs):
    import concourse.bacc as bacc
    from concourse.bass_utils import run_bass_kernel_spmd

    arrays = laid_out(inputs)
    nc = bacc.Bacc("TRN2", target_bir_lowering=False, num_devices=1)
    g = {k: nc.dram_tensor(f"in_{k}", v.shape, F32, kind="ExternalInput").ap() for k, v in arrays.items()}
    out = nc.dram_tensor("out", (P, N), F32, kind="ExternalOutput").ap()
    program(nc, g, out)
    r = run_bass_kernel_spmd(nc, [{f"in_{k}": v for k, v in arrays.items()}], core_ids=[0])
    return r.results[0]["out"].T.reshape(B, IMG, IMG, P)
```
